# Optimizing a Trainium2 kernel written in Bass

```python
import numpy as np
import jax
import jax.numpy as jnp

def _softmax(x, axis=-1):
    return jax.nn.softmax(x, axis=axis)

def _gelu(x):
    return jax.nn.gelu(x, approximate=True)

def _silu(x):
    return jax.nn.silu(x)

def _sigmoid(x):
    return jax.nn.sigmoid(x)

def _layernorm(x, axis=-1, eps=1e-05):
    m = jnp.mean(x, axis=axis, keepdims=True)
    v = jnp.var(x, axis=axis, keepdims=True)
    return (x - m) / jnp.sqrt(v + eps)

def _scatter_add(tgt, idx, src, axis=0):
    return tgt.at[idx].add(src)

def _segment_sum(src, seg, n):
    return jax.ops.segment_sum(src, seg, n)
kernel_name = 'mk_adaln_attn_ffn_d1_seqx_r8_da409b'

def setup_inputs(seed: int=0):
    np.random.seed(seed)
    _w = jnp.asarray

    def _rec_inputs():
        import jax
        import jax.numpy as jnp
        _rk = jax.random.key(seed)
        x = 7.22e-05 + 1 * jax.random.normal(jax.random.fold_in(_rk, 1), (32, 128, 128), jnp.float32)
        _lenS = 128 - jax.random.randint(jax.random.fold_in(_rk, 7), (32,), 0, max(1, 128 // 4) + 1, jnp.int32)
        _lenS2 = 128 - jax.random.randint(jax.random.fold_in(_rk, 8), (32,), 0, max(1, 128 // 4) + 1, jnp.int32)
        cond_64 = -0.104238 + 1.01173 * jax.random.normal(jax.random.fold_in(_rk, 11), (32, 64), jnp.float32)
        _validS = jnp.arange(128)[None, :] < _lenS[:, None]
        _validS2 = jnp.arange(128)[None, :] < _lenS2[:, None]
        _causal = jnp.tril(jnp.ones((128, 128), dtype=bool))
        mask_BxS_bf1 = jnp.ones((32, 128), dtype=bool)
        return (x, cond_64, mask_BxS_bf1)
    x, cond_64, mask_BxS_bf1 = _rec_inputs()

    def _L0_cond_setup():
        import jax, jax.numpy as jnp
        import numpy as np
        B, S, H = (4, 256, 128)
        E = 8
        M = 64
        K = 2
        N_SHARED = 2
        SM = M * N_SHARED
        G = 64
        GE_TEMP = 1.0
        ALPHA = 0.001
        SEQ_AUX = True
        NORM_TOPK = True
        COS_TEMP = 0.78
        CONS_ALPHA = 0.01
        LEAKY_SLOPE = 0.01
        EPS_COS = 1e-08

        def _leaky(x):
            return jnp.where(x >= 0, x, LEAKY_SLOPE * x)

        def _moe_forward(hidden_states, g, wt, wg, w_gate, w_up, w_down, sw_gate, sw_up, sw_down):
            b, s, h = hidden_states.shape
            x = hidden_states.reshape(-1, h)
            T = x.shape[0]
            logits_h = x @ wt.T
            logits_g = g @ wg.T
            logits_g = jnp.repeat(logits_g, s, axis=0)
            logits = (logits_h + logits_g / GE_TEMP) / (1.0 + 1.0 / GE_TEMP)
            scores = jax.nn.softmax(logits, axis=-1)
            topk_w, topk_idx = jax.lax.top_k(scores, K)
            if K > 1 and NORM_TOPK:
                topk_w = topk_w / (topk_w.sum(-1, keepdims=True) + 1e-20)
            onehot = jax.nn.one_hot(topk_idx.reshape(b, s * K), E, dtype=jnp.float32)
            ce = onehot.sum(1) / (s * K / E)
            aux_loss = (ce * scores.reshape(b, s, E).mean(1)).sum(1).mean() * ALPHA
            gp = _leaky(jnp.einsum('th,ehm->etm', x, w_gate))
            up = jnp.einsum('th,ehm->etm', x, w_up)
            y_all = jnp.einsum('etm,emh->eth', gp * up, w_down)
            y_sel = y_all[topk_idx, jnp.arange(T)[:, None], :]
            y = (y_sel * topk_w[..., None]).sum(1).reshape(b, s, h)
            p = _leaky(hidden_states @ sw_gate) * (hidden_states @ sw_up) @ sw_down
            y = y + p
            num = jnp.sum(y * p, -1)
            den = jnp.maximum(jnp.linalg.norm(y, axis=-1), EPS_COS) * jnp.maximum(jnp.linalg.norm(p, axis=-1), EPS_COS)
            closs = CONS_ALPHA * jnp.mean(num / den / (1.0 + COS_TEMP))
            return (y, aux_loss + closs)
        key = jax.random.key(seed)
        ks = jax.random.split(key, 12)
        sh = 1.0 / np.sqrt(H)
        sm = 1.0 / np.sqrt(M)
        ssm = 1.0 / np.sqrt(SM)
        sg = 1.0 / np.sqrt(G)
        return {'hidden_states': jax.random.normal(ks[0], (B, S, H), jnp.float32), 'g': jax.random.normal(ks[1], (B, G), jnp.float32), 'wt': jax.random.uniform(ks[2], (E, H), jnp.float32, -sh, sh), 'wg': jax.random.uniform(ks[3], (E, G), jnp.float32, -sg, sg), 'w_gate': jax.random.uniform(ks[4], (E, H, M), jnp.float32, -sh, sh), 'w_up': jax.random.uniform(ks[5], (E, H, M), jnp.float32, -sh, sh), 'w_down': jax.random.uniform(ks[6], (E, M, H), jnp.float32, -sm, sm), 'sw_gate': jax.random.uniform(ks[7], (H, SM), jnp.float32, -sh, sh), 'sw_up': jax.random.uniform(ks[8], (H, SM), jnp.float32, -sh, sh), 'sw_down': jax.random.uniform(ks[9], (SM, H), jnp.float32, -ssm, ssm)}
    _L0_cond_all = _L0_cond_setup()
    _L0_cond_in = {k: v for k, v in _L0_cond_all.items() if k in ('wt', 'wg', 'w_gate', 'w_up', 'w_down', 'sw_gate', 'sw_up', 'sw_down')}
    del _L0_cond_all

    def _L0_attn_setup():
        import jax, jax.numpy as jnp
        import numpy as np
        N_EMBD = 128
        BLOCK_SIZE = 256
        ATTN_SPAN = 32
        LN_EPS = 1e-05

        def _band_mask(T, span, dtype):
            ones = jnp.ones((T, T), dtype=dtype)
            return jnp.tril(ones, 0) * (1.0 - jnp.tril(ones, -span))

        def _layer_norm(h, w, b):
            mu = jnp.mean(h, axis=-1, keepdims=True)
            var = jnp.var(h, axis=-1, keepdims=True)
            return (h - mu) * jax.lax.rsqrt(var + LN_EPS) * w + b
        key = jax.random.key(seed)
        k_x, k_w, k_b, k_lw = jax.random.split(key, 4)
        B, T, C = (4, BLOCK_SIZE, N_EMBD)
        x = jax.random.normal(k_x, (B, T, C), dtype=jnp.float32)
        lim = 1.0 / np.sqrt(C)
        W_qkv = jax.random.uniform(k_w, (C, 3 * C), minval=-lim, maxval=lim, dtype=jnp.float32)
        b_qkv = jax.random.uniform(k_b, (3 * C,), minval=-lim, maxval=lim, dtype=jnp.float32)
        ln_w = jnp.ones((C,), dtype=jnp.float32)
        ln_b = jnp.zeros((C,), dtype=jnp.float32)
        return {'x': x, 'W_qkv': W_qkv, 'b_qkv': b_qkv, 'ln_w': ln_w, 'ln_b': ln_b}
    _L0_attn_all = _L0_attn_setup()
    _L0_attn_in = {k: v for k, v in _L0_attn_all.items() if k in ('W_qkv', 'b_qkv', 'ln_w', 'ln_b')}
    del _L0_attn_all

    def _L0_cond2_setup():
        import jax, jax.numpy as jnp
        import numpy as np
        DIM = 128
        HEADS = 16
        DIM_HEAD = 64
        SCALE = 8.0

        def ln(x, g, eps=1e-05):
            mean = x.mean(axis=-1, keepdims=True)
            var = ((x - mean) ** 2).mean(axis=-1, keepdims=True)
            return (x - mean) * jax.lax.rsqrt(var + eps) * g

        def l2norm(t):
            n = jnp.maximum(jnp.linalg.norm(t, axis=-1, keepdims=True), 1e-12)
            return t / n

        def rel_pos_bias(n, w0, b0, g0, w1, b1, g1, w2, b2, dtype):
            pos = jnp.arange(-n + 1, n, dtype=dtype)[:, None]
            h = jax.nn.silu(ln(pos @ w0 + b0, g0))
            h = jax.nn.silu(ln(h @ w1 + b1, g1))
            h = h @ w2 + b2
            i = jnp.arange(n)
            idx = i[:, None] - i[None, :] + n - 1
            bias = h[idx]
            return jnp.transpose(bias, (2, 0, 1))
        key = jax.random.key(seed)
        ks = jax.random.split(key, 16)
        b, n = (2, 256)
        inner = HEADS * DIM_HEAD
        s = 0.02
        return {'x': jax.random.normal(ks[0], (b, n, DIM), jnp.float32), 'mask': jnp.ones((b, n), dtype=bool), 'g_norm': jnp.ones((DIM,), jnp.float32), 'Wq': jax.random.normal(ks[1], (DIM, inner), jnp.float32) * s, 'Wkv': jax.random.normal(ks[2], (DIM, 2 * DIM_HEAD), jnp.float32) * s, 'q_scale': jnp.ones((DIM_HEAD,), jnp.float32), 'k_scale': jnp.ones((DIM_HEAD,), jnp.float32), 'null_kv': jax.random.normal(ks[3], (2, DIM_HEAD), jnp.float32), 'null_attn_bias': jax.random.normal(ks[4], (HEADS,), jnp.float32), 'w0': jax.random.normal(ks[5], (1, DIM), jnp.float32) * s, 'b0': jnp.zeros((DIM,), jnp.float32), 'g0': jnp.ones((DIM,), jnp.float32), 'w1': jax.random.normal(ks[6], (DIM, DIM), jnp.float32) * s, 'b1': jnp.zeros((DIM,), jnp.float32), 'g1': jnp.ones((DIM,), jnp.float32), 'w2': jax.random.normal(ks[7], (DIM, HEADS), jnp.float32) * s, 'b2': jnp.zeros((HEADS,), jnp.float32), 'Wout': jax.random.normal(ks[8], (inner, DIM), jnp.float32) * s, 'g_out': jnp.ones((DIM,), jnp.float32)}
    _L0_cond2_all = _L0_cond2_setup()
    _L0_cond2_in = {k: v for k, v in _L0_cond2_all.items() if k in ('g_norm', 'Wq', 'Wkv', 'q_scale', 'k_scale', 'null_attn_bias', 'w0', 'b0', 'g0', 'w1', 'b1', 'g1', 'w2', 'b2', 'Wout', 'g_out')}
    del _L0_cond2_all

    def _L0_ffn_setup():
        import jax, jax.numpy as jnp
        import numpy as np
        D_IN, D_HID = (128, 512)

        def _ternary(key, shape):
            return jax.random.randint(key, shape, -1, 2).astype(jnp.float32)

        def _tlin(x, w, s):
            return jnp.einsum('bsi,oi->bso', x, w) * s
        key = jax.random.key(seed)
        ks = jax.random.split(key, 12)
        inv = lambda fan: 1.0 / np.sqrt(fan).astype(np.float32)
        return {'x': jax.random.normal(ks[0], (4, 256, D_IN), dtype=jnp.float32), 'w1_w': _ternary(ks[1], (D_HID, D_IN)), 'w1_s': jax.random.uniform(ks[2], (D_HID,), dtype=jnp.float32) * inv(D_IN), 'w2_w': _ternary(ks[3], (D_HID, D_IN)), 'w2_s': jax.random.uniform(ks[4], (D_HID,), dtype=jnp.float32) * inv(D_IN), 'h1_w': _ternary(ks[5], (D_HID, D_HID)), 'h1_s': jax.random.uniform(ks[6], (D_HID,), dtype=jnp.float32) * inv(D_HID), 'h2_w': _ternary(ks[7], (D_HID, D_HID)), 'h2_s': jax.random.uniform(ks[8], (D_HID,), dtype=jnp.float32) * inv(D_HID), 'w3_w': _ternary(ks[9], (D_IN, D_HID)), 'w3_s': jax.random.uniform(ks[10], (D_IN,), dtype=jnp.float32) * inv(D_HID)}
    _L0_ffn_all = _L0_ffn_setup()
    _L0_ffn_in = {k: v for k, v in _L0_ffn_all.items() if k in ('w1_w', 'w1_s', 'w2_w', 'w2_s', 'h1_w', 'h1_s', 'h2_w', 'h2_s', 'w3_w', 'w3_s')}
    del _L0_ffn_all
    return {'x': x, 'cond_64': cond_64, 'mask_BxS_bf1': mask_BxS_bf1, 'L0_cond_wt': _L0_cond_in['wt'], 'L0_cond_wg': _L0_cond_in['wg'], 'L0_cond_w_gate': _L0_cond_in['w_gate'], 'L0_cond_w_up': _L0_cond_in['w_up'], 'L0_cond_w_down': _L0_cond_in['w_down'], 'L0_cond_sw_gate': _L0_cond_in['sw_gate'], 'L0_cond_sw_up': _L0_cond_in['sw_up'], 'L0_cond_sw_down': _L0_cond_in['sw_down'], 'L0_attn_W_qkv': _L0_attn_in['W_qkv'], 'L0_attn_b_qkv': _L0_attn_in['b_qkv'], 'L0_attn_ln_w': _L0_attn_in['ln_w'], 'L0_attn_ln_b': _L0_attn_in['ln_b'], 'L0_cond2_g_norm': _L0_cond2_in['g_norm'], 'L0_cond2_Wq': _L0_cond2_in['Wq'], 'L0_cond2_Wkv': _L0_cond2_in['Wkv'], 'L0_cond2_q_scale': _L0_cond2_in['q_scale'], 'L0_cond2_k_scale': _L0_cond2_in['k_scale'], 'L0_cond2_null_attn_bias': _L0_cond2_in['null_attn_bias'], 'L0_cond2_w0': _L0_cond2_in['w0'], 'L0_cond2_b0': _L0_cond2_in['b0'], 'L0_cond2_g0': _L0_cond2_in['g0'], 'L0_cond2_w1': _L0_cond2_in['w1'], 'L0_cond2_b1': _L0_cond2_in['b1'], 'L0_cond2_g1': _L0_cond2_in['g1'], 'L0_cond2_w2': _L0_cond2_in['w2'], 'L0_cond2_b2': _L0_cond2_in['b2'], 'L0_cond2_Wout': _L0_cond2_in['Wout'], 'L0_cond2_g_out': _L0_cond2_in['g_out'], 'L0_ffn_w1_w': _L0_ffn_in['w1_w'], 'L0_ffn_w1_s': _L0_ffn_in['w1_s'], 'L0_ffn_w2_w': _L0_ffn_in['w2_w'], 'L0_ffn_w2_s': _L0_ffn_in['w2_s'], 'L0_ffn_h1_w': _L0_ffn_in['h1_w'], 'L0_ffn_h1_s': _L0_ffn_in['h1_s'], 'L0_ffn_h2_w': _L0_ffn_in['h2_w'], 'L0_ffn_h2_s': _L0_ffn_in['h2_s'], 'L0_ffn_w3_w': _L0_ffn_in['w3_w'], 'L0_ffn_w3_s': _L0_ffn_in['w3_s']}

def reference(x, cond_64, mask_BxS_bf1, L0_cond_wt, L0_cond_wg, L0_cond_w_gate, L0_cond_w_up, L0_cond_w_down, L0_cond_sw_gate, L0_cond_sw_up, L0_cond_sw_down, L0_attn_W_qkv, L0_attn_b_qkv, L0_attn_ln_w, L0_attn_ln_b, L0_cond2_g_norm, L0_cond2_Wq, L0_cond2_Wkv, L0_cond2_q_scale, L0_cond2_k_scale, L0_cond2_null_attn_bias, L0_cond2_w0, L0_cond2_b0, L0_cond2_g0, L0_cond2_w1, L0_cond2_b1, L0_cond2_g1, L0_cond2_w2, L0_cond2_b2, L0_cond2_Wout, L0_cond2_g_out, L0_ffn_w1_w, L0_ffn_w1_s, L0_ffn_w2_w, L0_ffn_w2_s, L0_ffn_h1_w, L0_ffn_h1_s, L0_ffn_h2_w, L0_ffn_h2_s, L0_ffn_w3_w, L0_ffn_w3_s):
    import jax
    import jax.numpy as jnp

    def _L0_cond_ref(hidden_states, g, wt, wg, w_gate, w_up, w_down, sw_gate, sw_up, sw_down):
        import jax, jax.numpy as jnp
        import numpy as np
        B, S, H = (4, 256, 128)
        E = 8
        M = 64
        K = 2
        N_SHARED = 2
        SM = M * N_SHARED
        G = 64
        GE_TEMP = 1.0
        ALPHA = 0.001
        SEQ_AUX = True
        NORM_TOPK = True
        COS_TEMP = 0.78
        CONS_ALPHA = 0.01
        LEAKY_SLOPE = 0.01
        EPS_COS = 1e-08

        def _leaky(x):
            return jnp.where(x >= 0, x, LEAKY_SLOPE * x)

        def _moe_forward(hidden_states, g, wt, wg, w_gate, w_up, w_down, sw_gate, sw_up, sw_down):
            b, s, h = hidden_states.shape
            x = hidden_states.reshape(-1, h)
            T = x.shape[0]
            logits_h = x @ wt.T
            logits_g = g @ wg.T
            logits_g = jnp.repeat(logits_g, s, axis=0)
            logits = (logits_h + logits_g / GE_TEMP) / (1.0 + 1.0 / GE_TEMP)
            scores = jax.nn.softmax(logits, axis=-1)
            topk_w, topk_idx = jax.lax.top_k(scores, K)
            if K > 1 and NORM_TOPK:
                topk_w = topk_w / (topk_w.sum(-1, keepdims=True) + 1e-20)
            onehot = jax.nn.one_hot(topk_idx.reshape(b, s * K), E, dtype=jnp.float32)
            ce = onehot.sum(1) / (s * K / E)
            aux_loss = (ce * scores.reshape(b, s, E).mean(1)).sum(1).mean() * ALPHA
            gp = _leaky(jnp.einsum('th,ehm->etm', x, w_gate))
            up = jnp.einsum('th,ehm->etm', x, w_up)
            y_all = jnp.einsum('etm,emh->eth', gp * up, w_down)
            y_sel = y_all[topk_idx, jnp.arange(T)[:, None], :]
            y = (y_sel * topk_w[..., None]).sum(1).reshape(b, s, h)
            p = _leaky(hidden_states @ sw_gate) * (hidden_states @ sw_up) @ sw_down
            y = y + p
            num = jnp.sum(y * p, -1)
            den = jnp.maximum(jnp.linalg.norm(y, axis=-1), EPS_COS) * jnp.maximum(jnp.linalg.norm(p, axis=-1), EPS_COS)
            closs = CONS_ALPHA * jnp.mean(num / den / (1.0 + COS_TEMP))
            return (y, aux_loss + closs)
        y, _ = _moe_forward(hidden_states, g, wt, wg, w_gate, w_up, w_down, sw_gate, sw_up, sw_down)
        return y

    def _L0_attn_ref(x, W_qkv, b_qkv, ln_w, ln_b):
        import jax, jax.numpy as jnp
        import numpy as np
        N_EMBD = 128
        BLOCK_SIZE = 256
        ATTN_SPAN = 32
        LN_EPS = 1e-05

        def _band_mask(T, span, dtype):
            ones = jnp.ones((T, T), dtype=dtype)
            return jnp.tril(ones, 0) * (1.0 - jnp.tril(ones, -span))

        def _layer_norm(h, w, b):
            mu = jnp.mean(h, axis=-1, keepdims=True)
            var = jnp.var(h, axis=-1, keepdims=True)
            return (h - mu) * jax.lax.rsqrt(var + LN_EPS) * w + b
        B, T, C = x.shape
        qkv = x @ W_qkv + b_qkv
        q, k, v = jnp.split(qkv, 3, axis=-1)
        scale = np.sqrt(C * ATTN_SPAN).astype(np.float32)
        scores = jnp.einsum('bid,bjd->bij', q, k) / scale
        scores = scores * _band_mask(T, ATTN_SPAN, x.dtype)[None, :, :]
        out = jnp.einsum('bij,bjd->bid', scores, v)
        return _layer_norm(out, ln_w, ln_b)

    def _L0_cond2_ref(x, mask, g_norm, Wq, Wkv, q_scale, k_scale, null_kv, null_attn_bias, w0, b0, g0, w1, b1, g1, w2, b2, Wout, g_out):
        import jax, jax.numpy as jnp
        import numpy as np
        DIM = 128
        HEADS = 16
        DIM_HEAD = 64
        SCALE = 8.0

        def ln(x, g, eps=1e-05):
            mean = x.mean(axis=-1, keepdims=True)
            var = ((x - mean) ** 2).mean(axis=-1, keepdims=True)
            return (x - mean) * jax.lax.rsqrt(var + eps) * g

        def l2norm(t):
            n = jnp.maximum(jnp.linalg.norm(t, axis=-1, keepdims=True), 1e-12)
            return t / n

        def rel_pos_bias(n, w0, b0, g0, w1, b1, g1, w2, b2, dtype):
            pos = jnp.arange(-n + 1, n, dtype=dtype)[:, None]
            h = jax.nn.silu(ln(pos @ w0 + b0, g0))
            h = jax.nn.silu(ln(h @ w1 + b1, g1))
            h = h @ w2 + b2
            i = jnp.arange(n)
            idx = i[:, None] - i[None, :] + n - 1
            bias = h[idx]
            return jnp.transpose(bias, (2, 0, 1))
        b, n, _ = x.shape
        xn = ln(x, g_norm)
        q = (xn @ Wq).reshape(b, n, HEADS, DIM_HEAD).transpose(0, 2, 1, 3)
        kv = xn @ Wkv
        k, v = (kv[..., :DIM_HEAD], kv[..., DIM_HEAD:])
        nk = jnp.broadcast_to(null_kv[0], (b, 1, DIM_HEAD))
        nv = jnp.broadcast_to(null_kv[1], (b, 1, DIM_HEAD))
        k = jnp.concatenate([nk, k], axis=1)
        v = jnp.concatenate([nv, v], axis=1)
        q = l2norm(q) * q_scale
        k = l2norm(k) * k_scale
        sim = jnp.einsum('bhid,bjd->bhij', q, k) * SCALE
        bias = rel_pos_bias(n, w0, b0, g0, w1, b1, g1, w2, b2, q.dtype)
        null_bias = jnp.broadcast_to(null_attn_bias[:, None, None], (HEADS, n, 1))
        attn_bias = jnp.concatenate([null_bias, bias], axis=-1)
        sim = sim + attn_bias
        neg = -jnp.finfo(sim.dtype).max
        causal = jnp.triu(jnp.ones((n, n + 1), dtype=bool), k=2)
        sim = jnp.where(causal, neg, sim)
        m = jnp.pad(mask, ((0, 0), (1, 0)), constant_values=True)[:, None, None, :]
        sim = jnp.where(m, sim, neg)
        attn = jax.nn.softmax(sim, axis=-1)
        out = jnp.einsum('bhij,bjd->bhid', attn, v)
        out = out.transpose(0, 2, 1, 3).reshape(b, n, HEADS * DIM_HEAD)
        return ln(out @ Wout, g_out)

    def _L0_ffn_ref(x, w1_w, w1_s, w2_w, w2_s, h1_w, h1_s, h2_w, h2_s, w3_w, w3_s):
        import jax, jax.numpy as jnp
        import numpy as np
        D_IN, D_HID = (128, 512)

        def _ternary(key, shape):
            return jax.random.randint(key, shape, -1, 2).astype(jnp.float32)

        def _tlin(x, w, s):
            return jnp.einsum('bsi,oi->bso', x, w) * s
        h = jax.nn.silu(_tlin(x, w1_w, w1_s)) * _tlin(x, w2_w, w2_s)
        h = jax.nn.gelu(_tlin(h, h1_w, h1_s), approximate=False)
        h = jax.nn.gelu(_tlin(h, h2_w, h2_s), approximate=False)
        return _tlin(h, w3_w, w3_s)
    x = x + _L0_attn_ref(_L0_cond_ref(x, cond_64, L0_cond_wt, L0_cond_wg, L0_cond_w_gate, L0_cond_w_up, L0_cond_w_down, L0_cond_sw_gate, L0_cond_sw_up, L0_cond_sw_down), L0_attn_W_qkv, L0_attn_b_qkv, L0_attn_ln_w, L0_attn_ln_b)
    x = x + _L0_ffn_ref(_L0_cond2_ref(x, mask_BxS_bf1, L0_cond2_g_norm, L0_cond2_Wq, L0_cond2_Wkv, L0_cond2_q_scale, L0_cond2_k_scale, cond_64, L0_cond2_null_attn_bias, L0_cond2_w0, L0_cond2_b0, L0_cond2_g0, L0_cond2_w1, L0_cond2_b1, L0_cond2_g1, L0_cond2_w2, L0_cond2_b2, L0_cond2_Wout, L0_cond2_g_out), L0_ffn_w1_w, L0_ffn_w1_s, L0_ffn_w2_w, L0_ffn_w2_s, L0_ffn_h1_w, L0_ffn_h1_s, L0_ffn_h2_w, L0_ffn_h2_s, L0_ffn_w3_w, L0_ffn_w3_s)
    return x

_drawn_inputs = setup_inputs


def setup_inputs(seed=0):
    import zlib

    import numpy as np

    out = dict(_drawn_inputs(seed))
    spreads = {'L0_attn_ln_w': (1.0, 0.2),
     'L0_attn_ln_b': (0.0, 0.1),
     'L0_cond2_g_norm': (1.0, 0.2),
     'L0_cond2_q_scale': (1.0, 0.2),
     'L0_cond2_k_scale': (1.0, 0.2),
     'L0_cond2_b0': (0.0, 0.1),
     'L0_cond2_g0': (1.0, 0.2),
     'L0_cond2_b1': (0.0, 0.1),
     'L0_cond2_g1': (1.0, 0.2),
     'L0_cond2_b2': (0.0, 0.1),
     'L0_cond2_g_out': (1.0, 0.2)}
    factors = {}
    for name, (base, spread) in spreads.items():
        noise = np.random.default_rng([zlib.crc32(name.encode()), seed]).standard_normal(out[name].shape)
        drawn = base * np.exp(spread * noise) if base else spread * noise
        out[name] = jnp.asarray(drawn.astype(out[name].dtype))
    for name, factor in factors.items():
        out[name] = (out[name] * factor).astype(out[name].dtype)
    return out
```

```python
import concourse.bass as bass
from concourse import mybir
from contextlib import ExitStack

B, S, D = 32, 128, 128
GB = 4
NG = B // GB
GT = GB * S
E, EM = 8, 64
NC_ = E * EM // 128
NX = NC_ + 1
HEADS, DH = 16, 64
NP = HEADS // 2
NK = S + 1
HID = 512
NO = HID // 128
SPAN = 32
LN_EPS = 1e-5
BIG = 1e30
SCALE = 8.0

ORDER = (
    [("sim", 0), ("rw", 0), ("exp", 0), ("exp", 1), ("ex", 0), ("bias", 2), ("exp", 2), ("PT", 0), ("exp", 3), ("PV", 0),
     ("exp", 4), ("OT", 0), ("zT", 0), ("z", 0)]
    + [("sim", 1), ("l1", 0), ("l1", 1), ("ex", 1), ("bias", 3), ("l1", 2), ("l1", 3), ("down", 0), ("PT", 1), ("qkv", 0),
       ("PV", 1), ("l2", 0), ("OT", 1), ("scores", 0), ("z", 1)]
    + [("sim", 2), ("l2", 1), ("ex", 2), ("l2", 2), ("l2", 3), ("PT", 2), ("move1", 0), ("move2", 0), ("mix", 0), ("PV", 2),
       ("l3", 0), ("OT", 2), ("bias+", 0), ("z", 2)]
    + [("sim", 3), ("l3", 1), ("ex", 3), ("bias+", 1), ("l3", 2), ("l3", 3), ("PT", 3), ("xnT", 0), ("kv", 0), ("PV", 3),
       ("q", 0), ("OT", 3), ("q", 1), ("z", 3)]
    + [("q", 2), ("q", 3), ("q", 4), ("kT", 0), ("q", 5), ("q", 6), ("q", 7), ("ssq", 0), ("l4", 0)]
)
STAGE = {s: "A" for s in ("rw", "exp", "down", "qkv", "scores", "mix", "xnT", "kv", "q", "ssq", "kT", "bias+")}
STAGE |= {s: "B" for s in ("bias", "sim", "ex", "PT", "PV", "OT", "z", "move2")}
STAGE |= {s: "C" for s in ("zT", "l1", "l2", "l3", "l4", "move1")}
LOOP = 2
SHIFT = {"A": 1, "B": 0, "C": -1}

USES = {"rw": "M", "exp": "MMM", "down": "M", "qkv": "MMM", "scores": "M", "mix": "M", "xnT": "M",
        "kv": "M", "q": "M", "ssq": "", "kT": "M", "sim": "S" * NP, "PT": "TTTT", "PV": "TT", "OT": "TT", "zT": "M",
        "l1": "MM", "l2": "M", "l3": "M", "l4": "M"}
BANKS = {"M": 3, "S": 2, "T": 2}


def uses(step, k):
    if (step, k) == ("q", 0):
        return "MS"
    return "MM" if (step, k) == ("exp", NX - 1) else USES.get(step, "")


def stages_of(it):
    return [s for s in "ABC" if 0 <= it + SHIFT[s] < NG]


def bank_plan():
    last, plan = {}, {}
    for it in range(-1, NG + 1):
        active, turn, here = stages_of(it), {r: 0 for r in BANKS}, {}
        for step, k in ORDER:
            for n, ring in enumerate(uses(step, k)):
                bank = (ring, turn[ring] % BANKS[ring])
                turn[ring] += 1
                if STAGE[step] not in active:
                    continue
                here[step, k, n] = (bank, last.get(bank), it)
                last[bank] = (step, k, n, it)
        plan[it] = {u: (bank, before and (*before[:3], it - before[3])) for u, (bank, before, _) in here.items()}
    for it in range(LOOP, NG - 1):
        assert plan[it] == plan[LOOP], "the loop's iterations differ"
    return plan


PLAN = bank_plan()


def layer_kernel(nc, a, out):
    fp32, u8 = mybir.dt.float32, mybir.dt.uint8
    ALU, ACT, AX = mybir.AluOpType, mybir.ActivationFunctionType, mybir.AxisListType.X
    ctx = ExitStack()
    with ctx:
        def sb(name, shape, dt=fp32):
            return ctx.enter_context(nc.sbuf_tensor("sb_" + name, shape, dt))

        def sem(name):
            return ctx.enter_context(nc.semaphore("s_" + name))

        class Signal:

            def __init__(self, name, per_group):
                self.sem, self.per = sem(name), per_group

            def at(self, g, n):
                v = g * self.per + n
                return max(v, 0) if isinstance(v, int) else v

        xg = sb("xg", [128, GT])
        xs = sb("xs", [128, GB, D])
        x1 = sb("x1", [128, 3, GB, D])
        wg, wu = sb("wg", [128, NX * 128]), sb("wu", [128, NX * 128])
        wd = sb("wd", [128, NX, D])
        wqkv = sb("wqkv", [128, 3 * D])
        wq2, wkv2, wout = sb("wq2", [128, HEADS * DH]), sb("wkv2", [128, 2 * DH]), sb("wout", [128, NP, D])
        w1, w2 = sb("w1", [128, HID]), sb("w2", [128, HID])
        h1, h2, w3 = sb("h1", [128, NO, HID]), sb("h2", [128, NO, HID]), sb("w3", [128, NO, D])
        wt, wgT, condT = sb("wt", [128, E]), sb("wgT", [64, E]), sb("condT", [64, B])
        pw1, pw2, pb2 = sb("pw1", [128, 128]), sb("pw2", [128, HEADS]), sb("pb2", [HEADS, 1])
        NCOL = 4 * NO + 8
        cols = sb("cols", [128, NCOL])
        w1s, w2s, h1s, h2s = (cols[:, NO * i:NO * i + NO] for i in range(4))
        bq, bk, gnorm, gout, qsc, ksc, nkey, nval = (cols[:, 4 * NO + i:4 * NO + i + 1] for i in range(8))
        NROW = 9 * 128 + 2 * DH + HEADS
        rows = sb("rows", [128, NROW])
        lnw, lnb, bv, w3s, pw0, pb0, pg0, pb1, pg1 = (rows[:, 128 * i:128 * i + 128] for i in range(9))
        nkey_r, nval_r = rows[:, 1152:1152 + DH], rows[:, 1152 + DH:1152 + 2 * DH]
        nbias = rows[:, 1152 + 2 * DH:NROW]
        mask = sb("mask", [128, GB, S], u8)
        ident = sb("ident", [128, 128])
        band = sb("band", [128, 128])
        halves = sb("halves", [128, 2])
        ones = sb("ones", [64, 128])
        sel = sb("sel", [E, NC_, 128])
        eps = sb("eps", [128, GB])
        mhalf = sb("mhalf", [128, 16])
        route = sb("route", [128, B * E])[:]
        rg = sb("rg", [128, GB * E])
        wT = sb("wT", [E, GT])
        bias0 = sb("bias0", [128, HEADS, S])
        biasm = sb("biasm", [128, 2, HEADS, NK])
        maskn = sb("maskn", [128, GB, S])
        gs = sb("gs", [128, 2, GT])
        hT = sb("hT", [128, NX, GT])
        yT, qT, kT = sb("yT", [128, GT]), sb("qT", [128, GT]), sb("kT", [128, GT])
        v1, st = sb("v1", [128, GB, D]), sb("st", [128, GB, S])
        n1, xnT = sb("n1", [128, GB, D]), sb("xnT", [128, GT])
        bs = sb("bs", [128, 3, GB, 6])
        mv = sb("mv", [128, 3, GB, 2])
        ve = sb("ve", [128, 3, GB])
        idle = sb("idle", [128, 1])
        rstd = sb("rstd", [128, 3, GB])
        sq, qs = sb("sq", [128, 2, GT]), sb("qs", [128, NP, GT])
        kv, ksq = sb("kv", [128, GB, 2 * DH]), sb("ksq", [128, GB, DH])
        vd, kd = sb("vd", [128, GB, DH]), sb("kd", [128, GB, 2, DH])
        ss, rk = sb("ss", [128, GB]), sb("rk", [128, GB])
        qss, rq = sb("qss", [128, GB * HEADS]), sb("rq", [128, GB * HEADS])
        kbd = sb("kbd", [128, GB, 2, NK])
        sm = sb("sm", [128, 2, HEADS, NK])
        nmx, den, rden = sb("nmx", [128, 2, HEADS]), sb("den", [128, 2, HEADS]), sb("rden", [128, HEADS])
        pT, on, oT = sb("pT", [128, HEADS, S]), sb("on", [128, HEADS, DH]), sb("oT", [128, NP, S])
        n3, zT = sb("n3", [128, GB, D]), sb("zT", [128, GT])
        al, hA, hB = sb("al", [128, 2, GT]), sb("hA", [128, NO, GT]), sb("hB", [128, NO, GT])
        res = sb("res", [128, GB, D])
        xT = qs[:].rearrange("p c t -> p (c t)")
        lgt, *rt = (hA[:, i // 2, i % 2 * 256:(i % 2 + 1) * 256] for i in range(8))
        ph = [hB[:, 0, 128 * i:128 * i + 128] for i in range(4)]
        nks = hB[:, 1, 0:DH]
        flip = hB[:, 1, 256:384]
        prev = hB[0:HEADS, 2, 0:2 * S]
        cg = hB[0:64, 3, 0:B * E]
        r1 = [hB[:, 1, 64 + B * i:64 + B * (i + 1)] for i in range(6)]
        prank = sb("prank", [128, E])
        pos = sb("pos", [128, 1])
        pi = sb("pi", [128, 1], mybir.dt.int32)
        pst = sb("pst", [128, 6])
        pmv = sb("pmv", [128, 2])
        prs = sb("prs", [128, 2])
        nkr = sb("nkr", [128, 3])

        banks = {(r, i): ctx.enter_context(nc.psum_tensor(f"ps_{r}{i}", [128, 512], fp32))
                 for r, n in BANKS.items() for i in range(n)}
        zbank = ctx.enter_context(nc.psum_tensor("ps_z", [128, 512], fp32))
        toeplitz = nc.dram_tensor("toeplitz", (HEADS, 2 * S), fp32, kind="Internal").ap()

        load = {n: sem("ld_" + n) for n in a if n not in ("x", "mask")}
        mask_loaded = Signal("mask_loaded", 16)
        s_toep, s_toepl = sem("toep_stored"), sem("bias_loaded")
        const = sem("const")
        pa, pd, pp, pg = sem("pro_act"), sem("pro_dve"), sem("pro_pe"), sem("pro_pool")
        x_loaded, xs_loaded = Signal("x_loaded", 16), Signal("xs_loaded", 16)
        xb_ready = Signal("xb_ready", 1)
        x1_in_b, x1_in_c = Signal("x1_in_b", 1), Signal("x1_in_c", 1)
        own_x = Signal("own_x", 4)
        rw_taken, rw_psum, rw_turned = Signal("rw_taken", 1), Signal("rw_psum", 1), Signal("rw_turned", 1)
        expert_psum = Signal("expert_psum", 3 * NX - 1)
        gate_copied = Signal("gate_copied", NX)
        leaked = Signal("leaked", NX)
        upped = Signal("upped", NC_)
        hidden = Signal("hidden", NX)
        y_psum, y_copied = Signal("y_psum", 1), Signal("y_copied", 1)
        qkv_psum, qk_copied, v_ready = Signal("qkv_psum", 3), Signal("qk_copied", 2), Signal("v_ready", 1)
        scores_psum, banded = Signal("scores_psum", 1), Signal("banded", 1)
        mix_psum = Signal("mix_psum", 1)
        mixed = Signal("mixed", 1)
        n2_ready, xn_psum, xn_copied = Signal("n2_ready", 1), Signal("xn_psum", 1), Signal("xn_copied", 1)
        ln_var = {s: Signal("var_" + s, n) for s, n in (("x", 2), ("z", 1))}
        ln_eps = {s: Signal("eps_" + s, n) for s, n in (("x", 2), ("z", 1))}
        ln_rstd = {s: Signal("rstd_" + s, n) for s, n in (("x", 2), ("z", 1))}
        kv_psum, kv_copied, v_shifted = Signal("kv_psum", 1), Signal("kv_copied", 1), Signal("v_shifted", 1)
        k_squares, k_rnorm, k_normed = Signal("k_squares", 1), Signal("k_rnorm", 1), Signal("k_normed", 1)
        kT_psum, kT_copied = Signal("kT_psum", 1), Signal("kT_copied", 1)
        q_psum, q_squared, q_copied = Signal("q_psum", NP), Signal("q_squared", NP), Signal("q_copied", NP)
        ssq_psum, ssq_copied, q_rnorm = Signal("ssq_psum", NP), Signal("ssq_copied", 1), Signal("q_rnorm", GB)
        mask_row, bias_ready = Signal("mask_row", 1), Signal("bias_ready", GB)
        sim_psum, biased = Signal("sim_psum", GB * NP), Signal("biased", GB * NP)
        max_ready, exps = Signal("max_ready", GB), Signal("exps", GB * 4)
        pt_psum = Signal("pt_psum", GB * 4)
        pt_act, pt_dve = Signal("pt_act", GB * 2), Signal("pt_dve", GB * 2)
        rden_ready = Signal("rden_ready", GB)
        pv_psum, normed = Signal("pv_psum", GB * 2), Signal("normed", GB * 2)
        ot_psum, ot_copied = Signal("ot_psum", GB * 2), Signal("ot_copied", GB * 2)
        z_psum, n3_ready = Signal("z_psum", GB), Signal("n3_ready", 1)
        zT_psum, zT_copied = Signal("zT_psum", 1), Signal("zT_copied", 1)
        l1_psum, silued, l1_ready = Signal("l1_psum", 2 * NO), Signal("silued", NO), Signal("l1_ready", NO)
        l2_psum, l2_ready = Signal("l2_psum", NO), Signal("l2_ready", NO)
        l3_psum, l3_ready = Signal("l3_psum", NO), Signal("l3_ready", NO)
        l4_psum, scaled, out_ready = Signal("l4_psum", 1), Signal("scaled", 1), Signal("out_ready", 1)
        stored = sem("stored")

        DRAINED = {}
        for c in range(NX):
            DRAINED |= {("exp", c, 0): (gate_copied, c + 1), ("exp", c, 2): (hidden, c + 1),
                        ("exp", c, 1): (upped, c + 1) if c < NC_ else (hidden, c + 1)}
        DRAINED |= {("rw", 0, 0): (rw_turned, 1), ("down", 0, 0): (y_copied, 1), ("qkv", 0, 0): (qk_copied, 1), ("qkv", 0, 1): (qk_copied, 2),
                    ("qkv", 0, 2): (v_ready, 1), ("scores", 0, 0): (banded, 1), ("mix", 0, 0): (mixed, 1),
                    ("xnT", 0, 0): (xn_copied, 1), ("kv", 0, 0): (kv_copied, 1), ("q", 0, 1): (ssq_copied, 1),
                    ("kT", 0, 0): (kT_copied, 1), ("zT", 0, 0): (zT_copied, 1), ("l4", 0, 0): (scaled, 1)}
        DRAINED |= {("q", c, 0): (q_copied, c + 1) for c in range(NP)}
        for k in range(GB):
            DRAINED |= {("sim", k, p): (biased, k * NP + p + 1) for p in range(NP)}
            DRAINED |= {("PT", k, n): ((pt_act, pt_dve)[n % 2], 2 * k + n // 2 + 1) for n in range(4)}
            DRAINED |= {("PV", k, n): (normed, 2 * k + n + 1) for n in range(2)}
            DRAINED |= {("OT", k, n): (ot_copied, 2 * k + n + 1) for n in range(2)}
        for o in range(NO):
            DRAINED |= {("l1", o, 0): (silued, o + 1), ("l1", o, 1): (l1_ready, o + 1),
                        ("l2", o, 0): (l2_ready, o + 1), ("l3", o, 0): (l3_ready, o + 1)}

        def kind(it):
            return it if isinstance(it, int) else LOOP

        def bank(it, step, k, n=0):
            return banks[PLAN[kind(it)][step, k, n][0]]

        def drained_before(it, step, k, n=0):
            before = PLAN[kind(it)][step, k, n][1]
            if before is None:
                return const, 0
            signal, count = DRAINED[before[:3]]
            g = it - before[3] + SHIFT[STAGE[before[0]]]
            return signal.sem, signal.at(g, count)

        def iterations(eng, steps):
            def body(it):
                for step, k in ORDER:
                    if STAGE[step] in stages_of(kind(it)) and step in steps:
                        steps[step](it, it + SHIFT[STAGE[step]], k)
            for it in range(-1, LOOP):
                body(it)
            with eng.Fori(LOOP, NG - 1) as it:
                body(it)
            body(NG - 1)
            body(NG)

        block = ctx.enter_context(nc.Block())

        @block.sync
        def _(sp):
            def fetch(name, dst, src=None):
                sp.dma_start(dst, a[name] if src is None else src).then_inc(load[name], 16)

            fetch("cols", cols[:])
            fetch("rows", rows[:], bass.AP(tensor=a["rows"].tensor, offset=0, ap=[[0, 128], [1, NROW]]))
            fetch("wt", wt[:])
            fetch("wgT", wgT[:])
            fetch("condT", condT[:])
            fetch("pw1", pw1[:])
            fetch("pw2", pw2[:])
            fetch("pb2", pb2[:])
            fetch("xT", xT)
            fetch("wg", wg[:])
            fetch("wu", wu[:])
            fetch("wd", wd[:])
            fetch("wqkv", wqkv[:])
            sp.wait_ge(pa, 5)
            sp.dma_start(toeplitz, prev).then_inc(s_toep, 16)
            sp.wait_ge(s_toep, 16)
            sp.dma_start(pT[:], bass.AP(tensor=toeplitz.tensor, offset=0,
                                        ap=[[1, 128], [2 * S, HEADS], [1, S]])).then_inc(s_toepl, 16)
            fetch("wq2", wq2[:])
            fetch("wkv2", wkv2[:])
            fetch("wout", wout[:])
            fetch("w1", w1[:])
            fetch("w2", w2[:])
            fetch("h1", h1[:])
            fetch("h2", h2[:])
            fetch("w3", w3[:])

            def load_x(it, g, k):
                sp.wait_ge(expert_psum.sem, expert_psum.at(g, 0))
                sp.dma_start(xg[:], a["xT"][:, bass.ds(g * GT, GT)]).then_inc(x_loaded.sem, 16)
                sp.wait_ge(own_x.sem, own_x.at(g, 0))
                sp.dma_start(xs[:], a["x"][bass.ds(g * GB, GB), :, :].rearrange("b p f -> p b f"))\
                    .then_inc(xs_loaded.sem, 16)

            def load_mask(it, g, k):
                first = g * GT if isinstance(g, int) else sp.snap(g * GT)
                sp.wait_ge(mask_row.sem, mask_row.at(g, 0))
                sp.dma_start(mask[:].rearrange("p b s -> p (b s)"), a["mask"][bass.ds(first, GT)].unsqueeze(0).broadcast_to([128, GT]))\
                    .then_inc(mask_loaded.sem, 16)

            def store(it, g, k):
                sp.wait_ge(out_ready.sem, out_ready.at(g, 1))
                sp.dma_start(out[bass.ds(g * GB, GB), :, :].rearrange("b p f -> p b f"), res[:]).then_inc(stored, 16)

            iterations(sp, {"rw": load_x, "mix": load_mask, "l4": store})
            sp.wait_ge(stored, 16 * NG)

        @block.gpsimd
        def _(pool):
            pool.memset(ident[:], 0.0)
            pool.memset(band[:], 1.0 / 64.0)
            pool.memset(sel[:], 0.0)
            pool.memset(ones[:], 1.0)
            pool.memset(eps[:], LN_EPS)
            pool.memset(mhalf[:], -0.5)
            pool.memset(kbd[:], 0.0)
            pool.memset(prev, -BIG)
            pool.memset(flip, 0.0)
            pool.iota(pi[:], [[0, 1]], base=S - 1, channel_multiplier=-1).then_inc(const, 1)
            pool.wait_ge(const, 1)
            pool.affine_select(ident[:], ident[:], [[-1, 128]], ALU.not_equal, 1.0, base=0, channel_multiplier=1)
            pool.affine_select(flip, flip, [[1, 128]], ALU.not_equal, 1.0, base=1 - S, channel_multiplier=1)
            pool.affine_select(band[:], band[:], [[1, 128]], ALU.is_ge, 0.0, base=0, channel_multiplier=-1)
            pool.affine_select(sel[:].rearrange("e c (a m) -> e c a m", a=2), sel[:].rearrange("e c (a m) -> e c a m", a=2),
                               [[-2, NC_], [-1, 2], [0, EM]], ALU.not_equal, 1.0, base=0, channel_multiplier=1)
            for e in range(E):
                pool.memset(prank[:, e:e + 1], float(E - e))
            pool.tensor_copy(pos[:], pi[:]).then_inc(const, 1)
            pool.wait_ge(const, 2)
            pool.affine_select(band[:], band[:], [[-1, 128]], ALU.is_ge, 0.0, base=SPAN - 1, channel_multiplier=1)\
                .then_inc(const, 1)

            def power(out_, var, base, add, gate):
                pool.wait_ge(pd, gate)
                pool.tensor_scalar(prs[:, 0:1], var, add, 1.0, ALU.add, ALU.mult).then_inc(pg, 1)
                pool.wait_ge(pg, base)
                pool.tensor_tensor(out_, prs[:, 0:1], mhalf[:, 0:1], ALU.pow).then_inc(pg, 1)

            power(prs[:, 1:2], pmv[:, 1:2], 1, LN_EPS, 4)
            power(prs[:, 1:2], pmv[:, 1:2], 3, LN_EPS, 9)
            pool.wait_ge(pd, 15)
            pool.tensor_tensor(nkr[:, 2:3], nkr[:, 1:2], mhalf[:, 0:1], ALU.pow).then_inc(pg, 1)
            pool.wait_ge(load["rows"], 16)
            for b in range(2):
                last = pool.tensor_copy(biasm[:, b, :, 0], nbias)
            last.then_inc(pg, 1)
            pool.wait_ge(pa, 10)

            def rsqrt(src, dst, eps_buf, which, ln, n):
                def part(it, g, k):
                    pool.wait_ge(ln_var[ln].sem, ln_var[ln].at(g, n))
                    pool.tensor_tensor(ve[:, which], mv[:, which, :, 1], eps[:], ALU.add)\
                        .then_inc(ln_eps[ln].sem, 1)
                    pool.wait_ge(ln_eps[ln].sem, ln_eps[ln].at(g, n))
                    pool.tensor_tensor(rstd[:, which], ve[:, which], mhalf[:, 0:GB], ALU.pow)\
                        .then_inc(ln_rstd[ln].sem, 1)
                return part

            ln1, ln2, ln3 = (rsqrt(None, None, None, w, s, n) for w, s, n in ((0, "x", 1), (1, "x", 2), (2, "z", 1)))

            def norms(it, g, k):
                pool.wait_ge(xs_loaded.sem, xs_loaded.at(g, 16))
                pool.tensor_tensor(xs[:], xs[:], lnb.unsqueeze(1).broadcast_to([128, GB, D]), ALU.add)\
                    .then_inc(xb_ready.sem, 1)
                ln1(it, g, k)
                ln2(it, g, k)

            def k_norm(it, g, k):
                pool.wait_ge(k_squares.sem, k_squares.at(g, 1))
                pool.tensor_tensor(rk[:], ss[:], mhalf[:, 0:GB], ALU.pow).then_inc(k_rnorm.sem, 1)

            def q_norm(it, g, k):
                pool.wait_ge(ssq_copied.sem, ssq_copied.at(g, 1))
                for b in range(GB):
                    cut = slice(b * HEADS, (b + 1) * HEADS)
                    pool.tensor_tensor(rq[:, cut], qss[:, cut], mhalf[:], ALU.pow).then_inc(q_rnorm.sem, 1)

            def bias(it, g, k):
                pool.wait_ge(mask_row.sem, mask_row.at(g, 1))
                pool.wait_ge(biased.sem, biased.at(g, (k - 1) * NP) if k >= 1 else biased.at(g - 1, (GB - 1) * NP))
                pool.tensor_tensor(biasm[:, k % 2, :, 1:NK], bias0[:],
                                   maskn[:, k].unsqueeze(1).broadcast_to([128, HEADS, S]), ALU.add)\
                    .then_inc(bias_ready.sem, 1)

            iterations(pool, {"mix": norms, "kv": k_norm, "ssq": q_norm, "bias": bias, "bias+": bias, "zT": ln3})

        @block.scalar
        def _(act):
            for n in range(2):
                act.wait_ge(pd, (6, 11)[n])
                act.activation(ph[1], ph[0], ACT.Silu).then_inc(pa, 1)
                act.wait_ge(pp, 1 + 2 * n)
                act.activation(ph[2], banks["S", 0][:, 0:128], ACT.Copy).then_inc(pa, 1)
            act.wait_ge(pp, 4)
            act.wait_ge(load["pb2"], 16)
            act.activation(prev[:, 0:S], banks["S", 1][0:HEADS, 0:S], ACT.Identity, bias=pb2[:]).then_inc(pa, 1)
            act.wait_ge(pd, 19)
            act.activation(rt[1], rt[0], ACT.Exp).then_inc(pa, 1)

            for n in range(4):
                act.wait_ge(pp, 6 + n)
                act.activation(bias0[:, 4 * n:4 * n + 4].rearrange("p h s -> p (h s)"),
                               banks["ST"[n // 2], n % 2][:], ACT.Copy).then_inc(pa, 1)

            def expert(it, g, c):
                act.wait_ge(expert_psum.sem, expert_psum.at(g, 3 * c + 1))
                act.wait_ge(hidden.sem, hidden.at(g, max(c - 1, 0)))
                act.activation(gs[:, c % 2], bank(it, "exp", c, 0)[:], ACT.Copy).then_inc(gate_copied.sem, 1)

            def rw_copy(it, g, k):
                act.wait_ge(rw_psum.sem, rw_psum.at(g, 1))
                act.wait_ge(expert_psum.sem, expert_psum.at(g, 0))
                act.activation(wT[:], bank(it, "rw", 0)[0:E], ACT.Copy).then_inc(rw_turned.sem, 1)

            def y_copy(it, g, k):
                act.wait_ge(y_psum.sem, y_psum.at(g, 1))
                act.wait_ge(qkv_psum.sem, qkv_psum.at(g, 0))
                act.activation(yT[:], bank(it, "down", 0)[:], ACT.Copy).then_inc(y_copied.sem, 1)

            def qk(it, g, k):
                for n, (dst, b) in enumerate(((qT, bq), (kT, bk))):
                    act.wait_ge(qkv_psum.sem, qkv_psum.at(g, n + 1))
                    act.wait_ge(scores_psum.sem, scores_psum.at(g, 0))
                    act.activation(dst[:], bank(it, "qkv", 0, n)[:], ACT.Identity, bias=b).then_inc(qk_copied.sem, 1)

            def xn(it, g, k):
                act.wait_ge(xn_psum.sem, xn_psum.at(g, 1))
                act.wait_ge(kv_psum.sem, kv_psum.at(g, 0))
                act.wait_ge(q_psum.sem, q_psum.at(g, 0))
                act.activation(xnT[:], bank(it, "xnT", 0)[:], ACT.Copy, scale=gnorm).then_inc(xn_copied.sem, 1)

            def q_tile(it, g, c):
                act.wait_ge(q_psum.sem, q_psum.at(g, c + 1))
                act.wait_ge(ssq_psum.sem, ssq_psum.at(g, max(c - 1, 0)))
                act.activation(sq[:, c % 2], bank(it, "q", c)[:], ACT.Square).then_inc(q_squared.sem, 1)

            def kT_copy(it, g, k):
                act.wait_ge(kT_psum.sem, kT_psum.at(g, 1))
                act.wait_ge(sim_psum.sem, sim_psum.at(g, 0))
                src = bank(it, "kT", 0)[:].rearrange("p (b s) -> p b s", b=GB)
                act.activation(kbd[0:64, :, 0, 1:NK], src[0:64], ACT.Copy, scale=ksc[0:64])
                act.activation(kbd[64:128, :, 1, 1:NK], src[64:128], ACT.Copy, scale=ksc[64:128])\
                    .then_inc(kT_copied.sem, 1)

            def exp(it, g, k):
                act.wait_ge(max_ready.sem, max_ready.at(g, k + 1))
                act.wait_ge(rden_ready.sem, rden_ready.at(g, k - 1) if k >= 1 else rden_ready.at(g - 1, GB - 1))
                for h in range(HEADS):
                    ins = act.activation(sm[:, k % 2, h], sm[:, k % 2, h], ACT.Exp, bias=nmx[:, k % 2, h:h + 1],
                                         accum_out=den[:, k % 2, h:h + 1])
                    if h % 4 == 3:
                        ins.then_inc(exps.sem, 1)

            def pt_copy(it, g, k):
                for n in (0, 2):
                    act.wait_ge(pt_psum.sem, pt_psum.at(g, 4 * k + n + 1))
                    act.wait_ge(pv_psum.sem, pv_psum.at(g, 2 * k))
                    act.activation(pT[:, 4 * n:4 * n + 4].rearrange("p h s -> p (h s)"), bank(it, "PT", k, n)[:],
                                   ACT.Copy).then_inc(pt_act.sem, 1)

            def ot_copy(it, g, k):
                for n in range(2):
                    act.wait_ge(ot_psum.sem, ot_psum.at(g, 2 * k + n + 1))
                    act.wait_ge(z_psum.sem, z_psum.at(g, k))
                    act.activation(oT[:, 4 * n:4 * n + 4].rearrange("p c s -> p (c s)"), bank(it, "OT", k, n)[:],
                                   ACT.Identity, bias=nval).then_inc(ot_copied.sem, 1)

            def zT_copy(it, g, k):
                act.wait_ge(zT_psum.sem, zT_psum.at(g, 1))
                act.wait_ge(l1_psum.sem, l1_psum.at(g, 0))
                act.activation(zT[:], bank(it, "zT", 0)[:], ACT.Copy, scale=gout).then_inc(zT_copied.sem, 1)

            def silu(it, g, o):
                act.wait_ge(l1_psum.sem, l1_psum.at(g, 2 * o + 1))
                act.wait_ge(l1_ready.sem, l1_ready.at(g, max(o - 1, 0)))
                act.activation(al[:, o % 2], bank(it, "l1", o, 0)[:], ACT.Silu, scale=w1s[:, o:o + 1])\
                    .then_inc(silued.sem, 1)

            def gelu2(it, g, o):
                act.wait_ge(l2_psum.sem, l2_psum.at(g, o + 1))
                act.wait_ge(l3_psum.sem, l3_psum.at(g, 0))
                act.activation(hB[:, o], bank(it, "l2", o)[:], ACT.Gelu, scale=h1s[:, o:o + 1]).then_inc(l2_ready.sem, 1)

            def gelu3(it, g, o):
                act.wait_ge(l3_psum.sem, l3_psum.at(g, o + 1))
                act.wait_ge(l2_psum.sem, l2_psum.at(g, NO))
                act.activation(hA[:, o], bank(it, "l3", o)[:], ACT.Gelu, scale=h2s[:, o:o + 1]).then_inc(l3_ready.sem, 1)

            act.wait_ge(load["cols"], 16)
            iterations(act, {"rw": rw_copy, "exp": expert, "down": y_copy, "qkv": qk, "xnT": xn, "q": q_tile, "kT": kT_copy,
                             "ex": exp, "PT": pt_copy, "OT": ot_copy, "zT": zT_copy,
                             "l1": silu, "l2": gelu2, "l3": gelu3})

        @block.vector
        def _(dve):
            done = [0]

            def link(ins):
                done[0] += 1
                ins.then_inc(pd, 1)
                dve.wait_ge(pd, done[0])

            def te(t):
                return t.rearrange("p (b e) -> p b e", e=E)

            def over(t):
                return t.unsqueeze(2).broadcast_to([128, B, E])

            for n in range(2):
                for m in range(2):
                    dve.memset(halves[64 * m:64 * m + 64, n:n + 1], float(n == m))
            dve.wait_ge(load["rows"], 16)
            dve.wait_ge(const, 3)
            link(dve.scalar_tensor_tensor(ph[3], pw0, pos[:], pb0, ALU.mult, ALU.add))
            link(dve.bn_stats(pst[:], ph[3]))
            link(dve.bn_aggr(pmv[:], pst[:]))
            dve.wait_ge(load["condT"], 16)
            dve.wait_ge(load["wgT"], 16)
            link(dve.tensor_tensor(cg.rearrange("p (b e) -> p b e", e=E), condT[:].unsqueeze(2).broadcast_to([64, B, E]),
                                   wgT[:].unsqueeze(1).broadcast_to([64, B, E]), ALU.mult))
            dve.wait_ge(pg, 2)
            link(dve.tensor_scalar(ph[0], ph[3], pmv[:, 0:1], prs[:, 1:2], ALU.subtract, ALU.mult))
            link(dve.tensor_tensor(ph[0], ph[0], pg0, ALU.mult))
            dve.wait_ge(pp, 2)
            link(dve.tensor_tensor(ph[3], banks["S", 1][:, 0:128], pb1, ALU.add))
            link(dve.bn_stats(pst[:], ph[3]))
            link(dve.bn_aggr(pmv[:], pst[:]))
            dve.wait_ge(pg, 4)
            link(dve.tensor_scalar(ph[0], ph[3], pmv[:, 0:1], prs[:, 1:2], ALU.subtract, ALU.mult))
            link(dve.tensor_tensor(ph[0], ph[0], pg1, ALU.mult))
            link(dve.tensor_tensor(nks, nkey_r, nkey_r, ALU.mult))
            link(dve.tensor_reduce(nkr[:, 0:1], nks, AX, ALU.add))
            dve.wait_ge(load["cols"], 16)
            link(dve.tensor_scalar(nkr[:, 1:2], nkr[:, 0:1], 1e-24, None, ALU.max))
            link(dve.tensor_copy(nkr[:, 0:1], nkey))
            dve.wait_ge(pg, 5)
            for b in range(GB):
                for n in range(2):
                    half = slice(64 * n, 64 * n + 64)
                    ins = dve.tensor_scalar(kbd[half, b, n, 0:1], nkr[half, 0:1], nkr[half, 2:3], ksc[half],
                                            ALU.mult, ALU.mult)
            link(ins)
            dve.wait_ge(pp, 5)
            link(dve.tensor_scalar(lgt, banks["M", 0][:, 0:B * E], 0.5, None, ALU.mult))
            link(dve.tensor_reduce(r1[0], te(lgt), AX, ALU.max))
            link(dve.tensor_tensor(te(rt[0]), te(lgt), over(r1[0]), ALU.subtract))
            dve.wait_ge(pa, 6)
            link(dve.tensor_reduce(r1[1], te(rt[1]), AX, ALU.add))
            link(dve.reciprocal(r1[2], r1[1]))
            link(dve.tensor_tensor(te(rt[2]), te(rt[1]), over(r1[2]), ALU.mult))
            rank = prank[:].unsqueeze(1).broadcast_to([128, B, E])

            def pick(scores, top, onehot):
                link(dve.tensor_reduce(top, te(scores), AX, ALU.max))
                link(dve.tensor_tensor(te(rt[3]), te(scores), over(top), ALU.is_equal))
                link(dve.tensor_tensor(te(rt[3]), te(rt[3]), rank, ALU.mult))
                link(dve.tensor_reduce(r1[5], te(rt[3]), AX, ALU.max))
                link(dve.tensor_tensor(te(onehot), rank, over(r1[5]), ALU.is_equal))

            pick(rt[2], r1[3], rt[4])
            link(dve.scalar_tensor_tensor(rt[5], rt[4], -4.0, rt[2], ALU.mult, ALU.add))
            pick(rt[5], r1[4], rt[6])
            link(dve.tensor_tensor(r1[0], r1[3], r1[4], ALU.add))
            link(dve.tensor_scalar(r1[0], r1[0], 1e-20, None, ALU.add))
            link(dve.reciprocal(r1[1], r1[0]))
            link(dve.tensor_tensor(route, rt[4], rt[6], ALU.add))
            link(dve.tensor_tensor(route, route, rt[2], ALU.mult))
            link(dve.tensor_tensor(te(route), te(route), over(r1[1]), ALU.mult))
            ROUTED.append(done[0])

            own = {"x": own_x, "k": Signal("own_k", 2), "z": Signal("own_z", 1)}

            def row4(r):
                return r.unsqueeze(1).broadcast_to([128, GB, D])

            def expert(it, g, c):
                dve.wait_ge(gate_copied.sem, gate_copied.at(g, c + 1))
                dve.scalar_tensor_tensor(gs[:, c % 2], gs[:, c % 2], 0.01, gs[:, c % 2], ALU.mult, ALU.max)\
                    .then_inc(leaked.sem, 1)
                dve.wait_ge(expert_psum.sem, expert_psum.at(g, 3 * c + 2))
                dve.wait_ge(leaked.sem, leaked.at(g, c + 1))
                dve.wait_ge(y_psum.sem, y_psum.at(g, 0))
                if c < NC_:
                    dve.tensor_tensor(gs[:, c % 2], bank(it, "exp", c, 1)[:], gs[:, c % 2], ALU.mult)\
                        .then_inc(upped.sem, 1)
                    dve.wait_ge(expert_psum.sem, expert_psum.at(g, 3 * c + 3))
                    dve.wait_ge(upped.sem, upped.at(g, c + 1))
                    dve.tensor_tensor(hT[:, c], bank(it, "exp", c, 2)[:], gs[:, c % 2], ALU.mult)\
                        .then_inc(hidden.sem, 1)
                else:
                    dve.tensor_tensor(hT[:, c], bank(it, "exp", c, 1)[:], gs[:, c % 2], ALU.mult)\
                        .then_inc(hidden.sem, 1)

            def rw_take(it, g, k):
                dve.wait_ge(rw_psum.sem, rw_psum.at(g, 0))
                dve.tensor_copy(rg[:], route[:, bass.ds(g * GB * E, GB * E)]).then_inc(rw_taken.sem, 1)

            def values(it, g, k):
                dve.wait_ge(qkv_psum.sem, qkv_psum.at(g, 3))
                dve.wait_ge(mix_psum.sem, mix_psum.at(g, 0))
                dve.tensor_tensor(v1[:], bank(it, "qkv", 0, 2)[:].rearrange("p (b d) -> p b d", b=GB), row4(bv), ALU.add)\
                    .then_inc(v_ready.sem, 1)

            def banding(it, g, k):
                dve.wait_ge(scores_psum.sem, scores_psum.at(g, 1))
                dve.wait_ge(mix_psum.sem, mix_psum.at(g, 0))
                dve.tensor_tensor(st[:], bank(it, "scores", 0)[:].rearrange("p (b s) -> p b s", b=GB),
                                  band[:].unsqueeze(1).broadcast_to([128, GB, S]), ALU.mult).then_inc(banded.sem, 1)

            def stats(src, which, chn, g, n, var, vn):
                for b in range(GB):
                    ins = dve.bn_stats(bs[:, which, b], src[:, b])
                ins.then_inc(chn.sem, 1)
                dve.wait_ge(chn.sem, chn.at(g, n))
                dve.memset(idle[:], 0.0)
                for b in range(GB):
                    ins = dve.bn_aggr(mv[:, which, b], bs[:, which, b])
                ins.then_inc(var.sem, 1)

            def norm(dst, src, which, signal):
                for b in range(GB):
                    ins = dve.tensor_scalar(dst[:, b], src[:, b], mv[:, which, b, 0:1], rstd[:, which, b:b + 1],
                                            ALU.subtract, ALU.mult)
                ins.then_inc(signal, 1)

            def ln_x(it, g, k):
                src = bank(it, "mix", 0)[:].rearrange("p (b d) -> p b d", b=GB)
                ox = own["x"]
                dve.wait_ge(mix_psum.sem, mix_psum.at(g, 1))
                stats(src, 0, ox, g, 1, ln_var["x"], 1)
                dve.wait_ge(ln_rstd["x"].sem, ln_rstd["x"].at(g, 1))
                dve.wait_ge(ln_var["x"].sem, ln_var["x"].at(g, 1))
                dve.wait_ge(xn_psum.sem, xn_psum.at(g, 0))
                norm(n1, src, 0, mixed.sem)
                dve.wait_ge(mixed.sem, mixed.at(g, 1))
                dve.tensor_tensor(n1[:], n1[:], row4(lnw), ALU.mult).then_inc(ox.sem, 1)
                dve.wait_ge(ox.sem, ox.at(g, 2))
                dve.wait_ge(xb_ready.sem, xb_ready.at(g, 1))
                dve.wait_ge(x1_in_b.sem, x1_in_b.at(g - 1, 1))
                dve.tensor_tensor(x1[:, 0], n1[:], xs[:], ALU.add).then_inc(ox.sem, 1)
                dve.wait_ge(ox.sem, ox.at(g, 3))
                stats(x1[:, 0], 1, ox, g, 4, ln_var["x"], 2)
                dve.wait_ge(ln_rstd["x"].sem, ln_rstd["x"].at(g, 2))
                dve.wait_ge(ln_var["x"].sem, ln_var["x"].at(g, 2))
                norm(n1, x1[:, 0], 1, n2_ready.sem)

            def move_to_c(it, g, k):
                dve.wait_ge(x1_in_b.sem, x1_in_b.at(g, 1))
                dve.wait_ge(out_ready.sem, out_ready.at(g - 1, 1))
                dve.tensor_copy(x1[:, 2], x1[:, 1]).then_inc(x1_in_c.sem, 1)

            def move_to_b(it, g, k):
                dve.wait_ge(own_x.sem, own_x.at(g, 3))
                dve.wait_ge(x1_in_c.sem, x1_in_c.at(g - 1, 1))
                dve.tensor_copy(x1[:, 1], x1[:, 0]).then_inc(x1_in_b.sem, 1)

            def keys(it, g, k):
                ok = own["k"]
                dve.wait_ge(kv_psum.sem, kv_psum.at(g, 1))
                dve.tensor_copy(kv[:].rearrange("p b d -> p (b d)"), bank(it, "kv", 0)[:]).then_inc(kv_copied.sem, 1)
                dve.wait_ge(kv_copied.sem, kv_copied.at(g, 1))
                dve.tensor_tensor(ksq[:], kv[:, :, 0:DH], kv[:, :, 0:DH], ALU.mult).then_inc(ok.sem, 1)
                dve.wait_ge(pv_psum.sem, pv_psum.at(g, 0))
                dve.tensor_tensor(vd[:], kv[:, :, DH:2 * DH], nval_r.unsqueeze(1).broadcast_to([128, GB, DH]),
                                  ALU.subtract).then_inc(v_shifted.sem, 1)
                dve.wait_ge(ok.sem, ok.at(g, 1))
                dve.tensor_reduce(ss[:], ksq[:], AX, ALU.add).then_inc(ok.sem, 1)
                dve.wait_ge(ok.sem, ok.at(g, 2))
                dve.tensor_scalar(ss[:], ss[:], 1e-24, None, ALU.max).then_inc(k_squares.sem, 1)

            def q_copy(it, g, c):
                dve.wait_ge(q_squared.sem, q_squared.at(g, c + 1))
                dve.wait_ge(sim_psum.sem, sim_psum.at(g, 0))
                dve.tensor_scalar(qs[:, c], bank(it, "q", c)[:], qsc, None, ALU.mult).then_inc(q_copied.sem, 1)

            def mask_scores(it, g, k):
                if k == 0:
                    dve.wait_ge(mask_loaded.sem, mask_loaded.at(g, 16))
                    dve.wait_ge(bias_ready.sem, bias_ready.at(g, 0))
                    dve.tensor_scalar(maskn[:], mask[:], -1.0, BIG, ALU.add, ALU.mult).then_inc(mask_row.sem, 1)

            def keys_normed(it, g, k):
                dve.wait_ge(k_rnorm.sem, k_rnorm.at(g, 1))
                dve.wait_ge(kT_psum.sem, kT_psum.at(g, 0))
                for n in range(2):
                    ins = dve.tensor_tensor(kd[:, :, n], kv[:, :, 0:DH], rk[:].unsqueeze(2).broadcast_to([128, GB, DH]),
                                            ALU.mult)
                ins.then_inc(k_normed.sem, 1)

            def q_sums(it, g, k):
                dve.wait_ge(ssq_psum.sem, ssq_psum.at(g, NP))
                dve.wait_ge(biased.sem, biased.at(g, 0))
                dve.tensor_scalar(qss[:], bank(it, "q", 0, 1)[:, 0:GB * HEADS], 1.0 / SCALE ** 2, 1e-24 / SCALE ** 2,
                                  ALU.mult, ALU.max).then_inc(ssq_copied.sem, 1)

            def score(it, g, k):
                dve.wait_ge(q_rnorm.sem, q_rnorm.at(g, k + 1))
                dve.wait_ge(bias_ready.sem, bias_ready.at(g, k + 1))
                dve.wait_ge(pt_psum.sem, pt_psum.at(g, 4 * (k - 1)) if k >= 1 else pt_psum.at(g - 1, 4 * (GB - 1)))
                for p in range(NP):
                    dve.wait_ge(sim_psum.sem, sim_psum.at(g, k * NP + p + 1))
                    for n in range(2):
                        h = 2 * p + n
                        ins = dve.scalar_tensor_tensor(sm[:, k % 2, h], bank(it, "sim", k, p)[:, n * NK:(n + 1) * NK],
                                                       rq[:, k * HEADS + h:k * HEADS + h + 1], biasm[:, k % 2, h],
                                                       ALU.mult, ALU.add)
                    ins.then_inc(biased.sem, 1)
                dve.wait_ge(biased.sem, biased.at(g, (k + 1) * NP))
                dve.tensor_reduce(nmx[:, k % 2], sm[:, k % 2], AX, ALU.max, negate=True).then_inc(max_ready.sem, 1)

            def pt_copy(it, g, k):
                dve.wait_ge(exps.sem, exps.at(g, 4 * (k + 1)))
                dve.wait_ge(normed.sem, normed.at(g, 2 * k))
                dve.reciprocal(rden[:], den[:, k % 2]).then_inc(rden_ready.sem, 1)
                for n in (1, 3):
                    dve.wait_ge(pt_psum.sem, pt_psum.at(g, 4 * k + n + 1))
                    dve.wait_ge(pv_psum.sem, pv_psum.at(g, 2 * k))
                    dve.tensor_copy(pT[:, 4 * n:4 * n + 4].rearrange("p h s -> p (h s)"), bank(it, "PT", k, n)[:])\
                        .then_inc(pt_dve.sem, 1)

            def pv_norm(it, g, k):
                dve.wait_ge(rden_ready.sem, rden_ready.at(g, k + 1))
                dve.wait_ge(ot_psum.sem, ot_psum.at(g, 2 * k))
                for n in range(2):
                    dve.wait_ge(pv_psum.sem, pv_psum.at(g, 2 * k + n + 1))
                    dve.tensor_tensor(on[:, 8 * n:8 * n + 8], bank(it, "PV", k, n)[:].rearrange("p (h d) -> p h d", h=8),
                                      rden[:, 8 * n:8 * n + 8].unsqueeze(2).broadcast_to([128, 8, DH]), ALU.mult)\
                        .then_inc(normed.sem, 1)

            def ln_z(it, g, k):
                src = zbank[:].rearrange("p (b d) -> p b d", b=GB)
                dve.wait_ge(z_psum.sem, z_psum.at(g, GB))
                stats(src, 2, own["z"], g, 1, ln_var["z"], 1)
                dve.wait_ge(ln_rstd["z"].sem, ln_rstd["z"].at(g, 1))
                dve.wait_ge(ln_var["z"].sem, ln_var["z"].at(g, 1))
                dve.wait_ge(zT_psum.sem, zT_psum.at(g, 0))
                norm(n3, src, 2, n3_ready.sem)

            def gated(it, g, o):
                dve.wait_ge(silued.sem, silued.at(g, o + 1))
                dve.wait_ge(l1_psum.sem, l1_psum.at(g, 2 * o + 2))
                dve.wait_ge(l4_psum.sem, l4_psum.at(g, 0))
                dve.scalar_tensor_tensor(hA[:, o], bank(it, "l1", o, 1)[:], w2s[:, o:o + 1], al[:, o % 2],
                                         ALU.mult, ALU.mult).then_inc(l1_ready.sem, 1)

            def result(it, g, k):
                dve.wait_ge(l4_psum.sem, l4_psum.at(g, 1))
                dve.wait_ge(stored, g * 16)
                dve.tensor_tensor(res[:], bank(it, "l4", 0)[:].rearrange("p (b d) -> p b d", b=GB), row4(w3s), ALU.mult)\
                    .then_inc(scaled.sem, 1)
                dve.wait_ge(scaled.sem, scaled.at(g, 1))
                dve.wait_ge(x1_in_c.sem, x1_in_c.at(g, 1))
                dve.tensor_tensor(res[:], res[:], x1[:, 2], ALU.add).then_inc(out_ready.sem, 1)

            iterations(dve, {"bias+": mask_scores, "move1": move_to_c, "move2": move_to_b, "rw": rw_take, "exp": expert, "qkv": values, "scores": banding, "mix": ln_x, "kv": keys, "ssq": q_sums, "kT": keys_normed, "q": q_copy,
                             "sim": score, "PT": pt_copy, "PV": pv_norm, "zT": ln_z, "l1": gated, "l4": result})

        @block.tensor
        def _(pe):
            pe.wait_ge(const, 3)
            pe.wait_ge(load["pw1"], 16)
            pe.wait_ge(load["pw2"], 16)
            for n in range(2):
                pe.wait_ge(pa, 1 + 2 * n)
                pe.transpose(banks["S", 0][:, 0:128], ph[1], ident[:]).then_inc(pp, 1)
                pe.wait_ge(pa, 2 + 2 * n)
                if n == 0:
                    pe.matmul(banks["S", 1][:, 0:128], ph[2], pw1[:], start=True, stop=True).then_inc(pp, 1)
                else:
                    pe.matmul(banks["S", 1][0:HEADS, 0:S], pw2[:], ph[2], start=True, stop=True).then_inc(pp, 1)
            pe.wait_ge(pd, 4)
            pe.wait_ge(load["wt"], 16)
            pe.wait_ge(load["xT"], 16)
            pe.matmul(banks["M", 0][:, 0:B * E], ones[:], cg, start=True, stop=True)
            for b in range(B):
                ins = pe.matmul(banks["M", 0][:, b * E:(b + 1) * E], xT[:, b * S:(b + 1) * S], wt[:],
                                start=False, stop=True, skip_group_check=True)
            ins.then_inc(pp, 1)
            pe.wait_ge(pd, ROUTED[0])
            pe.wait_ge(s_toepl, 16)
            for n in range(4):
                pe.matmul(banks["ST"[n // 2], n % 2][:], flip, pT[:, 4 * n:4 * n + 4].rearrange("p h s -> p (h s)"),
                          start=True, stop=True).then_inc(pp, 1)
            pe.wait_ge(pa, 10)

            def free(it, step, k, n=0):
                pe.wait_ge(*drained_before(it, step, k, n))
                return bank(it, step, k, n)

            waited = set()

            def weights(*names):
                for n in names:
                    if n not in waited:
                        waited.add(n)
                        pe.wait_ge(load[n], 16)

            def expert(it, g, c):
                weights("wg", "wu")
                if c == 0:
                    pe.wait_ge(x_loaded.sem, x_loaded.at(g, 16))
                    pe.wait_ge(rw_turned.sem, rw_turned.at(g, 1))
                x = xg[:]
                cut = slice(c * 128, (c + 1) * 128)
                pe.matmul(free(it, "exp", c, 0)[:], wg[:, cut], x, start=True, stop=True).then_inc(expert_psum.sem, 1)
                pe.matmul(free(it, "exp", c, 1)[:], wu[:, cut], x, start=True, stop=True).then_inc(expert_psum.sem, 1)
                if c < NC_:
                    pe.matmul(free(it, "exp", c, 2)[:], sel[:, c], wT[:], start=True, stop=True)\
                        .then_inc(expert_psum.sem, 1)

            def rw_turn(it, g, k):
                pe.wait_ge(rw_taken.sem, rw_taken.at(g, 1))
                ps = free(it, "rw", 0)
                for b in range(GB):
                    ins = pe.transpose(ps[0:E, b * S:(b + 1) * S], rg[:, b * E:(b + 1) * E], ident[:])
                ins.then_inc(rw_psum.sem, 1)

            def down(it, g, k):
                weights("wd")
                ps = free(it, "down", 0)
                for c in range(NX):
                    pe.wait_ge(hidden.sem, hidden.at(g, c + 1))
                    ins = pe.matmul(ps[:], wd[:, c], hT[:, c], start=(c == 0), stop=(c == NX - 1))
                ins.then_inc(y_psum.sem, 1)

            def qkv(it, g, k):
                weights("wqkv")
                pe.wait_ge(y_copied.sem, y_copied.at(g, 1))
                for n in range(2):
                    pe.matmul(free(it, "qkv", 0, n)[:], wqkv[:, n * D:(n + 1) * D], yT[:], start=True, stop=True)\
                        .then_inc(qkv_psum.sem, 1)
                ps = free(it, "qkv", 0, 2)
                for b in range(GB):
                    ins = pe.matmul(ps[:, b * D:(b + 1) * D], yT[:, b * S:(b + 1) * S], wqkv[:, 2 * D:3 * D],
                                    start=True, stop=True)
                ins.then_inc(qkv_psum.sem, 1)

            def scores(it, g, k):
                pe.wait_ge(qk_copied.sem, qk_copied.at(g, 2))
                ps = free(it, "scores", 0)
                for b in range(GB):
                    cut = slice(b * S, (b + 1) * S)
                    ins = pe.matmul(ps[:, cut], kT[:, cut], qT[:, cut], start=True, stop=True)
                ins.then_inc(scores_psum.sem, 1)

            def mix(it, g, k):
                pe.wait_ge(v_ready.sem, v_ready.at(g, 1))
                pe.wait_ge(banded.sem, banded.at(g, 1))
                ps = free(it, "mix", 0)
                for b in range(GB):
                    ins = pe.matmul(ps[:, b * D:(b + 1) * D], st[:, b], v1[:, b], start=True, stop=True)
                ins.then_inc(mix_psum.sem, 1)

            def turn(it, step, src, ready, g, signal):
                pe.wait_ge(ready.sem, ready.at(g, 1))
                ps = free(it, step, 0)
                for b in range(GB):
                    ins = pe.transpose(ps[:, b * S:(b + 1) * S], src(b), ident[:])
                ins.then_inc(signal.sem, 1)

            def xn_turn(it, g, k):
                turn(it, "xnT", lambda b: n1[:, b], n2_ready, g, xn_psum)

            def kv_proj(it, g, k):
                weights("wkv2")
                pe.wait_ge(xn_copied.sem, xn_copied.at(g, 1))
                ps = free(it, "kv", 0)
                for b in range(GB):
                    ins = pe.matmul(ps[:, b * 128:(b + 1) * 128], xnT[:, b * S:(b + 1) * S], wkv2[:], start=True, stop=True)
                ins.then_inc(kv_psum.sem, 1)

            def q_proj(it, g, c):
                weights("wq2")
                pe.matmul(free(it, "q", c)[:], wq2[:, c * 128:(c + 1) * 128], xnT[:], start=True, stop=True)\
                    .then_inc(q_psum.sem, 1)
                if c >= 1:
                    q_sum(it, g, c - 1)

            def q_sum(it, g, c):
                ps = free(it, "q", 0, 1) if c == 0 else bank(it, "q", 0, 1)
                pe.wait_ge(q_squared.sem, q_squared.at(g, c + 1))
                for b in range(GB):
                    ins = pe.matmul(ps[:, b * HEADS + 2 * c:b * HEADS + 2 * c + 2], sq[:, c % 2, b * S:(b + 1) * S],
                                    halves[:], start=True, stop=True)
                ins.then_inc(ssq_psum.sem, 1)

            def q_sums(it, g, k):
                q_sum(it, g, NP - 1)

            def k_turn(it, g, k):
                turn(it, "kT", lambda b: kd[:, b].rearrange("p n d -> p (n d)"), k_normed, g, kT_psum)

            def sim(it, g, k):
                pe.wait_ge(kT_copied.sem, kT_copied.at(g, 1))
                pe.wait_ge(q_copied.sem, q_copied.at(g, NP))
                for p in range(NP):
                    pe.matmul(free(it, "sim", k, p)[:, 0:2 * NK], qs[:, p, k * S:(k + 1) * S],
                              kbd[:, k].rearrange("p n s -> p (n s)"), start=True, stop=True).then_inc(sim_psum.sem, 1)

            def p_turn(it, g, k):
                for n in range(4):
                    pe.wait_ge(exps.sem, exps.at(g, 4 * k + n + 1))
                    ps = free(it, "PT", k, n)
                    for j in range(4):
                        ins = pe.transpose(ps[:, j * S:(j + 1) * S], sm[:, k % 2, 4 * n + j, 1:NK], ident[:])
                    ins.then_inc(pt_psum.sem, 1)

            def pv(it, g, k):
                pe.wait_ge(v_shifted.sem, v_shifted.at(g, 1))
                pe.wait_ge(pt_act.sem, pt_act.at(g, 2 * k + 2))
                pe.wait_ge(pt_dve.sem, pt_dve.at(g, 2 * k + 2))
                for n in range(2):
                    ps = bank(it, "PV", k, n)
                    for j in range(8):
                        ins = pe.matmul(ps[:, j * DH:(j + 1) * DH], pT[:, 8 * n + j], vd[:, k], start=True, stop=True)
                    ins.then_inc(pv_psum.sem, 1)

            def o_turn(it, g, k):
                for n in range(2):
                    pe.wait_ge(normed.sem, normed.at(g, 2 * k + n + 1))
                    ps = free(it, "OT", k, n)
                    for j in range(4):
                        h = 8 * n + 2 * j
                        ins = pe.transpose(ps[:, j * S:(j + 1) * S], on[:, h:h + 2].rearrange("p h d -> p (h d)"), ident[:])
                    ins.then_inc(ot_psum.sem, 1)

            def z_proj(it, g, k):
                weights("wout")
                if k == 0:
                    pe.wait_ge(n3_ready.sem, n3_ready.at(g, 0))
                for c in range(NP):
                    pe.wait_ge(ot_copied.sem, ot_copied.at(g, 2 * k + c // 4 + 1))
                    ins = pe.matmul(zbank[:, k * D:(k + 1) * D], oT[:, c], wout[:, c], start=(c == 0), stop=(c == NP - 1))
                ins.then_inc(z_psum.sem, 1)

            def z_turn(it, g, k):
                turn(it, "zT", lambda b: n3[:, b], n3_ready, g, zT_psum)

            def layer1(it, g, o):
                weights("w1", "w2")
                pe.wait_ge(zT_copied.sem, zT_copied.at(g, 1))
                for n, w in enumerate((w1, w2)):
                    pe.matmul(free(it, "l1", o, n)[:], w[:, o * 128:(o + 1) * 128], zT[:], start=True, stop=True)\
                        .then_inc(l1_psum.sem, 1)

            def layer(step, w, src, ready, signal):
                def part(it, g, o):
                    weights("h1", "h2")
                    ps = free(it, step, o)
                    for c in range(NO):
                        pe.wait_ge(ready.sem, ready.at(g, c + 1))
                        ins = pe.matmul(ps[:], w[:, c, o * 128:(o + 1) * 128], src[:, c], start=(c == 0), stop=(c == NO - 1))
                    ins.then_inc(signal.sem, 1)
                return part

            def layer4(it, g, k):
                weights("w3")
                pe.wait_ge(l3_ready.sem, l3_ready.at(g, NO))
                ps = free(it, "l4", 0)
                for b in range(GB):
                    for c in range(NO):
                        ins = pe.matmul(ps[:, b * D:(b + 1) * D], hA[:, c, b * S:(b + 1) * S], w3[:, c],
                                        start=(c == 0), stop=(c == NO - 1))
                ins.then_inc(l4_psum.sem, 1)

            iterations(pe, {"rw": rw_turn, "exp": expert, "down": down, "qkv": qkv, "scores": scores, "mix": mix, "xnT": xn_turn,
                            "kv": kv_proj, "q": q_proj, "ssq": q_sums, "kT": k_turn, "sim": sim, "PT": p_turn, "PV": pv,
                            "OT": o_turn, "z": z_proj, "zT": z_turn, "l1": layer1,
                            "l2": layer("l2", h1, hA, l1_ready, l2_psum), "l3": layer("l3", h2, hB, l2_ready, l3_psum),
                            "l4": layer4})


ROUTED = []


def kernel(**inputs):
    import numpy as np
    import concourse.bacc as bacc
    from concourse.bass_utils import run_bass_kernel_spmd

    x, cond = np.asarray(inputs["x"]), np.asarray(inputs["cond_64"])
    i = {k: np.asarray(v) for k, v in inputs.items()}
    L = {k[3:]: v for k, v in i.items() if k.startswith("L0_")}

    def tiles(w):
        return w.reshape(-1, 128, w.shape[1]).transpose(1, 0, 2)

    def col(v):
        return v.reshape(-1, 128).T

    twice = lambda v: np.concatenate([v, v])
    wexp = lambda w, s: np.concatenate([w.transpose(1, 0, 2).reshape(D, E * EM), s], axis=1)
    arrays = {
        "x": x,
        "xT": x.reshape(B * S, D).T,
        "mask": i["mask_BxS_bf1"].reshape(B * S),
        "cols": np.concatenate(
            [col(L["ffn_w1_s"]), col(L["ffn_w2_s"]), col(L["ffn_h1_s"]), col(L["ffn_h2_s"]),
             col(L["attn_b_qkv"][0:D]), col(L["attn_b_qkv"][D:2 * D]), col(L["cond2_g_norm"]), col(L["cond2_g_out"]),
             col(twice(L["cond2_q_scale"])), col(twice(L["cond2_k_scale"])), col(twice(cond[0])), col(twice(cond[1]))],
            axis=1),
        "rows": np.concatenate(
            [L["attn_ln_w"], L["attn_ln_b"], L["attn_b_qkv"][2 * D:], L["ffn_w3_s"], L["cond2_w0"][0], L["cond2_b0"],
             L["cond2_g0"], L["cond2_b1"], L["cond2_g1"], cond[0], cond[1], L["cond2_null_attn_bias"]])[None],
        "wt": L["cond_wt"].T, "wgT": L["cond_wg"].T, "condT": cond.T,
        "pw1": L["cond2_w1"], "pw2": L["cond2_w2"], "pb2": L["cond2_b2"][:, None],
        "wg": wexp(L["cond_w_gate"], L["cond_sw_gate"]), "wu": wexp(L["cond_w_up"], L["cond_sw_up"]),
        "wd": tiles(np.concatenate([L["cond_w_down"].reshape(E * EM, D), L["cond_sw_down"]])),
        "wqkv": L["attn_W_qkv"], "wq2": L["cond2_Wq"], "wkv2": L["cond2_Wkv"], "wout": tiles(L["cond2_Wout"]),
        "w1": L["ffn_w1_w"].T, "w2": L["ffn_w2_w"].T, "h1": tiles(L["ffn_h1_w"].T), "h2": tiles(L["ffn_h2_w"].T),
        "w3": tiles(L["ffn_w3_w"].T),
    }
    arrays = {n: np.ascontiguousarray(v) for n, v in arrays.items()}
    nc = bacc.Bacc("TRN2", target_bir_lowering=False, num_devices=1)
    aps = {n: nc.dram_tensor("in_" + n, v.shape, mybir.dt.from_np(v.dtype), kind="ExternalInput").ap()
           for n, v in arrays.items()}
    out = nc.dram_tensor("out_y", (B, S, D), mybir.dt.float32, kind="ExternalOutput").ap()
    ROUTED.clear()
    layer_kernel(nc, aps, out)
    r = run_bass_kernel_spmd(nc, [{"in_" + n: v for n, v in arrays.items()}], core_ids=[0])
    return r.results[0]["out_y"]
```

```python
import concourse.bass as bass
from concourse import mybir
from contextlib import ExitStack

B, S, D = 32, 128, 128
GB = 4
NG = B // GB
GT = GB * S
E, EM = 8, 64
NC_ = E * EM // 128
NX = NC_ + 1
HEADS, DH = 16, 64
NP = HEADS // 2
NK = S + 1
HID = 512
NO = HID // 128
SPAN = 32
LN_EPS = 1e-5
BIG = 1e30
SCALE = 8.0

ORDER = {
    "pe": """
        rw.0 sim.0 exp.0 sim.1 exp.1 sim.2 exp.2 sim.3 exp.3 sim.4-5 exp.4 down.0 PT.0 sim.6 PT.1 zT.0 sim.7
        PT.2 l1.0 PT.3 sim.8 l1.1 PV.0 qkv.0 sim.9 OT.0 scores.0 PV.1 sim.10 PT.4 l1.2 PT.5 sim.11 OT.1 PT.6
        l1.3 l2.0 sim.12 PT.7 mix.0 PV.2-3 l2.1 z.0 OT.2 z.1 l2.2 OT.3 sim.13 l2.3 PT.8 z.2 PT.9-10 l3.0 sim.14
        PT.11 xnT.0 sim.15 PV.4 z.3 l3.1-3 PV.5 OT.4 l4.0 q.0-1 PT.12 q.2 OT.5 q.3 qs.0-1 z.4 PT.13-14 z.5 PT.15
        kv.0 PV.6-7 qs.2-3 q.4-5 qs.4 OT.6 q.6 qs.5 q.7 kT.0 qs.6-7 OT.7 z.6-7
    """,
    "act": """
        rw.0 exp.0-3 ex.0-1 exp.4 ex.2 down.0 PT.0 zT.0 PT.1 ex.3 PT.2 l1.0-1 ex.4 qkv.0 ex.5 OT.0 ex.6-7 PT.3-4
        l1.2 OT.1 PT.5 l1.3 PT.6 ex.8 l2.0 ex.9 l2.1 ex.10 OT.2 PT.7 l2.2 OT.3 PT.8 l2.3 PT.9 ex.11 PT.10 l3.0-1
        PT.11 xnT.0 ex.12 l3.2-3 ex.13 OT.4 q.0-1 ex.14 PT.12 q.2 PT.13 OT.5 q.3 ex.15 PT.14 q.4-5 OT.6 q.6-7
        kT.0 PT.15 OT.7
    """,
    "dve": """
        rw.0 ln3.0 sim.0 exp.0 sim.1 exp.1 sim.2 exp.2 sim.3 max.0 PT.0 sim.4 exp.3 sim.5 exp.4 zT.0 sim.6 PT.1
        sim.7 max.1 rden.0 PT.2 sim.8 move1.0 PT.3 l1.0-1 move2.0 PV.0 maskn.0 qkv.0 scores.0 PT.4 sim.9 PV.1
        sim.10 PT.5 sim.11 l1.2 rden.1 max.2 PT.6 l1.3 PT.7 mix.0 PV.2 sim.12 PT.8 PV.3 ln1.0 sim.13 PT.9 ln2.0
        sim.14 PT.10-11 sim.15 PT.12 rden.2 max.3 PV.4-5 l4.0 q.0-1 PT.13-15 q.2 rden.3 PV.6 q.3 kv.0 q.4-5 kT.0
        PV.7 q.6-7 ssq.0
    """,
    "pool": """
        zT.0 bias.2-3 xb.0 bias+.0 ln1.0 ln2.0 bias+.1 kv.0 qn.0-3
    """,
    "sp": """
        rw.0 maskn.0 l4.0
    """,
}


def parsed(text):
    items = []
    for item in text.split():
        step, ks = item.split(".")
        first, *last = ks.split("-")
        items += [(step, k) for k in range(int(first), int(last[0] if last else first) + 1)]
    return items


ORDER = {engine: parsed(text) for engine, text in ORDER.items()}
STAGE = {s: "A" for s in ("rw", "exp", "down", "qkv", "scores", "mix", "xnT", "kv", "q", "qs", "ssq", "qn", "kT", "bias+", "maskn", "xb", "ln1", "ln2")}
STAGE |= {s: "B" for s in ("bias", "sim", "max", "ex", "rden", "PT", "PV", "OT", "z", "move2")}
STAGE |= {s: "C" for s in ("ln3", "zT", "l1", "l2", "l3", "l4", "move1")}
LOOP = 2
SHIFT = {"A": 1, "B": 0, "C": -1}

USES = {"rw": "M", "exp": "MMM", "down": "M", "qkv": "MMM", "scores": "M", "mix": "M", "xnT": "M",
        "kv": "M", "q": "M", "ssq": "", "kT": "M", "sim": "SS", "PT": "T", "PV": "T", "OT": "T", "zT": "M",
        "l1": "MM", "l2": "M", "l3": "M", "l4": "M"}
BANKS = {"M": 3, "S": 2, "T": 2}


def uses(step, k):
    if step == "qs":
        return "S" if k == 0 else ""
    return "MM" if (step, k) == ("exp", NX - 1) else USES.get(step, "")


def stages_of(it):
    return [s for s in "ABC" if 0 <= it + SHIFT[s] < NG]


def bank_plan():
    last, plan = {}, {}
    for it in range(-1, NG + 1):
        active, turn, here = stages_of(it), {r: 0 for r in BANKS}, {}
        for step, k in ORDER["pe"]:
            for n, ring in enumerate(uses(step, k)):
                bank = (ring, turn[ring] % BANKS[ring])
                turn[ring] += 1
                if STAGE[step] not in active:
                    continue
                here[step, k, n] = (bank, last.get(bank), it)
                last[bank] = (step, k, n, it)
        plan[it] = {u: (bank, before and (*before[:3], it - before[3])) for u, (bank, before, _) in here.items()}
    for it in range(LOOP, NG - 1):
        assert plan[it] == plan[LOOP], "the loop's iterations differ"
    return plan


PLAN = bank_plan()


def layer_kernel(nc, a, out):
    fp32, u8 = mybir.dt.float32, mybir.dt.uint8
    ALU, ACT, AX = mybir.AluOpType, mybir.ActivationFunctionType, mybir.AxisListType.X
    ctx = ExitStack()
    with ctx:
        def sb(name, shape, dt=fp32):
            return ctx.enter_context(nc.sbuf_tensor("sb_" + name, shape, dt))

        def sem(name):
            return ctx.enter_context(nc.semaphore("s_" + name))

        class Signal:

            def __init__(self, name, per_group):
                self.sem, self.per = sem(name), per_group

            def at(self, g, n):
                v = g * self.per + n
                return max(v, 0) if isinstance(v, int) else v

        xg = sb("xg", [128, GT])
        xs = sb("xs", [128, GB, D])
        x1 = sb("x1", [128, 3, GB, D])
        wg, wu = sb("wg", [128, NX * 128]), sb("wu", [128, NX * 128])
        wd = sb("wd", [128, NX, D])
        wqkv = sb("wqkv", [128, 3 * D])
        wq2, wkv2, wout = sb("wq2", [128, HEADS * DH]), sb("wkv2", [128, 2 * DH]), sb("wout", [128, NP, D])
        w1, w2 = sb("w1", [128, HID]), sb("w2", [128, HID])
        h1, h2, w3 = sb("h1", [128, NO, HID]), sb("h2", [128, NO, HID]), sb("w3", [128, NO, D])
        wt, wgT, condT = sb("wt", [128, E]), sb("wgT", [64, E]), sb("condT", [64, B])
        pw1, pw2, pb2 = sb("pw1", [128, 128]), sb("pw2", [128, HEADS]), sb("pb2", [HEADS, 1])
        NCOL = 4 * NO + 8
        cols = sb("cols", [128, NCOL])
        w1s, w2s, h1s, h2s = (cols[:, NO * i:NO * i + NO] for i in range(4))
        bq, bk, gnorm, gout, qsc, ksc, nkey, nval = (cols[:, 4 * NO + i:4 * NO + i + 1] for i in range(8))
        NROW = 9 * 128 + 2 * DH + HEADS
        rows = sb("rows", [128, NROW])
        lnw, lnb, bv, w3s, pw0, pb0, pg0, pb1, pg1 = (rows[:, 128 * i:128 * i + 128] for i in range(9))
        nkey_r, nval_r = rows[:, 1152:1152 + DH], rows[:, 1152 + DH:1152 + 2 * DH]
        nbias = rows[:, 1152 + 2 * DH:NROW]
        mask = sb("mask", [128, GB, S], u8)
        ident = sb("ident", [128, 128])
        band = sb("band", [128, 128])
        halves = sb("halves", [128, 2])
        ones = sb("ones", [64, 128])
        sel = sb("sel", [E, NC_, 128])
        eps = sb("eps", [128, GB])
        mhalf = sb("mhalf", [128, 16])
        route = sb("route", [128, B * E])[:]
        rg = sb("rg", [128, GB * E])
        wT = sb("wT", [E, GT])
        bias0 = sb("bias0", [128, HEADS, S])
        biasm = sb("biasm", [128, 2, HEADS, NK])
        maskn = sb("maskn", [128, GB, S])
        gs = sb("gs", [128, 2, GT])
        hT = sb("hT", [128, NX, GT])
        yT, qT, kT = sb("yT", [128, GT]), sb("qT", [128, GT]), sb("kT", [128, GT])
        v1, st = sb("v1", [128, GB, D]), sb("st", [128, GB, S])
        n1, xnT = sb("n1", [128, GB, D]), sb("xnT", [128, GT])
        bs = sb("bs", [128, 3, GB, 6])
        mv = sb("mv", [128, 3, GB, 2])
        ve = sb("ve", [128, 3, GB])
        idle = sb("idle", [128, 1])
        rstd = sb("rstd", [128, 3, GB])
        sq, qs = sb("sq", [128, 2, GT]), sb("qs", [128, NP, GT])
        kv, ksq = sb("kv", [128, GB, 2 * DH]), sb("ksq", [128, GB, DH])
        vd, kd = sb("vd", [128, GB, DH]), sb("kd", [128, GB, 2, DH])
        ss, rk = sb("ss", [128, GB]), sb("rk", [128, GB])
        qss, rq = sb("qss", [128, GB * HEADS]), sb("rq", [128, GB * HEADS])
        kbd = sb("kbd", [128, GB, 2, NK])
        sm = sb("sm", [128, 2, HEADS, NK])
        nmx, den, rden = sb("nmx", [128, 2, HEADS]), sb("den", [128, 2, HEADS]), sb("rden", [128, HEADS])
        pT, on, oT = sb("pT", [128, HEADS, S]), sb("on", [128, HEADS, DH]), sb("oT", [128, NP, S])
        n3, zT = sb("n3", [128, GB, D]), sb("zT", [128, GT])
        al, hA, hB = sb("al", [128, 2, GT]), sb("hA", [128, NO, GT]), sb("hB", [128, NO, GT])
        res = sb("res", [128, GB, D])
        xT = qs[:].rearrange("p c t -> p (c t)")
        lgt, *rt = (hA[:, i // 2, i % 2 * 256:(i % 2 + 1) * 256] for i in range(8))
        ph = [hB[:, 0, 128 * i:128 * i + 128] for i in range(4)]
        nks = hB[:, 1, 0:DH]
        flip = hB[:, 1, 256:384]
        prev = hB[0:HEADS, 2, 0:2 * S]
        cg = hB[0:64, 3, 0:B * E]
        r1 = [hB[:, 1, 64 + B * i:64 + B * (i + 1)] for i in range(6)]
        prank = sb("prank", [128, E])
        pos = sb("pos", [128, 1])
        pi = sb("pi", [128, 1], mybir.dt.int32)
        pst = sb("pst", [128, 6])
        pmv = sb("pmv", [128, 2])
        prs = sb("prs", [128, 2])
        nkr = sb("nkr", [128, 3])

        banks = {(r, i): ctx.enter_context(nc.psum_tensor(f"ps_{r}{i}", [128, 512], fp32))
                 for r, n in BANKS.items() for i in range(n)}
        zbank = ctx.enter_context(nc.psum_tensor("ps_z", [128, 512], fp32))
        toeplitz = nc.dram_tensor("toeplitz", (HEADS, 2 * S), fp32, kind="Internal").ap()

        load = {n: sem("ld_" + n) for n in a if n not in ("x", "mask")}
        mask_loaded = Signal("mask_loaded", 16)
        s_toep, s_toepl = sem("toep_stored"), sem("bias_loaded")
        const = sem("const")
        pa, pd, pp, pg = sem("pro_act"), sem("pro_dve"), sem("pro_pe"), sem("pro_pool")
        x_loaded, xs_loaded = Signal("x_loaded", 16), Signal("xs_loaded", 16)
        xb_ready = Signal("xb_ready", 1)
        x1_in_b, x1_in_c = Signal("x1_in_b", 1), Signal("x1_in_c", 1)
        own_x = Signal("own_x", 4)
        rw_taken, rw_psum, rw_turned = Signal("rw_taken", 1), Signal("rw_psum", 1), Signal("rw_turned", 1)
        expert_psum = Signal("expert_psum", 3 * NX - 1)
        gate_copied = Signal("gate_copied", NX)
        leaked = Signal("leaked", NX)
        upped = Signal("upped", NC_)
        hidden = Signal("hidden", NX)
        y_psum, y_copied = Signal("y_psum", 1), Signal("y_copied", 1)
        qkv_psum, qk_copied, v_ready = Signal("qkv_psum", 3), Signal("qk_copied", 2), Signal("v_ready", 1)
        scores_psum, banded = Signal("scores_psum", 1), Signal("banded", 1)
        mix_psum = Signal("mix_psum", 1)
        mixed = Signal("mixed", 1)
        n2_ready, xn_psum, xn_copied = Signal("n2_ready", 1), Signal("xn_psum", 1), Signal("xn_copied", 1)
        ln_var = {s: Signal("var_" + s, n) for s, n in (("x", 2), ("z", 1))}
        ln_eps = {s: Signal("eps_" + s, n) for s, n in (("x", 2), ("z", 1))}
        ln_rstd = {s: Signal("rstd_" + s, n) for s, n in (("x", 2), ("z", 1))}
        kv_psum, kv_copied, v_shifted = Signal("kv_psum", 1), Signal("kv_copied", 1), Signal("v_shifted", 1)
        k_squares, k_rnorm, k_normed = Signal("k_squares", 1), Signal("k_rnorm", 1), Signal("k_normed", 1)
        kT_psum, kT_copied = Signal("kT_psum", 1), Signal("kT_copied", 1)
        q_psum, q_squared, q_copied = Signal("q_psum", NP), Signal("q_squared", NP), Signal("q_copied", NP)
        ssq_psum, ssq_copied, q_rnorm = Signal("ssq_psum", NP), Signal("ssq_copied", 1), Signal("q_rnorm", GB)
        mask_row, bias_ready = Signal("mask_row", 1), Signal("bias_ready", GB)
        sim_psum, biased = Signal("sim_psum", GB * NP), Signal("biased", GB * NP)
        max_ready, exps = Signal("max_ready", GB), Signal("exps", GB * 4)
        pt_psum = Signal("pt_psum", GB * 4)
        pt_act, pt_dve = Signal("pt_act", GB * 2), Signal("pt_dve", GB * 2)
        rden_ready = Signal("rden_ready", GB)
        pv_psum, normed = Signal("pv_psum", GB * 2), Signal("normed", GB * 2)
        ot_psum, ot_copied = Signal("ot_psum", GB * 2), Signal("ot_copied", GB * 2)
        z_psum, n3_ready = Signal("z_psum", GB), Signal("n3_ready", 1)
        zT_psum, zT_copied = Signal("zT_psum", 1), Signal("zT_copied", 1)
        l1_psum, silued, l1_ready = Signal("l1_psum", 2 * NO), Signal("silued", NO), Signal("l1_ready", NO)
        l2_psum, l2_ready = Signal("l2_psum", NO), Signal("l2_ready", NO)
        l3_psum, l3_ready = Signal("l3_psum", NO), Signal("l3_ready", NO)
        l4_psum, scaled, out_ready = Signal("l4_psum", 1), Signal("scaled", 1), Signal("out_ready", 1)
        stored = sem("stored")

        DRAINED = {}
        for c in range(NX):
            DRAINED |= {("exp", c, 0): (gate_copied, c + 1), ("exp", c, 2): (hidden, c + 1),
                        ("exp", c, 1): (upped, c + 1) if c < NC_ else (hidden, c + 1)}
        DRAINED |= {("rw", 0, 0): (rw_turned, 1), ("down", 0, 0): (y_copied, 1), ("qkv", 0, 0): (qk_copied, 1), ("qkv", 0, 1): (qk_copied, 2),
                    ("qkv", 0, 2): (v_ready, 1), ("scores", 0, 0): (banded, 1), ("mix", 0, 0): (mixed, 1),
                    ("xnT", 0, 0): (xn_copied, 1), ("kv", 0, 0): (kv_copied, 1), ("qs", 0, 0): (ssq_copied, 1),
                    ("kT", 0, 0): (kT_copied, 1), ("zT", 0, 0): (zT_copied, 1), ("l4", 0, 0): (scaled, 1)}
        DRAINED |= {("q", c, 0): (q_copied, c + 1) for c in range(NP)}
        DRAINED |= {("sim", p // 2, p % 2): (biased, p + 1) for p in range(GB * NP)}
        DRAINED |= {("PT", n, 0): ((pt_act, pt_dve)[n % 2], n // 2 + 1) for n in range(4 * GB)}
        DRAINED |= {("PV", n, 0): (normed, n + 1) for n in range(2 * GB)}
        DRAINED |= {("OT", n, 0): (ot_copied, n + 1) for n in range(2 * GB)}
        for o in range(NO):
            DRAINED |= {("l1", o, 0): (silued, o + 1), ("l1", o, 1): (l1_ready, o + 1),
                        ("l2", o, 0): (l2_ready, o + 1), ("l3", o, 0): (l3_ready, o + 1)}

        def kind(it):
            return it if isinstance(it, int) else LOOP

        def bank(it, step, k, n=0):
            return banks[PLAN[kind(it)][step, k, n][0]]

        def drained_before(it, step, k, n=0):
            before = PLAN[kind(it)][step, k, n][1]
            if before is None:
                return None
            signal, count = DRAINED[before[:3]]
            return signal, (SHIFT[STAGE[before[0]]] - before[3]) * signal.per + count

        def iterations(eng, order, steps):
            def body(it):
                for step, k in order:
                    if STAGE[step] in stages_of(kind(it)):
                        steps[step](it, it + SHIFT[STAGE[step]], k)
            for it in range(-1, LOOP):
                body(it)
            with eng.Fori(LOOP, NG - 1) as it:
                body(it)
            body(NG - 1)
            body(NG)

        block = ctx.enter_context(nc.Block())

        @block.sync
        def _(sp):
            def fetch(name, dst, src=None):
                sp.dma_start(dst, a[name] if src is None else src).then_inc(load[name], 16)

            fetch("cols", cols[:])
            fetch("rows", rows[:], bass.AP(tensor=a["rows"].tensor, offset=0, ap=[[0, 128], [1, NROW]]))
            fetch("wt", wt[:])
            fetch("wgT", wgT[:])
            fetch("condT", condT[:])
            fetch("pw1", pw1[:])
            fetch("pw2", pw2[:])
            fetch("pb2", pb2[:])
            fetch("xT", xT)
            fetch("wg", wg[:])
            fetch("wu", wu[:])
            fetch("wd", wd[:])
            fetch("wqkv", wqkv[:])
            sp.wait_ge(pa, 5)
            sp.dma_start(toeplitz, prev).then_inc(s_toep, 16)
            sp.wait_ge(s_toep, 16)
            sp.dma_start(pT[:], bass.AP(tensor=toeplitz.tensor, offset=0,
                                        ap=[[1, 128], [2 * S, HEADS], [1, S]])).then_inc(s_toepl, 16)
            fetch("wq2", wq2[:])
            fetch("wkv2", wkv2[:])
            fetch("wout", wout[:])
            fetch("w1", w1[:])
            fetch("w2", w2[:])
            fetch("h1", h1[:])
            fetch("h2", h2[:])
            fetch("w3", w3[:])

            def load_x(it, g, k):
                sp.wait_ge(expert_psum.sem, expert_psum.at(g, 0))
                sp.dma_start(xg[:], a["xT"][:, bass.ds(g * GT, GT)]).then_inc(x_loaded.sem, 16)
                sp.wait_ge(own_x.sem, own_x.at(g, 0))
                sp.dma_start(xs[:], a["x"][bass.ds(g * GB, GB), :, :].rearrange("b p f -> p b f"))\
                    .then_inc(xs_loaded.sem, 16)

            def load_mask(it, g, k):
                first = g * GT if isinstance(g, int) else sp.snap(g * GT)
                sp.wait_ge(mask_row.sem, mask_row.at(g, 0))
                sp.dma_start(mask[:].rearrange("p b s -> p (b s)"), a["mask"][bass.ds(first, GT)].unsqueeze(0).broadcast_to([128, GT]))\
                    .then_inc(mask_loaded.sem, 16)

            def store(it, g, k):
                sp.wait_ge(out_ready.sem, out_ready.at(g, 1))
                sp.dma_start(out[bass.ds(g * GB, GB), :, :].rearrange("b p f -> p b f"), res[:]).then_inc(stored, 16)

            iterations(sp, ORDER["sp"], {"rw": load_x, "maskn": load_mask, "l4": store})
            sp.wait_ge(stored, 16 * NG)

        @block.gpsimd
        def _(pool):
            pool.memset(ident[:], 0.0)
            pool.memset(band[:], 1.0 / 64.0)
            pool.memset(sel[:], 0.0)
            pool.memset(ones[:], 1.0)
            pool.memset(eps[:], LN_EPS)
            pool.memset(mhalf[:], -0.5)
            pool.memset(kbd[:], 0.0)
            pool.memset(prev, -BIG)
            pool.memset(flip, 0.0)
            pool.iota(pi[:], [[0, 1]], base=S - 1, channel_multiplier=-1).then_inc(const, 1)
            pool.wait_ge(const, 1)
            pool.affine_select(ident[:], ident[:], [[-1, 128]], ALU.not_equal, 1.0, base=0, channel_multiplier=1)
            pool.affine_select(flip, flip, [[1, 128]], ALU.not_equal, 1.0, base=1 - S, channel_multiplier=1)
            pool.affine_select(band[:], band[:], [[1, 128]], ALU.is_ge, 0.0, base=0, channel_multiplier=-1)
            pool.affine_select(sel[:].rearrange("e c (a m) -> e c a m", a=2), sel[:].rearrange("e c (a m) -> e c a m", a=2),
                               [[-2, NC_], [-1, 2], [0, EM]], ALU.not_equal, 1.0, base=0, channel_multiplier=1)
            for e in range(E):
                pool.memset(prank[:, e:e + 1], float(E - e))
            pool.tensor_copy(pos[:], pi[:]).then_inc(const, 1)
            pool.wait_ge(const, 2)
            pool.affine_select(band[:], band[:], [[-1, 128]], ALU.is_ge, 0.0, base=SPAN - 1, channel_multiplier=1)\
                .then_inc(const, 1)

            def power(out_, var, base, add, gate):
                pool.wait_ge(pd, gate)
                pool.tensor_scalar(prs[:, 0:1], var, add, 1.0, ALU.add, ALU.mult).then_inc(pg, 1)
                pool.wait_ge(pg, base)
                pool.tensor_tensor(out_, prs[:, 0:1], mhalf[:, 0:1], ALU.pow).then_inc(pg, 1)

            power(prs[:, 1:2], pmv[:, 1:2], 1, LN_EPS, 4)
            power(prs[:, 1:2], pmv[:, 1:2], 3, LN_EPS, 9)
            pool.wait_ge(pd, 15)
            pool.tensor_tensor(nkr[:, 2:3], nkr[:, 1:2], mhalf[:, 0:1], ALU.pow).then_inc(pg, 1)
            pool.wait_ge(load["rows"], 16)
            for b in range(2):
                last = pool.tensor_copy(biasm[:, b, :, 0], nbias)
            last.then_inc(pg, 1)
            pool.wait_ge(pa, 10)

            def rsqrt(which, ln, n):
                def part(it, g, k):
                    pool.wait_ge(ln_var[ln].sem, ln_var[ln].at(g, n))
                    pool.tensor_tensor(ve[:, which], mv[:, which, :, 1], eps[:], ALU.add)\
                        .then_inc(ln_eps[ln].sem, 1)
                    pool.wait_ge(ln_eps[ln].sem, ln_eps[ln].at(g, n))
                    pool.tensor_tensor(rstd[:, which], ve[:, which], mhalf[:, 0:GB], ALU.pow)\
                        .then_inc(ln_rstd[ln].sem, 1)
                return part

            ln1, ln2, ln3 = (rsqrt(w, s, n) for w, s, n in ((0, "x", 1), (1, "x", 2), (2, "z", 1)))

            def add_lnb(it, g, k):
                pool.wait_ge(xs_loaded.sem, xs_loaded.at(g, 16))
                pool.tensor_tensor(xs[:], xs[:], lnb.unsqueeze(1).broadcast_to([128, GB, D]), ALU.add)\
                    .then_inc(xb_ready.sem, 1)

            def k_norm(it, g, k):
                pool.wait_ge(k_squares.sem, k_squares.at(g, 1))
                pool.tensor_tensor(rk[:], ss[:], mhalf[:, 0:GB], ALU.pow).then_inc(k_rnorm.sem, 1)

            def q_norm(it, g, k):
                pool.wait_ge(ssq_copied.sem, ssq_copied.at(g, 1))
                cut = slice(k * HEADS, (k + 1) * HEADS)
                pool.tensor_tensor(rq[:, cut], qss[:, cut], mhalf[:], ALU.pow).then_inc(q_rnorm.sem, 1)

            def bias(it, g, k):
                pool.wait_ge(mask_row.sem, mask_row.at(g, 1))
                pool.wait_ge(biased.sem, biased.at(g, (k - 1) * NP) if k >= 1 else biased.at(g - 1, (GB - 1) * NP))
                pool.tensor_tensor(biasm[:, k % 2, :, 1:NK], bias0[:],
                                   maskn[:, k].unsqueeze(1).broadcast_to([128, HEADS, S]), ALU.add)\
                    .then_inc(bias_ready.sem, 1)

            iterations(pool, ORDER["pool"], {"xb": add_lnb, "ln1": ln1, "ln2": ln2, "kv": k_norm, "qn": q_norm, "bias": bias,
                                             "bias+": bias, "zT": ln3})

        @block.scalar
        def _(act):
            for n in range(2):
                act.wait_ge(pd, (6, 11)[n])
                act.activation(ph[1], ph[0], ACT.Silu).then_inc(pa, 1)
                act.wait_ge(pp, 1 + 2 * n)
                act.activation(ph[2], banks["S", 0][:, 0:128], ACT.Copy).then_inc(pa, 1)
            act.wait_ge(pp, 4)
            act.wait_ge(load["pb2"], 16)
            act.activation(prev[:, 0:S], banks["S", 1][0:HEADS, 0:S], ACT.Identity, bias=pb2[:]).then_inc(pa, 1)
            act.wait_ge(pd, 19)
            act.activation(rt[1], rt[0], ACT.Exp).then_inc(pa, 1)

            for n in range(4):
                act.wait_ge(pp, 6 + n)
                act.activation(bias0[:, 4 * n:4 * n + 4].rearrange("p h s -> p (h s)"),
                               banks["ST"[n // 2], n % 2][:], ACT.Copy).then_inc(pa, 1)

            def expert(it, g, c):
                act.wait_ge(expert_psum.sem, expert_psum.at(g, 3 * c + 1))
                act.wait_ge(hidden.sem, hidden.at(g, max(c - 1, 0)))
                act.activation(gs[:, c % 2], bank(it, "exp", c, 0)[:], ACT.Copy).then_inc(gate_copied.sem, 1)

            def rw_copy(it, g, k):
                act.wait_ge(rw_psum.sem, rw_psum.at(g, 1))
                act.wait_ge(expert_psum.sem, expert_psum.at(g, 0))
                act.activation(wT[:], bank(it, "rw", 0)[0:E], ACT.Copy).then_inc(rw_turned.sem, 1)

            def y_copy(it, g, k):
                act.wait_ge(y_psum.sem, y_psum.at(g, 1))
                act.wait_ge(qkv_psum.sem, qkv_psum.at(g, 0))
                act.activation(yT[:], bank(it, "down", 0)[:], ACT.Copy).then_inc(y_copied.sem, 1)

            def qk(it, g, k):
                for n, (dst, b) in enumerate(((qT, bq), (kT, bk))):
                    act.wait_ge(qkv_psum.sem, qkv_psum.at(g, n + 1))
                    act.wait_ge(scores_psum.sem, scores_psum.at(g, 0))
                    act.activation(dst[:], bank(it, "qkv", 0, n)[:], ACT.Identity, bias=b).then_inc(qk_copied.sem, 1)

            def xn(it, g, k):
                act.wait_ge(xn_psum.sem, xn_psum.at(g, 1))
                act.wait_ge(kv_psum.sem, kv_psum.at(g, 0))
                act.wait_ge(q_psum.sem, q_psum.at(g, 0))
                act.activation(xnT[:], bank(it, "xnT", 0)[:], ACT.Copy, scale=gnorm).then_inc(xn_copied.sem, 1)

            def q_tile(it, g, c):
                act.wait_ge(q_psum.sem, q_psum.at(g, c + 1))
                act.wait_ge(ssq_psum.sem, ssq_psum.at(g, max(c - 1, 0)))
                act.activation(sq[:, c % 2], bank(it, "q", c)[:], ACT.Square).then_inc(q_squared.sem, 1)

            def kT_copy(it, g, k):
                act.wait_ge(kT_psum.sem, kT_psum.at(g, 1))
                act.wait_ge(sim_psum.sem, sim_psum.at(g, 0))
                src = bank(it, "kT", 0)[:].rearrange("p (b s) -> p b s", b=GB)
                act.activation(kbd[0:64, :, 0, 1:NK], src[0:64], ACT.Copy, scale=ksc[0:64])
                act.activation(kbd[64:128, :, 1, 1:NK], src[64:128], ACT.Copy, scale=ksc[64:128])\
                    .then_inc(kT_copied.sem, 1)

            def exp(it, g, n):
                k = n // 4
                act.wait_ge(max_ready.sem, max_ready.at(g, k + 1))
                act.wait_ge(rden_ready.sem, rden_ready.at(g, k - 1) if k >= 1 else rden_ready.at(g - 1, GB - 1))
                for h in range(n % 4 * 4, n % 4 * 4 + 4):
                    ins = act.activation(sm[:, k % 2, h], sm[:, k % 2, h], ACT.Exp, bias=nmx[:, k % 2, h:h + 1],
                                         accum_out=den[:, k % 2, h:h + 1])
                ins.then_inc(exps.sem, 1)

            def pt_copy(it, g, n):
                if n % 2 == 0:
                    heads = slice(n % 4 * 4, n % 4 * 4 + 4)
                    act.wait_ge(pt_psum.sem, pt_psum.at(g, n + 1))
                    act.wait_ge(pv_psum.sem, pv_psum.at(g, n // 4 * 2))
                    act.activation(pT[:, heads].rearrange("p h s -> p (h s)"), bank(it, "PT", n)[:],
                                   ACT.Copy).then_inc(pt_act.sem, 1)

            def ot_copy(it, g, n):
                pairs = slice(n % 2 * 4, n % 2 * 4 + 4)
                act.wait_ge(ot_psum.sem, ot_psum.at(g, n + 1))
                act.wait_ge(z_psum.sem, z_psum.at(g, n // 2))
                act.activation(oT[:, pairs].rearrange("p c s -> p (c s)"), bank(it, "OT", n)[:],
                               ACT.Identity, bias=nval).then_inc(ot_copied.sem, 1)

            def zT_copy(it, g, k):
                act.wait_ge(zT_psum.sem, zT_psum.at(g, 1))
                act.wait_ge(l1_psum.sem, l1_psum.at(g, 0))
                act.activation(zT[:], bank(it, "zT", 0)[:], ACT.Copy, scale=gout).then_inc(zT_copied.sem, 1)

            def silu(it, g, o):
                act.wait_ge(l1_psum.sem, l1_psum.at(g, 2 * o + 1))
                act.wait_ge(l1_ready.sem, l1_ready.at(g, max(o - 1, 0)))
                act.activation(al[:, o % 2], bank(it, "l1", o, 0)[:], ACT.Silu, scale=w1s[:, o:o + 1])\
                    .then_inc(silued.sem, 1)

            def gelu2(it, g, o):
                act.wait_ge(l2_psum.sem, l2_psum.at(g, o + 1))
                act.wait_ge(l3_psum.sem, l3_psum.at(g, 0))
                act.activation(hB[:, o], bank(it, "l2", o)[:], ACT.Gelu, scale=h1s[:, o:o + 1]).then_inc(l2_ready.sem, 1)

            def gelu3(it, g, o):
                act.wait_ge(l3_psum.sem, l3_psum.at(g, o + 1))
                act.wait_ge(l2_psum.sem, l2_psum.at(g, NO))
                act.activation(hA[:, o], bank(it, "l3", o)[:], ACT.Gelu, scale=h2s[:, o:o + 1]).then_inc(l3_ready.sem, 1)

            act.wait_ge(load["cols"], 16)
            iterations(act, ORDER["act"], {"rw": rw_copy, "exp": expert, "down": y_copy, "qkv": qk, "xnT": xn, "q": q_tile, "kT": kT_copy,
                             "ex": exp, "PT": pt_copy, "OT": ot_copy, "zT": zT_copy,
                             "l1": silu, "l2": gelu2, "l3": gelu3})

        @block.vector
        def _(dve):
            done = [0]

            def link(ins):
                done[0] += 1
                ins.then_inc(pd, 1)
                dve.wait_ge(pd, done[0])

            def te(t):
                return t.rearrange("p (b e) -> p b e", e=E)

            def over(t):
                return t.unsqueeze(2).broadcast_to([128, B, E])

            for n in range(2):
                for m in range(2):
                    dve.memset(halves[64 * m:64 * m + 64, n:n + 1], float(n == m))
            dve.wait_ge(load["rows"], 16)
            dve.wait_ge(const, 3)
            link(dve.scalar_tensor_tensor(ph[3], pw0, pos[:], pb0, ALU.mult, ALU.add))
            link(dve.bn_stats(pst[:], ph[3]))
            link(dve.bn_aggr(pmv[:], pst[:]))
            dve.wait_ge(load["condT"], 16)
            dve.wait_ge(load["wgT"], 16)
            link(dve.tensor_tensor(cg.rearrange("p (b e) -> p b e", e=E), condT[:].unsqueeze(2).broadcast_to([64, B, E]),
                                   wgT[:].unsqueeze(1).broadcast_to([64, B, E]), ALU.mult))
            dve.wait_ge(pg, 2)
            link(dve.tensor_scalar(ph[0], ph[3], pmv[:, 0:1], prs[:, 1:2], ALU.subtract, ALU.mult))
            link(dve.tensor_tensor(ph[0], ph[0], pg0, ALU.mult))
            dve.wait_ge(pp, 2)
            link(dve.tensor_tensor(ph[3], banks["S", 1][:, 0:128], pb1, ALU.add))
            link(dve.bn_stats(pst[:], ph[3]))
            link(dve.bn_aggr(pmv[:], pst[:]))
            dve.wait_ge(pg, 4)
            link(dve.tensor_scalar(ph[0], ph[3], pmv[:, 0:1], prs[:, 1:2], ALU.subtract, ALU.mult))
            link(dve.tensor_tensor(ph[0], ph[0], pg1, ALU.mult))
            link(dve.tensor_tensor(nks, nkey_r, nkey_r, ALU.mult))
            link(dve.tensor_reduce(nkr[:, 0:1], nks, AX, ALU.add))
            dve.wait_ge(load["cols"], 16)
            link(dve.tensor_scalar(nkr[:, 1:2], nkr[:, 0:1], 1e-24, None, ALU.max))
            link(dve.tensor_copy(nkr[:, 0:1], nkey))
            dve.wait_ge(pg, 5)
            for b in range(GB):
                for n in range(2):
                    half = slice(64 * n, 64 * n + 64)
                    ins = dve.tensor_scalar(kbd[half, b, n, 0:1], nkr[half, 0:1], nkr[half, 2:3], ksc[half],
                                            ALU.mult, ALU.mult)
            link(ins)
            dve.wait_ge(pp, 5)
            link(dve.tensor_scalar(lgt, banks["M", 0][:, 0:B * E], 0.5, None, ALU.mult))
            link(dve.tensor_reduce(r1[0], te(lgt), AX, ALU.max))
            link(dve.tensor_tensor(te(rt[0]), te(lgt), over(r1[0]), ALU.subtract))
            dve.wait_ge(pa, 6)
            link(dve.tensor_reduce(r1[1], te(rt[1]), AX, ALU.add))
            link(dve.reciprocal(r1[2], r1[1]))
            link(dve.tensor_tensor(te(rt[2]), te(rt[1]), over(r1[2]), ALU.mult))
            rank = prank[:].unsqueeze(1).broadcast_to([128, B, E])

            def pick(scores, top, onehot):
                link(dve.tensor_reduce(top, te(scores), AX, ALU.max))
                link(dve.tensor_tensor(te(rt[3]), te(scores), over(top), ALU.is_equal))
                link(dve.tensor_tensor(te(rt[3]), te(rt[3]), rank, ALU.mult))
                link(dve.tensor_reduce(r1[5], te(rt[3]), AX, ALU.max))
                link(dve.tensor_tensor(te(onehot), rank, over(r1[5]), ALU.is_equal))

            pick(rt[2], r1[3], rt[4])
            link(dve.scalar_tensor_tensor(rt[5], rt[4], -4.0, rt[2], ALU.mult, ALU.add))
            pick(rt[5], r1[4], rt[6])
            link(dve.tensor_tensor(r1[0], r1[3], r1[4], ALU.add))
            link(dve.tensor_scalar(r1[0], r1[0], 1e-20, None, ALU.add))
            link(dve.reciprocal(r1[1], r1[0]))
            link(dve.tensor_tensor(route, rt[4], rt[6], ALU.add))
            link(dve.tensor_tensor(route, route, rt[2], ALU.mult))
            link(dve.tensor_tensor(te(route), te(route), over(r1[1]), ALU.mult))
            ROUTED.append(done[0])

            own_k, own_z = Signal("own_k", 2), Signal("own_z", 1)

            def row4(r):
                return r.unsqueeze(1).broadcast_to([128, GB, D])

            def expert(it, g, c):
                dve.wait_ge(gate_copied.sem, gate_copied.at(g, c + 1))
                dve.scalar_tensor_tensor(gs[:, c % 2], gs[:, c % 2], 0.01, gs[:, c % 2], ALU.mult, ALU.max)\
                    .then_inc(leaked.sem, 1)
                dve.wait_ge(expert_psum.sem, expert_psum.at(g, 3 * c + 2))
                dve.wait_ge(leaked.sem, leaked.at(g, c + 1))
                dve.wait_ge(y_psum.sem, y_psum.at(g, 0))
                if c < NC_:
                    dve.tensor_tensor(gs[:, c % 2], bank(it, "exp", c, 1)[:], gs[:, c % 2], ALU.mult)\
                        .then_inc(upped.sem, 1)
                    dve.wait_ge(expert_psum.sem, expert_psum.at(g, 3 * c + 3))
                    dve.wait_ge(upped.sem, upped.at(g, c + 1))
                    dve.tensor_tensor(hT[:, c], bank(it, "exp", c, 2)[:], gs[:, c % 2], ALU.mult)\
                        .then_inc(hidden.sem, 1)
                else:
                    dve.tensor_tensor(hT[:, c], bank(it, "exp", c, 1)[:], gs[:, c % 2], ALU.mult)\
                        .then_inc(hidden.sem, 1)

            def rw_take(it, g, k):
                dve.wait_ge(rw_psum.sem, rw_psum.at(g, 0))
                dve.tensor_copy(rg[:], route[:, bass.ds(g * GB * E, GB * E)]).then_inc(rw_taken.sem, 1)

            def values(it, g, k):
                dve.wait_ge(qkv_psum.sem, qkv_psum.at(g, 3))
                dve.wait_ge(mix_psum.sem, mix_psum.at(g, 0))
                dve.tensor_tensor(v1[:], bank(it, "qkv", 0, 2)[:].rearrange("p (b d) -> p b d", b=GB), row4(bv), ALU.add)\
                    .then_inc(v_ready.sem, 1)

            def banding(it, g, k):
                dve.wait_ge(scores_psum.sem, scores_psum.at(g, 1))
                dve.wait_ge(mix_psum.sem, mix_psum.at(g, 0))
                dve.tensor_tensor(st[:], bank(it, "scores", 0)[:].rearrange("p (b s) -> p b s", b=GB),
                                  band[:].unsqueeze(1).broadcast_to([128, GB, S]), ALU.mult).then_inc(banded.sem, 1)

            def stats(src, which, chn, g, n, var):
                for b in range(GB):
                    ins = dve.bn_stats(bs[:, which, b], src[:, b])
                ins.then_inc(chn.sem, 1)
                dve.wait_ge(chn.sem, chn.at(g, n + 1))
                dve.memset(idle[:], 0.0)
                for b in range(GB):
                    ins = dve.bn_aggr(mv[:, which, b], bs[:, which, b])
                ins.then_inc(var.sem, 1)

            def norm(dst, src, which, signal):
                for b in range(GB):
                    ins = dve.tensor_scalar(dst[:, b], src[:, b], mv[:, which, b, 0:1], rstd[:, which, b:b + 1],
                                            ALU.subtract, ALU.mult)
                ins.then_inc(signal.sem, 1)

            def mix_stats(it, g, k):
                dve.wait_ge(mix_psum.sem, mix_psum.at(g, 1))
                stats(bank(it, "mix", 0)[:].rearrange("p (b d) -> p b d", b=GB), 0, own_x, g, 0, ln_var["x"])

            def ln_1(it, g, k):
                dve.wait_ge(ln_rstd["x"].sem, ln_rstd["x"].at(g, 1))
                dve.wait_ge(ln_var["x"].sem, ln_var["x"].at(g, 1))
                dve.wait_ge(xn_psum.sem, xn_psum.at(g, 0))
                norm(n1, bank(it, "mix", 0)[:].rearrange("p (b d) -> p b d", b=GB), 0, mixed)
                dve.wait_ge(mixed.sem, mixed.at(g, 1))
                dve.tensor_tensor(n1[:], n1[:], row4(lnw), ALU.mult).then_inc(own_x.sem, 1)
                dve.wait_ge(own_x.sem, own_x.at(g, 2))
                dve.wait_ge(xb_ready.sem, xb_ready.at(g, 1))
                dve.wait_ge(x1_in_b.sem, x1_in_b.at(g - 1, 1))
                dve.tensor_tensor(x1[:, 0], n1[:], xs[:], ALU.add).then_inc(own_x.sem, 1)
                dve.wait_ge(own_x.sem, own_x.at(g, 3))
                stats(x1[:, 0], 1, own_x, g, 3, ln_var["x"])

            def ln_2(it, g, k):
                dve.wait_ge(ln_rstd["x"].sem, ln_rstd["x"].at(g, 2))
                dve.wait_ge(ln_var["x"].sem, ln_var["x"].at(g, 2))
                norm(n1, x1[:, 0], 1, n2_ready)

            def move_to_c(it, g, k):
                dve.wait_ge(x1_in_b.sem, x1_in_b.at(g, 1))
                dve.wait_ge(out_ready.sem, out_ready.at(g - 1, 1))
                dve.tensor_copy(x1[:, 2], x1[:, 1]).then_inc(x1_in_c.sem, 1)

            def move_to_b(it, g, k):
                dve.wait_ge(own_x.sem, own_x.at(g, 3))
                dve.wait_ge(x1_in_c.sem, x1_in_c.at(g - 1, 1))
                dve.tensor_copy(x1[:, 1], x1[:, 0]).then_inc(x1_in_b.sem, 1)

            def keys(it, g, k):
                dve.wait_ge(kv_psum.sem, kv_psum.at(g, 1))
                dve.tensor_copy(kv[:].rearrange("p b d -> p (b d)"), bank(it, "kv", 0)[:]).then_inc(kv_copied.sem, 1)
                dve.wait_ge(kv_copied.sem, kv_copied.at(g, 1))
                dve.tensor_tensor(ksq[:], kv[:, :, 0:DH], kv[:, :, 0:DH], ALU.mult).then_inc(own_k.sem, 1)
                dve.wait_ge(pv_psum.sem, pv_psum.at(g, 0))
                dve.tensor_tensor(vd[:], kv[:, :, DH:2 * DH], nval_r.unsqueeze(1).broadcast_to([128, GB, DH]),
                                  ALU.subtract).then_inc(v_shifted.sem, 1)
                dve.wait_ge(own_k.sem, own_k.at(g, 1))
                dve.tensor_reduce(ss[:], ksq[:], AX, ALU.add).then_inc(own_k.sem, 1)
                dve.wait_ge(own_k.sem, own_k.at(g, 2))
                dve.tensor_scalar(ss[:], ss[:], 1e-24, None, ALU.max).then_inc(k_squares.sem, 1)

            def q_copy(it, g, c):
                dve.wait_ge(q_squared.sem, q_squared.at(g, c + 1))
                dve.wait_ge(sim_psum.sem, sim_psum.at(g, 0))
                dve.tensor_scalar(qs[:, c], bank(it, "q", c)[:], qsc, None, ALU.mult).then_inc(q_copied.sem, 1)

            def mask_scores(it, g, k):
                dve.wait_ge(mask_loaded.sem, mask_loaded.at(g, 16))
                dve.wait_ge(bias_ready.sem, bias_ready.at(g, 0))
                dve.tensor_scalar(maskn[:], mask[:], -1.0, BIG, ALU.add, ALU.mult).then_inc(mask_row.sem, 1)

            def keys_normed(it, g, k):
                dve.wait_ge(k_rnorm.sem, k_rnorm.at(g, 1))
                dve.wait_ge(kT_psum.sem, kT_psum.at(g, 0))
                for n in range(2):
                    ins = dve.tensor_tensor(kd[:, :, n], kv[:, :, 0:DH], rk[:].unsqueeze(2).broadcast_to([128, GB, DH]),
                                            ALU.mult)
                ins.then_inc(k_normed.sem, 1)

            def q_sums(it, g, k):
                dve.wait_ge(ssq_psum.sem, ssq_psum.at(g, NP))
                dve.wait_ge(biased.sem, biased.at(g, 0))
                dve.tensor_scalar(qss[:], bank(it, "qs", 0)[:, 0:GB * HEADS], 1.0 / SCALE ** 2, 1e-24 / SCALE ** 2,
                                  ALU.mult, ALU.max).then_inc(ssq_copied.sem, 1)

            def score(it, g, j):
                k = j // 4
                dve.wait_ge(q_rnorm.sem, q_rnorm.at(g, k + 1))
                dve.wait_ge(bias_ready.sem, bias_ready.at(g, k + 1))
                dve.wait_ge(pt_psum.sem, pt_psum.at(g, 4 * (k - 1)) if k >= 1 else pt_psum.at(g - 1, 4 * (GB - 1)))
                for m in range(2):
                    dve.wait_ge(sim_psum.sem, sim_psum.at(g, 2 * j + m + 1))
                    for n in range(2):
                        h = 4 * (j % 4) + 2 * m + n
                        ins = dve.scalar_tensor_tensor(sm[:, k % 2, h], bank(it, "sim", j, m)[:, n * NK:(n + 1) * NK],
                                                       rq[:, k * HEADS + h:k * HEADS + h + 1], biasm[:, k % 2, h],
                                                       ALU.mult, ALU.add)
                    ins.then_inc(biased.sem, 1)

            def maxima(it, g, k):
                dve.wait_ge(biased.sem, biased.at(g, (k + 1) * NP))
                dve.wait_ge(exps.sem, exps.at(g, 4 * (k - 1)) if k >= 1 else exps.at(g - 1, 4 * (GB - 1)))
                dve.tensor_reduce(nmx[:, k % 2], sm[:, k % 2], AX, ALU.max, negate=True).then_inc(max_ready.sem, 1)

            def sums_inverse(it, g, k):
                dve.wait_ge(exps.sem, exps.at(g, 4 * (k + 1)))
                dve.wait_ge(normed.sem, normed.at(g, 2 * k))
                dve.reciprocal(rden[:], den[:, k % 2]).then_inc(rden_ready.sem, 1)

            def pt_copy(it, g, n):
                if n % 2 == 1:
                    heads = slice(n % 4 * 4, n % 4 * 4 + 4)
                    dve.wait_ge(pt_psum.sem, pt_psum.at(g, n + 1))
                    dve.wait_ge(pv_psum.sem, pv_psum.at(g, n // 4 * 2))
                    dve.tensor_copy(pT[:, heads].rearrange("p h s -> p (h s)"), bank(it, "PT", n)[:])\
                        .then_inc(pt_dve.sem, 1)

            def pv_norm(it, g, n):
                dve.wait_ge(rden_ready.sem, rden_ready.at(g, n // 2 + 1))
                dve.wait_ge(ot_psum.sem, ot_psum.at(g, n // 2 * 2))
                dve.wait_ge(pv_psum.sem, pv_psum.at(g, n + 1))
                heads = slice(n % 2 * 8, n % 2 * 8 + 8)
                dve.tensor_tensor(on[:, heads], bank(it, "PV", n)[:].rearrange("p (h d) -> p h d", h=8),
                                  rden[:, heads].unsqueeze(2).broadcast_to([128, 8, DH]), ALU.mult)\
                    .then_inc(normed.sem, 1)

            z_rows = zbank[:].rearrange("p (b d) -> p b d", b=GB)

            def z_stats(it, g, k):
                dve.wait_ge(z_psum.sem, z_psum.at(g, GB))
                stats(z_rows, 2, own_z, g, 0, ln_var["z"])

            def ln_z(it, g, k):
                dve.wait_ge(ln_rstd["z"].sem, ln_rstd["z"].at(g, 1))
                dve.wait_ge(ln_var["z"].sem, ln_var["z"].at(g, 1))
                dve.wait_ge(zT_psum.sem, zT_psum.at(g, 0))
                norm(n3, z_rows, 2, n3_ready)

            def gated(it, g, o):
                dve.wait_ge(silued.sem, silued.at(g, o + 1))
                dve.wait_ge(l1_psum.sem, l1_psum.at(g, 2 * o + 2))
                dve.wait_ge(l4_psum.sem, l4_psum.at(g, 0))
                dve.scalar_tensor_tensor(hA[:, o], bank(it, "l1", o, 1)[:], w2s[:, o:o + 1], al[:, o % 2],
                                         ALU.mult, ALU.mult).then_inc(l1_ready.sem, 1)

            def result(it, g, k):
                dve.wait_ge(l4_psum.sem, l4_psum.at(g, 1))
                dve.wait_ge(stored, g * 16)
                dve.tensor_tensor(res[:], bank(it, "l4", 0)[:].rearrange("p (b d) -> p b d", b=GB), row4(w3s), ALU.mult)\
                    .then_inc(scaled.sem, 1)
                dve.wait_ge(scaled.sem, scaled.at(g, 1))
                dve.wait_ge(x1_in_c.sem, x1_in_c.at(g, 1))
                dve.tensor_tensor(res[:], res[:], x1[:, 2], ALU.add).then_inc(out_ready.sem, 1)

            iterations(dve, ORDER["dve"], {
                "rw": rw_take, "exp": expert, "qkv": values, "scores": banding, "mix": mix_stats, "ln1": ln_1, "ln2": ln_2,
                "kv": keys, "kT": keys_normed, "q": q_copy, "ssq": q_sums, "maskn": mask_scores, "move1": move_to_c,
                "move2": move_to_b, "sim": score, "max": maxima, "rden": sums_inverse, "PT": pt_copy, "PV": pv_norm,
                "ln3": z_stats, "zT": ln_z, "l1": gated, "l4": result})

        @block.tensor
        def _(pe):
            pe.wait_ge(const, 3)
            pe.wait_ge(load["pw1"], 16)
            pe.wait_ge(load["pw2"], 16)
            for n in range(2):
                pe.wait_ge(pa, 1 + 2 * n)
                pe.transpose(banks["S", 0][:, 0:128], ph[1], ident[:]).then_inc(pp, 1)
                pe.wait_ge(pa, 2 + 2 * n)
                if n == 0:
                    pe.matmul(banks["S", 1][:, 0:128], ph[2], pw1[:], start=True, stop=True).then_inc(pp, 1)
                else:
                    pe.matmul(banks["S", 1][0:HEADS, 0:S], pw2[:], ph[2], start=True, stop=True).then_inc(pp, 1)
            pe.wait_ge(pd, 4)
            pe.wait_ge(load["wt"], 16)
            pe.wait_ge(load["xT"], 16)
            pe.matmul(banks["M", 0][:, 0:B * E], ones[:], cg, start=True, stop=True)
            for b in range(B):
                ins = pe.matmul(banks["M", 0][:, b * E:(b + 1) * E], xT[:, b * S:(b + 1) * S], wt[:],
                                start=False, stop=True, skip_group_check=True)
            ins.then_inc(pp, 1)
            pe.wait_ge(pd, ROUTED[0])
            pe.wait_ge(s_toepl, 16)
            for n in range(4):
                pe.matmul(banks["ST"[n // 2], n % 2][:], flip, pT[:, 4 * n:4 * n + 4].rearrange("p h s -> p (h s)"),
                          start=True, stop=True).then_inc(pp, 1)
            pe.wait_ge(pa, 10)

            def free(it, step, k, n=0, *data):
                events = {signal: SHIFT[STAGE[step]] * signal.per + count for signal, count in data}
                drained = drained_before(it, step, k, n)
                if drained is not None:
                    signal, count = drained
                    events[signal] = max(count, events.get(signal, count))
                for signal, count in events.items():
                    pe.wait_ge(signal.sem, signal.at(it, count))
                return bank(it, step, k, n)

            waited = set()

            def weights(*names):
                for n in names:
                    if n not in waited:
                        waited.add(n)
                        pe.wait_ge(load[n], 16)

            def expert(it, g, c):
                weights("wg", "wu")
                x = xg[:]
                cut = slice(c * 128, (c + 1) * 128)
                pe.matmul(free(it, "exp", c, 0, (x_loaded, 16))[:], wg[:, cut], x, start=True, stop=True).then_inc(expert_psum.sem, 1)
                pe.matmul(free(it, "exp", c, 1)[:], wu[:, cut], x, start=True, stop=True).then_inc(expert_psum.sem, 1)
                if c < NC_:
                    pe.matmul(free(it, "exp", c, 2, (rw_turned, 1))[:], sel[:, c], wT[:], start=True, stop=True)\
                        .then_inc(expert_psum.sem, 1)

            def rw_turn(it, g, k):
                ps = free(it, "rw", 0, 0, (rw_taken, 1))
                for b in range(GB):
                    ins = pe.transpose(ps[0:E, b * S:(b + 1) * S], rg[:, b * E:(b + 1) * E], ident[:])
                ins.then_inc(rw_psum.sem, 1)

            def down(it, g, k):
                weights("wd")
                ps = free(it, "down", 0, 0, (hidden, 1))
                for c in range(NX):
                    if c > 0:
                        pe.wait_ge(hidden.sem, hidden.at(g, c + 1))
                    ins = pe.matmul(ps[:], wd[:, c], hT[:, c], start=(c == 0), stop=(c == NX - 1))
                ins.then_inc(y_psum.sem, 1)

            def qkv(it, g, k):
                weights("wqkv")
                for n in range(2):
                    pe.matmul(free(it, "qkv", 0, n, (y_copied, 1))[:], wqkv[:, n * D:(n + 1) * D], yT[:], start=True, stop=True)\
                        .then_inc(qkv_psum.sem, 1)
                ps = free(it, "qkv", 0, 2)
                for b in range(GB):
                    ins = pe.matmul(ps[:, b * D:(b + 1) * D], yT[:, b * S:(b + 1) * S], wqkv[:, 2 * D:3 * D],
                                    start=True, stop=True)
                ins.then_inc(qkv_psum.sem, 1)

            def scores(it, g, k):
                ps = free(it, "scores", 0, 0, (qk_copied, 2))
                for b in range(GB):
                    cut = slice(b * S, (b + 1) * S)
                    ins = pe.matmul(ps[:, cut], kT[:, cut], qT[:, cut], start=True, stop=True)
                ins.then_inc(scores_psum.sem, 1)

            def mix(it, g, k):
                ps = free(it, "mix", 0, 0, (v_ready, 1), (banded, 1))
                for b in range(GB):
                    ins = pe.matmul(ps[:, b * D:(b + 1) * D], st[:, b], v1[:, b], start=True, stop=True)
                ins.then_inc(mix_psum.sem, 1)

            def turn(it, step, src, ready, g, signal):
                ps = free(it, step, 0, 0, (ready, 1))
                for b in range(GB):
                    ins = pe.transpose(ps[:, b * S:(b + 1) * S], src(b), ident[:])
                ins.then_inc(signal.sem, 1)

            def xn_turn(it, g, k):
                turn(it, "xnT", lambda b: n1[:, b], n2_ready, g, xn_psum)

            def kv_proj(it, g, k):
                weights("wkv2")
                ps = free(it, "kv", 0, 0, (xn_copied, 1))
                for b in range(GB):
                    ins = pe.matmul(ps[:, b * 128:(b + 1) * 128], xnT[:, b * S:(b + 1) * S], wkv2[:], start=True, stop=True)
                ins.then_inc(kv_psum.sem, 1)

            def q_proj(it, g, c):
                weights("wq2")
                pe.matmul(free(it, "q", c, 0, (xn_copied, 1))[:], wq2[:, c * 128:(c + 1) * 128], xnT[:], start=True, stop=True)\
                    .then_inc(q_psum.sem, 1)

            def q_sum(it, g, c):
                ps = free(it, "qs", 0) if c == 0 else bank(it, "qs", 0)
                pe.wait_ge(q_squared.sem, q_squared.at(g, c + 1))
                for b in range(GB):
                    ins = pe.matmul(ps[:, b * HEADS + 2 * c:b * HEADS + 2 * c + 2], sq[:, c % 2, b * S:(b + 1) * S],
                                    halves[:], start=True, stop=True)
                ins.then_inc(ssq_psum.sem, 1)

            def k_turn(it, g, k):
                turn(it, "kT", lambda b: kd[:, b].rearrange("p n d -> p (n d)"), k_normed, g, kT_psum)

            def sim(it, g, j):
                k = j // 4
                for m in range(2):
                    pe.matmul(free(it, "sim", j, m, (kT_copied, 1), (q_copied, NP))[:, 0:2 * NK], qs[:, 2 * (j % 4) + m, k * S:(k + 1) * S],
                              kbd[:, k].rearrange("p n s -> p (n s)"), start=True, stop=True).then_inc(sim_psum.sem, 1)

            def p_turn(it, g, n):
                ps = free(it, "PT", n, 0, (exps, n + 1))
                for j in range(4):
                    ins = pe.transpose(ps[:, j * S:(j + 1) * S], sm[:, n // 4 % 2, n % 4 * 4 + j, 1:NK], ident[:])
                ins.then_inc(pt_psum.sem, 1)

            def pv(it, g, n):
                ps = free(it, "PV", n, 0, (v_shifted, 1), (pt_act, n + 1), (pt_dve, n + 1))
                for j in range(8):
                    ins = pe.matmul(ps[:, j * DH:(j + 1) * DH], pT[:, n % 2 * 8 + j], vd[:, n // 2], start=True, stop=True)
                ins.then_inc(pv_psum.sem, 1)

            def o_turn(it, g, n):
                ps = free(it, "OT", n, 0, (normed, n + 1))
                for j in range(4):
                    h = n % 2 * 8 + 2 * j
                    ins = pe.transpose(ps[:, j * S:(j + 1) * S], on[:, h:h + 2].rearrange("p h d -> p (h d)"), ident[:])
                ins.then_inc(ot_psum.sem, 1)

            def z_proj(it, g, n):
                weights("wout")
                if n == 0:
                    pe.wait_ge(n3_ready.sem, n3_ready.at(g, 0))
                pe.wait_ge(ot_copied.sem, ot_copied.at(g, n + 1))
                k = n // 2
                for c in range(n % 2 * 4, n % 2 * 4 + 4):
                    ins = pe.matmul(zbank[:, k * D:(k + 1) * D], oT[:, c], wout[:, c], start=(c == 0), stop=(c == NP - 1))
                if n % 2 == 1:
                    ins.then_inc(z_psum.sem, 1)

            def z_turn(it, g, k):
                turn(it, "zT", lambda b: n3[:, b], n3_ready, g, zT_psum)

            def layer1(it, g, o):
                weights("w1", "w2")
                for n, w in enumerate((w1, w2)):
                    pe.matmul(free(it, "l1", o, n, (zT_copied, 1))[:], w[:, o * 128:(o + 1) * 128], zT[:], start=True, stop=True)\
                        .then_inc(l1_psum.sem, 1)

            def layer(step, w, src, ready, signal):
                def part(it, g, o):
                    weights("h1", "h2")
                    ps = free(it, step, o, 0, (ready, 1 if o == 0 else NO))
                    for c in range(NO):
                        if o == 0 and c > 0:
                            pe.wait_ge(ready.sem, ready.at(g, c + 1))
                        ins = pe.matmul(ps[:], w[:, c, o * 128:(o + 1) * 128], src[:, c], start=(c == 0), stop=(c == NO - 1))
                    ins.then_inc(signal.sem, 1)
                return part

            def layer4(it, g, k):
                weights("w3")
                ps = free(it, "l4", 0, 0, (l3_ready, NO))
                for b in range(GB):
                    for c in range(NO):
                        ins = pe.matmul(ps[:, b * D:(b + 1) * D], hA[:, c, b * S:(b + 1) * S], w3[:, c],
                                        start=(c == 0), stop=(c == NO - 1))
                ins.then_inc(l4_psum.sem, 1)

            iterations(pe, ORDER["pe"], {
                "rw": rw_turn, "exp": expert, "down": down, "qkv": qkv, "scores": scores, "mix": mix, "xnT": xn_turn,
                "kv": kv_proj, "q": q_proj, "qs": q_sum, "kT": k_turn, "sim": sim, "PT": p_turn, "PV": pv, "OT": o_turn,
                "z": z_proj, "zT": z_turn, "l1": layer1, "l2": layer("l2", h1, hA, l1_ready, l2_psum),
                "l3": layer("l3", h2, hB, l2_ready, l3_psum), "l4": layer4})


ROUTED = []


def kernel(**inputs):
    import numpy as np
    import concourse.bacc as bacc
    from concourse.bass_utils import run_bass_kernel_spmd

    x, cond = np.asarray(inputs["x"]), np.asarray(inputs["cond_64"])
    i = {k: np.asarray(v) for k, v in inputs.items()}
    L = {k[3:]: v for k, v in i.items() if k.startswith("L0_")}

    def tiles(w):
        return w.reshape(-1, 128, w.shape[1]).transpose(1, 0, 2)

    def col(v):
        return v.reshape(-1, 128).T

    twice = lambda v: np.concatenate([v, v])
    wexp = lambda w, s: np.concatenate([w.transpose(1, 0, 2).reshape(D, E * EM), s], axis=1)
    arrays = {
        "x": x,
        "xT": x.reshape(B * S, D).T,
        "mask": i["mask_BxS_bf1"].reshape(B * S),
        "cols": np.concatenate(
            [col(L["ffn_w1_s"]), col(L["ffn_w2_s"]), col(L["ffn_h1_s"]), col(L["ffn_h2_s"]),
             col(L["attn_b_qkv"][0:D]), col(L["attn_b_qkv"][D:2 * D]), col(L["cond2_g_norm"]), col(L["cond2_g_out"]),
             col(twice(L["cond2_q_scale"])), col(twice(L["cond2_k_scale"])), col(twice(cond[0])), col(twice(cond[1]))],
            axis=1),
        "rows": np.concatenate(
            [L["attn_ln_w"], L["attn_ln_b"], L["attn_b_qkv"][2 * D:], L["ffn_w3_s"], L["cond2_w0"][0], L["cond2_b0"],
             L["cond2_g0"], L["cond2_b1"], L["cond2_g1"], cond[0], cond[1], L["cond2_null_attn_bias"]])[None],
        "wt": L["cond_wt"].T, "wgT": L["cond_wg"].T, "condT": cond.T,
        "pw1": L["cond2_w1"], "pw2": L["cond2_w2"], "pb2": L["cond2_b2"][:, None],
        "wg": wexp(L["cond_w_gate"], L["cond_sw_gate"]), "wu": wexp(L["cond_w_up"], L["cond_sw_up"]),
        "wd": tiles(np.concatenate([L["cond_w_down"].reshape(E * EM, D), L["cond_sw_down"]])),
        "wqkv": L["attn_W_qkv"], "wq2": L["cond2_Wq"], "wkv2": L["cond2_Wkv"], "wout": tiles(L["cond2_Wout"]),
        "w1": L["ffn_w1_w"].T, "w2": L["ffn_w2_w"].T, "h1": tiles(L["ffn_h1_w"].T), "h2": tiles(L["ffn_h2_w"].T),
        "w3": tiles(L["ffn_w3_w"].T),
    }
    arrays = {n: np.ascontiguousarray(v) for n, v in arrays.items()}
    nc = bacc.Bacc("TRN2", target_bir_lowering=False, num_devices=1)
    aps = {n: nc.dram_tensor("in_" + n, v.shape, mybir.dt.from_np(v.dtype), kind="ExternalInput").ap()
           for n, v in arrays.items()}
    out = nc.dram_tensor("out_y", (B, S, D), mybir.dt.float32, kind="ExternalOutput").ap()
    ROUTED.clear()
    layer_kernel(nc, aps, out)
    r = run_bass_kernel_spmd(nc, [{"in_" + n: v for n, v in arrays.items()}], core_ids=[0])
    return r.results[0]["out_y"]
```

```python
import concourse.bass as bass
from concourse import mybir
from contextlib import ExitStack

B, S, D = 32, 128, 128
GB = 4
NG = B // GB
GT = GB * S
E, EM = 8, 64
NC_ = E * EM // 128
NX = NC_ + 1
HEADS, DH = 16, 64
NP = HEADS // 2
NK = S + 1
HID = 512
NO = HID // 128
SPAN = 32
LN_EPS = 1e-5
BIG = 1e30
SCALE = 8.0

ORDER = {
    "pe": """
        rw.0 sim.0 exp.0 sim.1 exp.1-2 sim.2 exp.3 sim.3 exp.4 down.0 PT.0 sim.4 zT.0 PT.1 sim.5 qkv.0 l1.0 PT.2
        sim.6 l1.1 PV.0 l1.2-3 l2.0 sim.7 PT.3 scores.0 l2.1 PT.4 sim.8 z.0 PT.5 l2.2 sim.9 l2.3 mix.0 PV.1 PT.6
        sim.10 l3.0 PT.7 sim.11 z.1 PV.2 sim.12 PV.3 PT.8 l3.1 z.2 PT.9 sim.13 l3.2-3 z.3 xnT.0 PT.10 sim.14
        PV.4 q.0-1 sim.15 PT.11 kv.0 qs.0 l4.0 qs.1 q.2-3 PT.12 q.4 qs.2 PV.5 qs.3 q.5 z.4 qs.4 q.6 qs.5 q.7
        qs.6 PT.13 qs.7 PT.14 z.5 PT.15 kT.0 PV.6-7 z.6-7
    """,
    "act": """
        xh.0 rw.0 exp.0-4 ex.0-2 PT.0 down.0 zT.0 ex.3 PT.1 qkv.0 l1.0-1 PT.2 l1.2-3 ex.4-5 PT.3 PV.0 l2.0-1
        PT.4 ex.6 PT.5 ex.7 l2.2 PV.1 PT.6 l2.3 ex.8 PT.7 ex.9 PV.2 ex.10 l3.0 PV.3 PT.8 l3.1 ex.11 PT.9 l3.2-3
        xnT.0 PT.10 ex.12 q.0 PV.4 q.1 ex.13 PT.11 q.2 ex.14 q.3 PT.12 ex.15 q.4-7 PV.5 PT.13-15 kT.0 PV.6-7
    """,
    "dve": """
        rw.0 xl.0 ln3.0 rwl.0 sim.0 exp.0 sim.1 exp.1-2 max.0 sim.2 exp.3 max.1-2 inv.0 sim.3 exp.4 zT.0 inv.1
        max.3 inv.2 sim.4 down.0 zl.0 PT.0 inv.3 sim.5 move1.0 PT.1 max.4 qkv.0 l1.0 max.5 l1.1-2 sim.6 PT.2
        l1.3 inv.4 move2.0 max.6 sim.7 inv.5 PT.3 scores.0 max.7 sim.8 PT.4 max.8 inv.6 sim.9 PT.5 inv.7 mix.0
        max.9 sim.10 PT.6 sim.11 inv.8 max.10 inv.9 PT.7 ln1.0 inv.10 sim.12 max.11 ln2.0 PT.8 sim.13 PT.9
        max.12 xnT.0 inv.11 PT.10 sim.14 max.13 q.0 sim.15 inv.12 max.14 q.1 kv.0 inv.13 max.15 PT.11 l4.0
        inv.14 maskn.0 q.2-3 PT.12 inv.15 kT.0 q.4-7 ssq.0 PT.13-15 vs.0
    """,
    "pool": """
        zT.0 pn.0 bias.4 pn.1 bias.5 pn.2 bias.6 pn.3 bias.7-10 pn.4 bias.11 pn.5-7 bias.12 ln1.0 bias.13 xb.0
        pn.8-9 bias.14 ln2.0 pn.10-11 bias.15 pn.12-14 bias+.0 kv.0 pn.15 bias+.1-3 qn.0-3
    """,
    "sp": """
        rw.0 l4.0 maskn.0
    """,
}


def parsed(text):
    items = []
    for item in text.split():
        step, ks = item.split(".")
        first, *last = ks.split("-")
        items += [(step, k) for k in range(int(first), int(last[0] if last else first) + 1)]
    return items


ORDER = {engine: parsed(text) for engine, text in ORDER.items()}
STAGE = {s: "A" for s in ("rw", "exp", "down", "qkv", "scores", "mix", "xnT", "kv", "q", "qs", "ssq", "qn", "kT",
                          "bias+", "maskn", "xb", "ln1", "ln2", "xh", "xl", "rwl", "vs")}
STAGE |= {s: "B" for s in ("bias", "sim", "max", "ex", "inv", "pn", "PT", "PV", "z", "move2")}
STAGE |= {s: "C" for s in ("ln3", "zT", "zl", "l1", "l2", "l3", "l4", "move1")}
LOOP = 2
SHIFT = {"A": 1, "B": 0, "C": -1}

USES = {"rw": "M", "exp": "MMM", "down": "M", "qkv": "MMM", "scores": "M", "mix": "M", "xnT": "M",
        "kv": "M", "q": "M", "ssq": "", "kT": "M", "sim": "SS", "PT": "T", "PV": "T", "zT": "M",
        "l1": "MM", "l2": "M", "l3": "M", "l4": "M"}
BANKS = {"M": 3, "S": 2, "T": 2}


def uses(step, k):
    if step == "qs":
        return "S" if k == 0 else ""
    return "MM" if (step, k) == ("exp", NX - 1) else USES.get(step, "")


def stages_of(it):
    return [s for s in "ABC" if 0 <= it + SHIFT[s] < NG]


def bank_plan():
    last, plan = {}, {}
    for it in range(-1, NG + 1):
        active, turn, here = stages_of(it), {r: 0 for r in BANKS}, {}
        for step, k in ORDER["pe"]:
            for n, ring in enumerate(uses(step, k)):
                bank = (ring, turn[ring] % BANKS[ring])
                turn[ring] += 1
                if STAGE[step] not in active:
                    continue
                here[step, k, n] = (bank, last.get(bank), it)
                last[bank] = (step, k, n, it)
        plan[it] = {u: (bank, before and (*before[:3], it - before[3])) for u, (bank, before, _) in here.items()}
    for it in range(LOOP, NG - 1):
        assert plan[it] == plan[LOOP], "the loop's iterations differ"
    return plan


PLAN = bank_plan()


def layer_kernel(nc, a, out):
    fp32, f32r, u8 = mybir.dt.float32, mybir.dt.float32r, mybir.dt.uint8
    ALU, ACT, AX = mybir.AluOpType, mybir.ActivationFunctionType, mybir.AxisListType.X
    ctx = ExitStack()
    with ctx:
        def sb(name, shape, dt=fp32):
            return ctx.enter_context(nc.sbuf_tensor("sb_" + name, shape, dt))

        def sem(name):
            return ctx.enter_context(nc.semaphore("s_" + name))

        class Signal:

            def __init__(self, name, per_group):
                self.sem, self.per = sem(name), per_group

            def at(self, g, n):
                v = g * self.per + n
                return max(v, 0) if isinstance(v, int) else v

        xg, xh, xl = sb("xg", [128, GT]), sb("xh", [128, GT], f32r), sb("xl", [128, GT], f32r)
        xs = sb("xs", [128, GB, D])
        x1 = sb("x1", [128, 3, GB, D])
        wgu = [sb("wgu" + n, [128, 2, NX * 128], f32r) for n in "hl"]
        wd = sb("wd", [128, NX, D])
        wqkv, wq2, wkv2, w12 = ([sb(name + n, [128, size], f32r) for n in "hl"]
                                for name, size in (("wqkv", 3 * D), ("wq2", HEADS * DH), ("wkv2", 2 * DH), ("w12", 2 * HID)))
        wout = sb("wout", [128, NP, D])
        h1, h2, w3 = sb("h1", [128, NO, HID]), sb("h2", [128, NO, HID]), sb("w3", [128, NO, D])
        wt, wgT, condT = sb("wt", [128, E]), sb("wgT", [64, E]), sb("condT", [64, B])
        pw1, pw2, pb2 = sb("pw1", [128, 128]), sb("pw2", [128, HEADS]), sb("pb2", [HEADS, 1])
        NCOL = 4 * NO + 8
        cols = sb("cols", [128, NCOL])
        w1s, w2s, h1s, h2s = (cols[:, NO * i:NO * i + NO] for i in range(4))
        bq, bk, gnorm, gout, qsc, ksc, nkey, nval = (cols[:, 4 * NO + i:4 * NO + i + 1] for i in range(8))
        NROW = 9 * 128 + 2 * DH + HEADS
        rows = sb("rows", [128, NROW])
        lnw, lnb, bv, w3s, pw0, pb0, pg0, pb1, pg1 = (rows[:, 128 * i:128 * i + 128] for i in range(9))
        nkey_r, nval_r = rows[:, 1152:1152 + DH], rows[:, 1152 + DH:1152 + 2 * DH]
        nbias = rows[:, 1152 + 2 * DH:NROW]
        mask = sb("mask", [128, GB, S], u8)
        ident = sb("ident", [128, 128])
        band = sb("band", [128, 128])
        halves = sb("halves", [128, 2])
        ones = sb("ones", [64, 128])
        sel = sb("sel", [E, NC_, 128], f32r)
        eps = sb("eps", [128, GB])
        mhalf = sb("mhalf", [128, 16])
        route = sb("route", [128, B * E])[:]
        rg = sb("rg", [128, GB * E])
        wTh, wTl = sb("wTh", [E, GT], f32r), sb("wTl", [E, GT], f32r)
        bias0 = sb("bias0", [128, HEADS, S])
        biasm = sb("biasm", [128, HEADS, NK])
        maskn = sb("maskn", [128, GB, S])
        gs = sb("gs", [128, 2, GT])
        hT = sb("hT", [128, NX, GT])
        yT, xnT = ([sb(name + n, [128, GT], f32r) for n in "hl"] for name in ("yT", "xnT"))
        qT, kT = hT[:, 0], hT[:, 1]
        v1, st = (gs[:, n].rearrange("p (b d) -> p b d", b=GB) for n in range(2))
        sq = hT[:, 0:2]
        ksq = hT[:, 2, 0:GB * DH].rearrange("p (b d) -> p b d", b=GB)
        kd = hT[:, 2].rearrange("p (b n d) -> p b n d", b=GB, n=2)
        kv, n1 = (hT[:, n].rearrange("p (b d) -> p b d", b=GB) for n in (3, 4))
        bs = sb("bs", [128, 3, GB, 6])
        mv = sb("mv", [128, 3, GB, 2])
        ve = sb("ve", [128, 3, GB])
        idle = sb("idle", [128, 1])
        rstd = sb("rstd", [128, 3, GB])
        qs = sb("qs", [128, NP, GT])
        vz = sb("vz", [128, GB, 2, 3 * DH], f32r)
        ss, rk = sb("ss", [128, GB]), sb("rk", [128, GB])
        qss, rq = sb("qss", [128, GB * HEADS]), sb("rq", [128, GB * HEADS])
        kbd = sb("kbd", [128, GB, 2, NK])
        sm = sb("sm", [128, HEADS, NK])
        nmx, den, rden = sb("nmx", [128, HEADS]), sb("den", [128, HEADS]), sb("rden", [128, HEADS])
        pTh, pTl, oT = sb("pTh", [128, HEADS, S], f32r), sb("pTl", [128, HEADS, S], f32r), sb("oT", [128, NP, S])
        n3, zT = sb("n3", [128, GB, D]), [sb("zT" + n, [128, GT], f32r) for n in "hl"]
        al, hA, hB = sb("al", [128, 2, GT]), sb("hA", [128, NO, GT]), sb("hB", [128, NO, GT])
        res = sb("res", [128, GB, D])
        xT = qs[:].rearrange("p c t -> p (c t)")
        lgt, *rt = (hA[:, i // 2, i % 2 * 256:(i % 2 + 1) * 256] for i in range(8))
        ph = [hB[:, 0, 128 * i:128 * i + 128] for i in range(4)]
        nks = hB[:, 1, 0:DH]
        flip = hB[:, 1, 256:384]
        prev = hB[0:HEADS, 2, 0:2 * S]
        cg = hB[0:64, 3, 0:B * E]
        r1 = [hB[:, 1, 64 + B * i:64 + B * (i + 1)] for i in range(6)]
        turned_bias = sm[:, :, 0:S]
        wgu_raw = hT[:].rearrange("p c t -> p (c t)")[:, 0:2 * NX * 128].rearrange("p (n m) -> p n m", n=2)
        raw = {"wqkv": n3[:].rearrange("p b d -> p (b d)")[:, 0:3 * D], "wq2": oT[:].rearrange("p c s -> p (c s)"),
               "wkv2": res[:].rearrange("p b d -> p (b d)")[:, 0:2 * DH], "w12": al[:].rearrange("p n t -> p (n t)")}
        parts = {"wqkv": wqkv, "wq2": wq2, "wkv2": wkv2, "w12": w12}
        sel_raw = xs[0:E].rearrange("p b d -> p (b d)")
        prank = sb("prank", [128, E])
        pos = sb("pos", [128, 1])
        pi = sb("pi", [128, 1], mybir.dt.int32)
        pst = sb("pst", [128, 6])
        pmv = sb("pmv", [128, 2])
        prs = sb("prs", [128, 2])
        nkr = sb("nkr", [128, 3])

        banks = {(r, i): ctx.enter_context(nc.psum_tensor(f"ps_{r}{i}", [128, 512], fp32))
                 for r, n in BANKS.items() for i in range(n)}
        zbank = ctx.enter_context(nc.psum_tensor("ps_z", [128, 512], fp32))
        toeplitz = nc.dram_tensor("toeplitz", (HEADS, 2 * S), fp32, kind="Internal").ap()

        load = {n: sem("ld_" + n) for n in a if n not in ("x", "mask")}
        mask_loaded = Signal("mask_loaded", 16)
        s_toep, s_toepl = sem("toep_stored"), sem("bias_loaded")
        const = sem("const")
        pa, pd, pp, pg = sem("pro_act"), sem("pro_dve"), sem("pro_pe"), sem("pro_pool")
        x_loaded, xs_loaded = Signal("x_loaded", 16), Signal("xs_loaded", 16)
        xb_ready = Signal("xb_ready", 1)
        x1_in_b, x1_in_c = Signal("x1_in_b", 1), Signal("x1_in_c", 1)
        own_x = Signal("own_x", 4)
        rw_taken, rw_psum, rw_turned = Signal("rw_taken", 1), Signal("rw_psum", 1), Signal("rw_turned", 1)
        expert_psum = Signal("expert_psum", 3 * NX - 1)
        x_high, x_low, w_high, w_low = Signal("x_high", 1), Signal("x_low", 1), sem("w_high"), sem("w_low")
        rw_low = Signal("rw_low", 1)
        gate_copied = Signal("gate_copied", NX)
        leaked = Signal("leaked", NX)
        upped = Signal("upped", NC_)
        hidden = Signal("hidden", NX)
        parts_high, parts_low = {n: sem("high_" + n) for n in parts}, {n: sem("low_" + n) for n in parts}
        y_low, xn_low, z_low = Signal("y_low", 1), Signal("xn_low", 1), Signal("z_low", 1)
        y_psum, y_copied = Signal("y_psum", 1), Signal("y_copied", 1)
        qkv_psum, qk_copied, v_ready = Signal("qkv_psum", 3), Signal("qk_copied", 2), Signal("v_ready", 1)
        scores_psum, banded = Signal("scores_psum", 1), Signal("banded", 1)
        mix_psum = Signal("mix_psum", 1)
        mixed = Signal("mixed", 1)
        n2_ready, xn_psum, xn_copied = Signal("n2_ready", 1), Signal("xn_psum", 1), Signal("xn_copied", 1)
        ln_var = {s: Signal("var_" + s, n) for s, n in (("x", 2), ("z", 1))}
        ln_eps = {s: Signal("eps_" + s, n) for s, n in (("x", 2), ("z", 1))}
        ln_rstd = {s: Signal("rstd_" + s, n) for s, n in (("x", 2), ("z", 1))}
        kv_psum, kv_copied, v_shifted = Signal("kv_psum", 1), Signal("kv_copied", 1), Signal("v_shifted", 1)
        k_squares, k_rnorm, k_normed = Signal("k_squares", 1), Signal("k_rnorm", 1), Signal("k_normed", 1)
        kT_psum, kT_copied = Signal("kT_psum", 1), Signal("kT_copied", 1)
        q_psum, q_squared, q_copied = Signal("q_psum", NP), Signal("q_squared", NP), Signal("q_copied", NP)
        ssq_psum, ssq_copied, q_rnorm = Signal("ssq_psum", NP), Signal("ssq_copied", 1), Signal("q_rnorm", GB)
        mask_row, bias_ready = Signal("mask_row", 1), Signal("bias_ready", 4 * GB)
        sim_psum, biased = Signal("sim_psum", GB * NP), Signal("biased", GB * NP)
        max_ready, exps = Signal("max_ready", GB * 4), Signal("exps", GB * 4)
        pt_psum = Signal("pt_psum", GB * 4)
        pt_high, pt_low = Signal("pt_high", GB * 4), Signal("pt_low", GB * 4)
        rden_ready, p_normed = Signal("rden_ready", GB * 4), Signal("p_normed", GB * 4)
        pv_psum, ot_copied = Signal("pv_psum", GB * 2), Signal("ot_copied", GB * 2)
        z_psum, n3_ready = Signal("z_psum", GB * 2), Signal("n3_ready", 1)
        zT_psum, zT_copied = Signal("zT_psum", 1), Signal("zT_copied", 1)
        l1_psum, silued, l1_ready = Signal("l1_psum", 2 * NO), Signal("silued", NO), Signal("l1_ready", NO)
        l2_psum, l2_ready = Signal("l2_psum", NO), Signal("l2_ready", NO)
        l3_psum, l3_ready = Signal("l3_psum", NO), Signal("l3_ready", NO)
        l4_psum, scaled, out_ready = Signal("l4_psum", 1), Signal("scaled", 1), Signal("out_ready", 1)
        stored = sem("stored")

        DRAINED = {}
        for c in range(NX):
            DRAINED |= {("exp", c, 0): (gate_copied, c + 1), ("exp", c, 2): (hidden, c + 1),
                        ("exp", c, 1): (upped, c + 1) if c < NC_ else (hidden, c + 1)}
        DRAINED |= {("rw", 0, 0): (rw_low, 1), ("down", 0, 0): (y_low, 1),
                    ("qkv", 0, 0): (qk_copied, 1), ("qkv", 0, 1): (qk_copied, 2), ("qkv", 0, 2): (v_ready, 1), ("scores", 0, 0): (banded, 1), ("mix", 0, 0): (mixed, 1),
                    ("xnT", 0, 0): (xn_low, 1), ("kv", 0, 0): (kv_copied, 1), ("qs", 0, 0): (ssq_copied, 1),
                    ("kT", 0, 0): (kT_copied, 1), ("zT", 0, 0): (z_low, 1), ("l4", 0, 0): (scaled, 1)}
        DRAINED |= {("q", c, 0): (q_copied, c + 1) for c in range(NP)}
        DRAINED |= {("sim", p // 2, p % 2): (biased, p + 1) for p in range(GB * NP)}
        DRAINED |= {("PT", n, 0): (pt_low, n + 1) for n in range(4 * GB)}
        DRAINED |= {("PV", n, 0): (ot_copied, n + 1) for n in range(2 * GB)}
        for o in range(NO):
            DRAINED |= {("l1", o, 0): (silued, o + 1), ("l1", o, 1): (l1_ready, o + 1),
                        ("l2", o, 0): (l2_ready, o + 1), ("l3", o, 0): (l3_ready, o + 1)}

        def kind(it):
            return it if isinstance(it, int) else LOOP

        def bank(it, step, k, n=0):
            return banks[PLAN[kind(it)][step, k, n][0]]

        def drained_before(it, step, k, n=0):
            before = PLAN[kind(it)][step, k, n][1]
            if before is None:
                return None
            signal, count = DRAINED[before[:3]]
            return signal, (SHIFT[STAGE[before[0]]] - before[3]) * signal.per + count

        def iterations(eng, order, steps):
            def body(it):
                for step, k in order:
                    if STAGE[step] in stages_of(kind(it)):
                        steps[step](it, it + SHIFT[STAGE[step]], k)
            for it in range(-1, LOOP):
                body(it)
            with eng.Fori(LOOP, NG - 1) as it:
                body(it)
            body(NG - 1)
            body(NG)

        block = ctx.enter_context(nc.Block())

        @block.sync
        def _(sp):
            def fetch(name, dst, src=None):
                sp.dma_start(dst, a[name] if src is None else src).then_inc(load[name], 16)

            fetch("cols", cols[:])
            fetch("rows", rows[:], bass.AP(tensor=a["rows"].tensor, offset=0, ap=[[0, 128], [1, NROW]]))
            fetch("wt", wt[:])
            fetch("wgT", wgT[:])
            fetch("condT", condT[:])
            fetch("pw1", pw1[:])
            fetch("pw2", pw2[:])
            fetch("pb2", pb2[:])
            fetch("xT", xT)
            fetch("wg", wgu_raw[:, 0])
            fetch("wu", wgu_raw[:, 1])
            fetch("wd", wd[:])
            fetch("wqkv", raw["wqkv"])
            sp.wait_ge(pa, 5)
            sp.dma_start(toeplitz, prev).then_inc(s_toep, 16)
            sp.wait_ge(s_toep, 16)
            sp.dma_start(turned_bias, bass.AP(tensor=toeplitz.tensor, offset=0,
                                        ap=[[1, 128], [2 * S, HEADS], [1, S]])).then_inc(s_toepl, 16)
            fetch("wq2", raw["wq2"])
            fetch("wkv2", raw["wkv2"])
            fetch("wout", wout[:])
            fetch("w12", raw["w12"])
            fetch("h1", h1[:])
            fetch("h2", h2[:])
            fetch("w3", w3[:])

            def load_x(it, g, k):
                sp.wait_ge(x_low.sem, x_low.at(g, 0))
                sp.dma_start(xg[:], a["xT"][:, bass.ds(g * GT, GT)]).then_inc(x_loaded.sem, 16)
                sp.wait_ge(own_x.sem, own_x.at(g, 0))
                sp.dma_start(xs[:], a["x"][bass.ds(g * GB, GB), :, :].rearrange("b p f -> p b f"))\
                    .then_inc(xs_loaded.sem, 16)

            def load_mask(it, g, k):
                first = g * GT if isinstance(g, int) else sp.snap(g * GT)
                sp.wait_ge(mask_row.sem, mask_row.at(g, 0))
                sp.dma_start(mask[:].rearrange("p b s -> p (b s)"),
                             a["mask"][bass.ds(first, GT)].unsqueeze(0).broadcast_to([128, GT]))\
                    .then_inc(mask_loaded.sem, 16)

            def store(it, g, k):
                sp.wait_ge(out_ready.sem, out_ready.at(g, 1))
                sp.dma_start(out[bass.ds(g * GB, GB), :, :].rearrange("b p f -> p b f"), res[:]).then_inc(stored, 16)

            iterations(sp, ORDER["sp"], {"rw": load_x, "maskn": load_mask, "l4": store})
            sp.wait_ge(stored, 16 * NG)

        @block.gpsimd
        def _(pool):
            pool.memset(ident[:], 0.0)
            pool.memset(band[:], 1.0 / 64.0)
            pool.memset(sel_raw, 0.0)
            pool.memset(ones[:], 1.0)
            pool.memset(eps[:], LN_EPS)
            pool.memset(mhalf[:], -0.5)
            pool.memset(kbd[:], 0.0)
            pool.memset(prev, -BIG)
            pool.memset(flip, 0.0)
            pool.iota(pi[:], [[0, 1]], base=S - 1, channel_multiplier=-1).then_inc(const, 1)
            pool.wait_ge(const, 1)
            pool.affine_select(ident[:], ident[:], [[-1, 128]], ALU.not_equal, 1.0, base=0, channel_multiplier=1)
            pool.affine_select(flip, flip, [[1, 128]], ALU.not_equal, 1.0, base=1 - S, channel_multiplier=1)
            pool.affine_select(band[:], band[:], [[1, 128]], ALU.is_ge, 0.0, base=0, channel_multiplier=-1)
            sel_4d = sel_raw.rearrange("e (c a m) -> e c a m", c=NC_, a=2)
            pool.affine_select(sel_4d, sel_4d,
                               [[-2, NC_], [-1, 2], [0, EM]], ALU.not_equal, 1.0, base=0, channel_multiplier=1)
            for e in range(E):
                pool.memset(prank[:, e:e + 1], float(E - e))
            pool.tensor_copy(pos[:], pi[:]).then_inc(const, 1)
            pool.wait_ge(const, 2)
            pool.affine_select(band[:], band[:], [[-1, 128]], ALU.is_ge, 0.0, base=SPAN - 1, channel_multiplier=1)\
                .then_inc(const, 1)

            def power(out_, var, base, add, gate):
                pool.wait_ge(pd, gate)
                pool.tensor_scalar(prs[:, 0:1], var, add, 1.0, ALU.add, ALU.mult).then_inc(pg, 1)
                pool.wait_ge(pg, base)
                pool.tensor_tensor(out_, prs[:, 0:1], mhalf[:, 0:1], ALU.pow).then_inc(pg, 1)

            power(prs[:, 1:2], pmv[:, 1:2], 1, LN_EPS, 4)
            power(prs[:, 1:2], pmv[:, 1:2], 3, LN_EPS, 9)
            pool.wait_ge(pd, 15)
            pool.tensor_tensor(nkr[:, 2:3], nkr[:, 1:2], mhalf[:, 0:1], ALU.pow).then_inc(pg, 1)
            pool.wait_ge(load["rows"], 16)
            pool.tensor_copy(biasm[:, :, 0], nbias).then_inc(pg, 1)
            pool.wait_ge(pa, 10)

            def rsqrt(which, ln, n):
                def part(it, g, k):
                    pool.wait_ge(ln_var[ln].sem, ln_var[ln].at(g, n))
                    pool.tensor_tensor(ve[:, which], mv[:, which, :, 1], eps[:], ALU.add)\
                        .then_inc(ln_eps[ln].sem, 1)
                    pool.wait_ge(ln_eps[ln].sem, ln_eps[ln].at(g, n))
                    pool.tensor_tensor(rstd[:, which], ve[:, which], mhalf[:, 0:GB], ALU.pow)\
                        .then_inc(ln_rstd[ln].sem, 1)
                return part

            ln1, ln2, ln3 = (rsqrt(w, s, n) for w, s, n in ((0, "x", 1), (1, "x", 2), (2, "z", 1)))

            def add_lnb(it, g, k):
                pool.wait_ge(xs_loaded.sem, xs_loaded.at(g, 16))
                pool.tensor_tensor(xs[:], xs[:], lnb.unsqueeze(1).broadcast_to([128, GB, D]), ALU.add)\
                    .then_inc(xb_ready.sem, 1)

            def k_norm(it, g, k):
                pool.wait_ge(k_squares.sem, k_squares.at(g, 1))
                pool.tensor_tensor(rk[:], ss[:], mhalf[:, 0:GB], ALU.pow).then_inc(k_rnorm.sem, 1)

            def q_norm(it, g, k):
                pool.wait_ge(ssq_copied.sem, ssq_copied.at(g, 1))
                cut = slice(k * HEADS, (k + 1) * HEADS)
                pool.tensor_tensor(rq[:, cut], qss[:, cut], mhalf[:], ALU.pow).then_inc(q_rnorm.sem, 1)

            def bias(it, g, j):
                heads = slice(j % 4 * 4, j % 4 * 4 + 4)
                pool.wait_ge(mask_row.sem, mask_row.at(g, 1))
                pool.wait_ge(biased.sem, biased.at(g, 2 * (j - 4) + 2))
                pool.tensor_tensor(biasm[:, heads, 1:NK], bias0[:, heads],
                                   maskn[:, j // 4].unsqueeze(1).broadcast_to([128, 4, S]), ALU.add)\
                    .then_inc(bias_ready.sem, 1)

            def p_norm(it, g, j):
                heads = slice(j % 4 * 4, j % 4 * 4 + 4)
                pool.wait_ge(rden_ready.sem, rden_ready.at(g, j + 1))
                pool.tensor_tensor(sm[:, heads, 1:NK], sm[:, heads, 1:NK],
                                   rden[:, heads].unsqueeze(2).broadcast_to([128, 4, S]), ALU.mult)\
                    .then_inc(p_normed.sem, 1)

            iterations(pool, ORDER["pool"], {"xb": add_lnb, "ln1": ln1, "ln2": ln2, "kv": k_norm, "qn": q_norm,
                                             "pn": p_norm, "bias": bias,
                                             "bias+": bias, "zT": ln3})

        @block.scalar
        def _(act):
            for n in range(2):
                act.wait_ge(pd, (6, 11)[n])
                act.activation(ph[1], ph[0], ACT.Silu).then_inc(pa, 1)
                act.wait_ge(pp, 1 + 2 * n)
                act.activation(ph[2], banks["S", 0][:, 0:128], ACT.Copy).then_inc(pa, 1)
            act.wait_ge(pp, 4)
            act.wait_ge(load["pb2"], 16)
            act.activation(prev[:, 0:S], banks["S", 1][0:HEADS, 0:S], ACT.Identity, bias=pb2[:]).then_inc(pa, 1)
            act.wait_ge(load["wg"], 16)
            act.wait_ge(load["wu"], 16)
            act.activation(wgu[0][:], wgu_raw, ACT.Copy).then_inc(w_high, 1)
            act.wait_ge(pd, 19)
            act.activation(rt[1], rt[0], ACT.Exp).then_inc(pa, 1)

            for n in range(4):
                act.wait_ge(pp, 6 + n)
                act.activation(bias0[:, 4 * n:4 * n + 4].rearrange("p h s -> p (h s)"),
                               banks["ST"[n // 2], n % 2][:], ACT.Copy).then_inc(pa, 1)

            def weights_high(*names):
                for n in names:
                    act.wait_ge(load[n], 16)
                    act.activation(parts[n][0][:], raw[n], ACT.Copy).then_inc(parts_high[n], 1)

            def expert(it, g, c):
                if kind(it) == -1 and c == NX - 1:
                    weights_high("wqkv", "wkv2", "wq2", "w12")
                act.wait_ge(expert_psum.sem, expert_psum.at(g, 3 * c + 1))
                act.wait_ge(mix_psum.sem, mix_psum.at(g, 0))
                act.wait_ge(hidden.sem, hidden.at(g, max(c - 1, 0)))
                act.activation(gs[:, c % 2], bank(it, "exp", c, 0)[:], ACT.Copy).then_inc(gate_copied.sem, 1)

            def x_split(it, g, k):
                act.wait_ge(x_loaded.sem, x_loaded.at(g, 16))
                act.wait_ge(expert_psum.sem, expert_psum.at(g, 0))
                act.activation(xh[:], xg[:], ACT.Copy).then_inc(x_high.sem, 1)

            def rw_copy(it, g, k):
                act.wait_ge(rw_psum.sem, rw_psum.at(g, 1))
                act.wait_ge(expert_psum.sem, expert_psum.at(g, 0))
                act.activation(wTh[:], bank(it, "rw", 0)[0:E], ACT.Copy).then_inc(rw_turned.sem, 1)

            def y_copy(it, g, k):
                act.wait_ge(y_psum.sem, y_psum.at(g, 1))
                act.wait_ge(qkv_psum.sem, qkv_psum.at(g, 0))
                act.activation(yT[0][:], bank(it, "down", 0)[:], ACT.Copy).then_inc(y_copied.sem, 1)

            def qk(it, g, k):
                for n, (dst, b) in enumerate(((qT, bq), (kT, bk))):
                    act.wait_ge(qkv_psum.sem, qkv_psum.at(g, n + 1))
                    act.wait_ge(scores_psum.sem, scores_psum.at(g, 0))
                    act.activation(dst, bank(it, "qkv", 0, n)[:], ACT.Identity, bias=b).then_inc(qk_copied.sem, 1)

            def xn(it, g, k):
                act.wait_ge(xn_psum.sem, xn_psum.at(g, 1))
                act.wait_ge(kv_psum.sem, kv_psum.at(g, 0))
                act.wait_ge(q_psum.sem, q_psum.at(g, 0))
                act.activation(xnT[0][:], bank(it, "xnT", 0)[:], ACT.Copy, scale=gnorm).then_inc(xn_copied.sem, 1)

            def q_tile(it, g, c):
                act.wait_ge(q_psum.sem, q_psum.at(g, c + 1))
                act.wait_ge(ssq_psum.sem, ssq_psum.at(g, max(c - 1, 0)))
                act.activation(sq[:, c % 2], bank(it, "q", c)[:], ACT.Square).then_inc(q_squared.sem, 1)

            def kT_copy(it, g, k):
                act.wait_ge(kT_psum.sem, kT_psum.at(g, 1))
                act.wait_ge(sim_psum.sem, sim_psum.at(g, 0))
                src = bank(it, "kT", 0)[:].rearrange("p (b s) -> p b s", b=GB)
                act.activation(kbd[0:64, :, 0, 1:NK], src[0:64], ACT.Copy, scale=ksc[0:64])
                act.activation(kbd[64:128, :, 1, 1:NK], src[64:128], ACT.Copy, scale=ksc[64:128])\
                    .then_inc(kT_copied.sem, 1)

            def exp(it, g, j):
                act.wait_ge(max_ready.sem, max_ready.at(g, j + 1))
                for h in range(j % 4 * 4, j % 4 * 4 + 4):
                    ins = act.activation(sm[:, h], sm[:, h], ACT.Exp, bias=nmx[:, h:h + 1], accum_out=den[:, h:h + 1])
                ins.then_inc(exps.sem, 1)

            def pt_copy(it, g, j):
                heads = slice(j % 4 * 4, j % 4 * 4 + 4)
                act.wait_ge(pt_psum.sem, pt_psum.at(g, j + 1))
                act.wait_ge(pv_psum.sem, pv_psum.at(g, j // 2 - 1))
                act.activation(pTh[:, heads].rearrange("p h s -> p (h s)"), bank(it, "PT", j)[:], ACT.Copy)\
                    .then_inc(pt_high.sem, 1)

            def ot_copy(it, g, n):
                pairs = slice(n % 2 * 4, n % 2 * 4 + 4)
                act.wait_ge(pv_psum.sem, pv_psum.at(g, n + 1))
                act.wait_ge(z_psum.sem, z_psum.at(g, n - 1))
                act.activation(oT[:, pairs].rearrange("p c s -> p (c s)"), bank(it, "PV", n)[:],
                               ACT.Identity, bias=nval).then_inc(ot_copied.sem, 1)

            def zT_copy(it, g, k):
                act.wait_ge(zT_psum.sem, zT_psum.at(g, 1))
                act.wait_ge(l1_psum.sem, l1_psum.at(g, 0))
                act.activation(zT[0][:], bank(it, "zT", 0)[:], ACT.Copy, scale=gout).then_inc(zT_copied.sem, 1)

            def silu(it, g, o):
                act.wait_ge(l1_psum.sem, l1_psum.at(g, 2 * o + 1))
                act.wait_ge(l1_ready.sem, l1_ready.at(g, max(o - 1, 0)))
                act.activation(al[:, o % 2], bank(it, "l1", o, 0)[:], ACT.Silu, scale=w1s[:, o:o + 1])\
                    .then_inc(silued.sem, 1)

            def gelu2(it, g, o):
                act.wait_ge(l2_psum.sem, l2_psum.at(g, o + 1))
                act.wait_ge(l3_psum.sem, l3_psum.at(g, 0))
                act.activation(hB[:, o], bank(it, "l2", o)[:], ACT.Gelu, scale=h1s[:, o:o + 1]).then_inc(l2_ready.sem, 1)

            def gelu3(it, g, o):
                act.wait_ge(l3_psum.sem, l3_psum.at(g, o + 1))
                act.wait_ge(l2_psum.sem, l2_psum.at(g, NO))
                act.activation(hA[:, o], bank(it, "l3", o)[:], ACT.Gelu, scale=h2s[:, o:o + 1]).then_inc(l3_ready.sem, 1)

            act.wait_ge(load["cols"], 16)
            iterations(act, ORDER["act"], {"xh": x_split, "rw": rw_copy, "exp": expert, "down": y_copy, "qkv": qk,
                                           "xnT": xn, "q": q_tile, "kT": kT_copy,
                             "ex": exp, "PT": pt_copy, "PV": ot_copy, "zT": zT_copy,
                             "l1": silu, "l2": gelu2, "l3": gelu3})

        @block.vector
        def _(dve):
            done = [0]

            def link(ins):
                done[0] += 1
                ins.then_inc(pd, 1)
                dve.wait_ge(pd, done[0])

            def te(t):
                return t.rearrange("p (b e) -> p b e", e=E)

            def over(t):
                return t.unsqueeze(2).broadcast_to([128, B, E])

            for n in range(2):
                for m in range(2):
                    dve.memset(halves[64 * m:64 * m + 64, n:n + 1], float(n == m))
            dve.wait_ge(load["rows"], 16)
            dve.wait_ge(const, 3)
            dve.tensor_copy(sel[:].rearrange("e c m -> e (c m)"), sel_raw).then_inc(w_low, 1)
            link(dve.scalar_tensor_tensor(ph[3], pw0, pos[:], pb0, ALU.mult, ALU.add))
            link(dve.bn_stats(pst[:], ph[3]))
            link(dve.bn_aggr(pmv[:], pst[:]))
            dve.wait_ge(load["condT"], 16)
            dve.wait_ge(load["wgT"], 16)
            link(dve.tensor_tensor(cg.rearrange("p (b e) -> p b e", e=E), condT[:].unsqueeze(2).broadcast_to([64, B, E]),
                                   wgT[:].unsqueeze(1).broadcast_to([64, B, E]), ALU.mult))
            dve.wait_ge(pg, 2)
            link(dve.tensor_scalar(ph[0], ph[3], pmv[:, 0:1], prs[:, 1:2], ALU.subtract, ALU.mult))
            link(dve.tensor_tensor(ph[0], ph[0], pg0, ALU.mult))
            dve.wait_ge(pp, 2)
            link(dve.tensor_tensor(ph[3], banks["S", 1][:, 0:128], pb1, ALU.add))
            link(dve.bn_stats(pst[:], ph[3]))
            link(dve.bn_aggr(pmv[:], pst[:]))
            dve.wait_ge(pg, 4)
            link(dve.tensor_scalar(ph[0], ph[3], pmv[:, 0:1], prs[:, 1:2], ALU.subtract, ALU.mult))
            link(dve.tensor_tensor(ph[0], ph[0], pg1, ALU.mult))
            link(dve.tensor_tensor(nks, nkey_r, nkey_r, ALU.mult))
            link(dve.tensor_reduce(nkr[:, 0:1], nks, AX, ALU.add))
            dve.wait_ge(load["cols"], 16)
            link(dve.tensor_scalar(nkr[:, 1:2], nkr[:, 0:1], 1e-24, None, ALU.max))
            link(dve.tensor_copy(nkr[:, 0:1], nkey))
            dve.wait_ge(pg, 5)
            for b in range(GB):
                for n in range(2):
                    half = slice(64 * n, 64 * n + 64)
                    ins = dve.tensor_scalar(kbd[half, b, n, 0:1], nkr[half, 0:1], nkr[half, 2:3], ksc[half],
                                            ALU.mult, ALU.mult)
            link(ins)
            dve.memset(vz[:].bitcast(fp32), 0.0).then_inc(w_low, 1)
            dve.wait_ge(w_high, 1)
            dve.tensor_tensor(wgu[1][:], wgu_raw, wgu[0][:].bitcast(fp32), ALU.subtract).then_inc(w_low, 1)
            dve.wait_ge(w_low, 3)
            dve.wait_ge(pp, 5)
            link(dve.tensor_scalar(lgt, banks["M", 0][:, 0:B * E], 0.5, None, ALU.mult))
            link(dve.tensor_reduce(r1[0], te(lgt), AX, ALU.max))
            link(dve.tensor_tensor(te(rt[0]), te(lgt), over(r1[0]), ALU.subtract))
            dve.wait_ge(pa, 6)
            link(dve.tensor_reduce(r1[1], te(rt[1]), AX, ALU.add))
            link(dve.reciprocal(r1[2], r1[1]))
            link(dve.tensor_tensor(te(rt[2]), te(rt[1]), over(r1[2]), ALU.mult))
            rank = prank[:].unsqueeze(1).broadcast_to([128, B, E])

            def pick(scores, top, onehot):
                link(dve.tensor_reduce(top, te(scores), AX, ALU.max))
                link(dve.tensor_tensor(te(rt[3]), te(scores), over(top), ALU.is_equal))
                link(dve.tensor_tensor(te(rt[3]), te(rt[3]), rank, ALU.mult))
                link(dve.tensor_reduce(r1[5], te(rt[3]), AX, ALU.max))
                link(dve.tensor_tensor(te(onehot), rank, over(r1[5]), ALU.is_equal))

            pick(rt[2], r1[3], rt[4])
            link(dve.scalar_tensor_tensor(rt[5], rt[4], -4.0, rt[2], ALU.mult, ALU.add))
            pick(rt[5], r1[4], rt[6])
            link(dve.tensor_tensor(r1[0], r1[3], r1[4], ALU.add))
            link(dve.tensor_scalar(r1[0], r1[0], 1e-20, None, ALU.add))
            link(dve.reciprocal(r1[1], r1[0]))
            link(dve.tensor_tensor(route, rt[4], rt[6], ALU.add))
            link(dve.tensor_tensor(route, route, rt[2], ALU.mult))
            link(dve.tensor_tensor(te(route), te(route), over(r1[1]), ALU.mult))

            own_k, own_v, own_z = Signal("own_k", 2), Signal("own_v", 2), Signal("own_z", 1)

            def row4(r):
                return r.unsqueeze(1).broadcast_to([128, GB, D])

            def weights_low(*names):
                for n in names:
                    dve.wait_ge(parts_high[n], 1)
                    dve.tensor_tensor(parts[n][1][:], raw[n], parts[n][0][:].bitcast(fp32), ALU.subtract)\
                        .then_inc(parts_low[n], 1)

            def low(dst, src, high, scale, signal):
                if scale is None:
                    dve.tensor_tensor(dst, src, high.bitcast(fp32), ALU.subtract).then_inc(signal.sem, 1)
                else:
                    dve.scalar_tensor_tensor(dst, src, scale, high.bitcast(fp32), ALU.mult, ALU.subtract)\
                        .then_inc(signal.sem, 1)

            def y_split(it, g, k):
                dve.wait_ge(y_copied.sem, y_copied.at(g, 1))
                dve.wait_ge(qkv_psum.sem, qkv_psum.at(g, 0))
                low(yT[1][:], bank(it, "down", 0)[:], yT[0][:], None, y_low)

            def xn_split(it, g, k):
                dve.wait_ge(xn_copied.sem, xn_copied.at(g, 1))
                dve.wait_ge(kv_psum.sem, kv_psum.at(g, 0))
                dve.wait_ge(q_psum.sem, q_psum.at(g, 0))
                low(xnT[1][:], bank(it, "xnT", 0)[:], xnT[0][:], gnorm, xn_low)

            def z_split(it, g, k):
                dve.wait_ge(zT_copied.sem, zT_copied.at(g, 1))
                dve.wait_ge(l1_psum.sem, l1_psum.at(g, 0))
                low(zT[1][:], bank(it, "zT", 0)[:], zT[0][:], gout, z_low)

            def expert(it, g, c):
                if kind(it) == -1 and c == NX - 1:
                    weights_low("wqkv", "wkv2", "wq2", "w12")
                dve.wait_ge(gate_copied.sem, gate_copied.at(g, c + 1))
                dve.scalar_tensor_tensor(gs[:, c % 2], gs[:, c % 2], 0.01, gs[:, c % 2], ALU.mult, ALU.max)\
                    .then_inc(leaked.sem, 1)
                dve.wait_ge(expert_psum.sem, expert_psum.at(g, 3 * c + 2))
                dve.wait_ge(leaked.sem, leaked.at(g, c + 1))
                dve.wait_ge(y_psum.sem, y_psum.at(g, 0))
                dve.wait_ge(ssq_psum.sem, ssq_psum.at(g, 0))
                dve.wait_ge(kT_psum.sem, kT_psum.at(g, 0))
                dve.wait_ge(xn_psum.sem, xn_psum.at(g, 0))
                if c < NC_:
                    dve.tensor_tensor(gs[:, c % 2], bank(it, "exp", c, 1)[:], gs[:, c % 2], ALU.mult)\
                        .then_inc(upped.sem, 1)
                    dve.wait_ge(expert_psum.sem, expert_psum.at(g, 3 * c + 3))
                    dve.wait_ge(upped.sem, upped.at(g, c + 1))
                    dve.tensor_tensor(hT[:, c], bank(it, "exp", c, 2)[:], gs[:, c % 2], ALU.mult)\
                        .then_inc(hidden.sem, 1)
                else:
                    dve.tensor_tensor(hT[:, c], bank(it, "exp", c, 1)[:], gs[:, c % 2], ALU.mult)\
                        .then_inc(hidden.sem, 1)

            def rw_take(it, g, k):
                dve.wait_ge(rw_psum.sem, rw_psum.at(g, 0))
                dve.tensor_copy(rg[:], route[:, bass.ds(g * GB * E, GB * E)]).then_inc(rw_taken.sem, 1)

            def x_split(it, g, k):
                dve.wait_ge(x_high.sem, x_high.at(g, 1))
                dve.wait_ge(expert_psum.sem, expert_psum.at(g, 0))
                dve.tensor_tensor(xl[:], xg[:], xh[:].bitcast(fp32), ALU.subtract).then_inc(x_low.sem, 1)

            def rw_split(it, g, k):
                dve.wait_ge(rw_turned.sem, rw_turned.at(g, 1))
                dve.wait_ge(expert_psum.sem, expert_psum.at(g, 0))
                dve.tensor_tensor(wTl[:], bank(it, "rw", 0)[0:E], wTh[:].bitcast(fp32), ALU.subtract)\
                    .then_inc(rw_low.sem, 1)

            def values(it, g, k):
                dve.wait_ge(qkv_psum.sem, qkv_psum.at(g, 3))
                dve.wait_ge(mix_psum.sem, mix_psum.at(g, 0))
                dve.tensor_tensor(v1, bank(it, "qkv", 0, 2)[:].rearrange("p (b d) -> p b d", b=GB), row4(bv), ALU.add)\
                    .then_inc(v_ready.sem, 1)

            def banding(it, g, k):
                dve.wait_ge(scores_psum.sem, scores_psum.at(g, 1))
                dve.wait_ge(mix_psum.sem, mix_psum.at(g, 0))
                dve.tensor_tensor(st, bank(it, "scores", 0)[:].rearrange("p (b s) -> p b s", b=GB),
                                  band[:].unsqueeze(1).broadcast_to([128, GB, S]), ALU.mult).then_inc(banded.sem, 1)

            def stats(src, which, chn, g, n, var):
                for b in range(GB):
                    ins = dve.bn_stats(bs[:, which, b], src[:, b])
                ins.then_inc(chn.sem, 1)
                dve.wait_ge(chn.sem, chn.at(g, n + 1))
                dve.memset(idle[:], 0.0)
                for b in range(GB):
                    ins = dve.bn_aggr(mv[:, which, b], bs[:, which, b])
                ins.then_inc(var.sem, 1)

            def norm(dst, src, which, signal):
                for b in range(GB):
                    ins = dve.tensor_scalar(dst[:, b], src[:, b], mv[:, which, b, 0:1], rstd[:, which, b:b + 1],
                                            ALU.subtract, ALU.mult)
                ins.then_inc(signal.sem, 1)

            def mix_stats(it, g, k):
                dve.wait_ge(mix_psum.sem, mix_psum.at(g, 1))
                stats(bank(it, "mix", 0)[:].rearrange("p (b d) -> p b d", b=GB), 0, own_x, g, 0, ln_var["x"])

            def ln_1(it, g, k):
                dve.wait_ge(ln_rstd["x"].sem, ln_rstd["x"].at(g, 1))
                dve.wait_ge(ln_var["x"].sem, ln_var["x"].at(g, 1))
                dve.wait_ge(xn_psum.sem, xn_psum.at(g, 0))
                norm(n1, bank(it, "mix", 0)[:].rearrange("p (b d) -> p b d", b=GB), 0, mixed)
                dve.wait_ge(mixed.sem, mixed.at(g, 1))
                dve.tensor_tensor(n1, n1, row4(lnw), ALU.mult).then_inc(own_x.sem, 1)
                dve.wait_ge(own_x.sem, own_x.at(g, 2))
                dve.wait_ge(xb_ready.sem, xb_ready.at(g, 1))
                dve.wait_ge(x1_in_b.sem, x1_in_b.at(g - 1, 1))
                dve.tensor_tensor(x1[:, 0], n1, xs[:], ALU.add).then_inc(own_x.sem, 1)
                dve.wait_ge(own_x.sem, own_x.at(g, 3))
                stats(x1[:, 0], 1, own_x, g, 3, ln_var["x"])

            def ln_2(it, g, k):
                dve.wait_ge(ln_rstd["x"].sem, ln_rstd["x"].at(g, 2))
                dve.wait_ge(ln_var["x"].sem, ln_var["x"].at(g, 2))
                norm(n1, x1[:, 0], 1, n2_ready)

            def move_to_c(it, g, k):
                dve.wait_ge(x1_in_b.sem, x1_in_b.at(g, 1))
                dve.wait_ge(out_ready.sem, out_ready.at(g - 1, 1))
                dve.tensor_copy(x1[:, 2], x1[:, 1]).then_inc(x1_in_c.sem, 1)

            def move_to_b(it, g, k):
                dve.wait_ge(own_x.sem, own_x.at(g, 3))
                dve.wait_ge(x1_in_c.sem, x1_in_c.at(g - 1, 1))
                dve.tensor_copy(x1[:, 1], x1[:, 0]).then_inc(x1_in_b.sem, 1)

            def keys(it, g, k):
                dve.wait_ge(kv_psum.sem, kv_psum.at(g, 1))
                dve.tensor_copy(kv.rearrange("p b d -> p (b d)"), bank(it, "kv", 0)[:]).then_inc(kv_copied.sem, 1)
                dve.wait_ge(kv_copied.sem, kv_copied.at(g, 1))
                dve.tensor_tensor(ksq, kv[:, :, 0:DH], kv[:, :, 0:DH], ALU.mult).then_inc(own_k.sem, 1)
                dve.wait_ge(own_k.sem, own_k.at(g, 1))
                dve.tensor_reduce(ss[:], ksq, AX, ALU.add).then_inc(own_k.sem, 1)
                dve.wait_ge(own_k.sem, own_k.at(g, 2))
                dve.tensor_scalar(ss[:], ss[:], 1e-24, None, ALU.max).then_inc(k_squares.sem, 1)

            def values_split(it, g, k):
                v = kv[:, :, DH:2 * DH]
                dve.tensor_tensor(v, v, nval_r.unsqueeze(1).broadcast_to([128, GB, DH]), ALU.subtract)\
                    .then_inc(own_v.sem, 1)
                dve.wait_ge(own_v.sem, own_v.at(g, 1))
                dve.wait_ge(pv_psum.sem, pv_psum.at(g, 0))
                vh, vl = (vz[:, :, n, DH:2 * DH] for n in range(2))
                dve.tensor_copy(vh, v).then_inc(own_v.sem, 1)
                dve.wait_ge(own_v.sem, own_v.at(g, 2))
                dve.tensor_tensor(vl, v, vh.bitcast(fp32), ALU.subtract).then_inc(v_shifted.sem, 1)

            def q_copy(it, g, c):
                dve.wait_ge(q_squared.sem, q_squared.at(g, c + 1))
                dve.wait_ge(sim_psum.sem, sim_psum.at(g, 0))
                dve.tensor_scalar(qs[:, c], bank(it, "q", c)[:], qsc, None, ALU.mult).then_inc(q_copied.sem, 1)

            def mask_scores(it, g, k):
                dve.wait_ge(mask_loaded.sem, mask_loaded.at(g, 16))
                dve.wait_ge(bias_ready.sem, bias_ready.at(g, 0))
                dve.tensor_scalar(maskn[:], mask[:], -1.0, BIG, ALU.add, ALU.mult).then_inc(mask_row.sem, 1)

            def keys_normed(it, g, k):
                dve.wait_ge(k_rnorm.sem, k_rnorm.at(g, 1))
                dve.wait_ge(kT_psum.sem, kT_psum.at(g, 0))
                for n in range(2):
                    ins = dve.tensor_tensor(kd[:, :, n], kv[:, :, 0:DH], rk[:].unsqueeze(2).broadcast_to([128, GB, DH]),
                                            ALU.mult)
                ins.then_inc(k_normed.sem, 1)

            def q_sums(it, g, k):
                dve.wait_ge(ssq_psum.sem, ssq_psum.at(g, NP))
                dve.wait_ge(biased.sem, biased.at(g, 0))
                dve.tensor_scalar(qss[:], bank(it, "qs", 0)[:, 0:GB * HEADS], 1.0 / SCALE ** 2, 1e-24 / SCALE ** 2,
                                  ALU.mult, ALU.max).then_inc(ssq_copied.sem, 1)

            def score(it, g, j):
                k = j // 4
                dve.wait_ge(q_rnorm.sem, q_rnorm.at(g, k + 1))
                dve.wait_ge(bias_ready.sem, bias_ready.at(g, j + 1))
                dve.wait_ge(pt_psum.sem, pt_psum.at(g, j - 3))
                for m in range(2):
                    dve.wait_ge(sim_psum.sem, sim_psum.at(g, 2 * j + m + 1))
                    for n in range(2):
                        h = 4 * (j % 4) + 2 * m + n
                        ins = dve.scalar_tensor_tensor(sm[:, h], bank(it, "sim", j, m)[:, n * NK:(n + 1) * NK],
                                                       rq[:, k * HEADS + h:k * HEADS + h + 1], biasm[:, h],
                                                       ALU.mult, ALU.add)
                    ins.then_inc(biased.sem, 1)

            def maxima(it, g, j):
                heads = slice(j % 4 * 4, j % 4 * 4 + 4)
                dve.wait_ge(biased.sem, biased.at(g, 2 * j + 2))
                dve.tensor_reduce(nmx[:, heads], sm[:, heads], AX, ALU.max, negate=True).then_inc(max_ready.sem, 1)

            def sums_inverse(it, g, j):
                heads = slice(j % 4 * 4, j % 4 * 4 + 4)
                dve.wait_ge(exps.sem, exps.at(g, j + 1))
                dve.reciprocal(rden[:, heads], den[:, heads]).then_inc(rden_ready.sem, 1)

            def pt_split(it, g, j):
                heads = slice(j % 4 * 4, j % 4 * 4 + 4)
                dve.wait_ge(pt_high.sem, pt_high.at(g, j + 1))
                dve.wait_ge(pv_psum.sem, pv_psum.at(g, j // 2 - 1))
                dve.tensor_tensor(pTl[:, heads].rearrange("p h s -> p (h s)"), bank(it, "PT", j)[:],
                                  pTh[:, heads].bitcast(fp32).rearrange("p h s -> p (h s)"), ALU.subtract)\
                    .then_inc(pt_low.sem, 1)

            z_rows = zbank[:].rearrange("p (b d) -> p b d", b=GB)

            def z_stats(it, g, k):
                dve.wait_ge(z_psum.sem, z_psum.at(g, 2 * GB))
                stats(z_rows, 2, own_z, g, 0, ln_var["z"])

            def ln_z(it, g, k):
                dve.wait_ge(ln_rstd["z"].sem, ln_rstd["z"].at(g, 1))
                dve.wait_ge(ln_var["z"].sem, ln_var["z"].at(g, 1))
                dve.wait_ge(zT_psum.sem, zT_psum.at(g, 0))
                norm(n3, z_rows, 2, n3_ready)

            def gated(it, g, o):
                dve.wait_ge(silued.sem, silued.at(g, o + 1))
                dve.wait_ge(l1_psum.sem, l1_psum.at(g, 2 * o + 2))
                dve.wait_ge(l4_psum.sem, l4_psum.at(g, 0))
                dve.scalar_tensor_tensor(hA[:, o], bank(it, "l1", o, 1)[:], w2s[:, o:o + 1], al[:, o % 2],
                                         ALU.mult, ALU.mult).then_inc(l1_ready.sem, 1)

            def result(it, g, k):
                dve.wait_ge(l4_psum.sem, l4_psum.at(g, 1))
                dve.wait_ge(stored, g * 16)
                dve.tensor_tensor(res[:], bank(it, "l4", 0)[:].rearrange("p (b d) -> p b d", b=GB), row4(w3s), ALU.mult)\
                    .then_inc(scaled.sem, 1)
                dve.wait_ge(scaled.sem, scaled.at(g, 1))
                dve.wait_ge(x1_in_c.sem, x1_in_c.at(g, 1))
                dve.tensor_tensor(res[:], res[:], x1[:, 2], ALU.add).then_inc(out_ready.sem, 1)

            iterations(dve, ORDER["dve"], {
                "rw": rw_take, "exp": expert, "qkv": values, "scores": banding, "mix": mix_stats, "ln1": ln_1, "ln2": ln_2,
                "kv": keys, "kT": keys_normed, "q": q_copy, "ssq": q_sums, "maskn": mask_scores, "move1": move_to_c,
                "move2": move_to_b, "sim": score, "max": maxima, "inv": sums_inverse, "PT": pt_split,
                "xl": x_split, "vs": values_split, "down": y_split, "xnT": xn_split, "zl": z_split, "rwl": rw_split,
                "ln3": z_stats, "zT": ln_z, "l1": gated, "l4": result})

        @block.tensor
        def _(pe):
            pe.wait_ge(const, 3)
            pe.wait_ge(load["pw1"], 16)
            pe.wait_ge(load["pw2"], 16)
            for n in range(2):
                pe.wait_ge(pa, 1 + 2 * n)
                pe.transpose(banks["S", 0][:, 0:128], ph[1], ident[:]).then_inc(pp, 1)
                pe.wait_ge(pa, 2 + 2 * n)
                if n == 0:
                    pe.matmul(banks["S", 1][:, 0:128], ph[2], pw1[:], start=True, stop=True).then_inc(pp, 1)
                else:
                    pe.matmul(banks["S", 1][0:HEADS, 0:S], pw2[:], ph[2], start=True, stop=True).then_inc(pp, 1)
            pe.wait_ge(pd, 4)
            pe.wait_ge(load["wt"], 16)
            pe.wait_ge(load["xT"], 16)
            pe.matmul(banks["M", 0][:, 0:B * E], ones[:], cg, start=True, stop=True)
            for b in range(B):
                ins = pe.matmul(banks["M", 0][:, b * E:(b + 1) * E], xT[:, b * S:(b + 1) * S], wt[:],
                                start=False, stop=True, skip_group_check=True)
            ins.then_inc(pp, 1)
            pe.wait_ge(s_toepl, 16)
            for n in range(4):
                pe.matmul(banks["ST"[n // 2], n % 2][:], flip, turned_bias[:, 4 * n:4 * n + 4],
                          start=True, stop=True).then_inc(pp, 1)
            pe.wait_ge(pa, 10)

            def three(ps, w, x, start=True, stop=True):
                for n, (i, j) in enumerate(((0, 0), (0, 1), (1, 0))):
                    ins = pe.matmul(ps, w[i], x[j], start=start and n == 0, stop=stop and n == 2)
                return ins

            def free(it, step, k, n=0, *data):
                events = {signal: SHIFT[STAGE[step]] * signal.per + count for signal, count in data}
                drained = drained_before(it, step, k, n)
                if drained is not None:
                    signal, count = drained
                    events[signal] = max(count, events.get(signal, count))
                for signal, count in events.items():
                    pe.wait_ge(signal.sem, signal.at(it, count))
                return bank(it, step, k, n)

            pe.wait_ge(w_low, 3)
            waited = set()

            def weights(*names):
                for n in names:
                    if n not in waited:
                        waited.add(n)
                        pe.wait_ge(*((parts_low[n], 1) if n in parts else (load[n], 16)))

            def expert(it, g, c):
                cut = slice(c * 128, (c + 1) * 128)
                for n in range(2):
                    three(free(it, "exp", c, n, (x_low, 1))[:], [w[:, n, cut] for w in wgu], (xh[:], xl[:]))\
                        .then_inc(expert_psum.sem, 1)
                if c < NC_:
                    ps = free(it, "exp", c, 2, (rw_low, 1))
                    pe.matmul(ps[:], sel[:, c], wTh[:], start=True, stop=False)
                    pe.matmul(ps[:], sel[:, c], wTl[:], start=False, stop=True).then_inc(expert_psum.sem, 1)

            def rw_turn(it, g, k):
                ps = free(it, "rw", 0, 0, (rw_taken, 1))
                for b in range(GB):
                    ins = pe.transpose(ps[0:E, b * S:(b + 1) * S], rg[:, b * E:(b + 1) * E], ident[:])
                ins.then_inc(rw_psum.sem, 1)

            def down(it, g, k):
                weights("wd")
                ps = free(it, "down", 0, 0, (hidden, 1))
                for c in range(NX):
                    if c > 0:
                        pe.wait_ge(hidden.sem, hidden.at(g, c + 1))
                    ins = pe.matmul(ps[:], wd[:, c], hT[:, c], start=(c == 0), stop=(c == NX - 1))
                ins.then_inc(y_psum.sem, 1)

            def qkv(it, g, k):
                weights("wqkv")
                for n in range(2):
                    three(free(it, "qkv", 0, n, (y_low, 1))[:], [w[:, n * D:(n + 1) * D] for w in wqkv],
                          [y[:] for y in yT]).then_inc(qkv_psum.sem, 1)
                ps = free(it, "qkv", 0, 2)
                for b in range(GB):
                    ins = three(ps[:, b * D:(b + 1) * D], [y[:, b * S:(b + 1) * S] for y in yT],
                                [w[:, 2 * D:3 * D] for w in wqkv])
                ins.then_inc(qkv_psum.sem, 1)

            def scores(it, g, k):
                ps = free(it, "scores", 0, 0, (qk_copied, 2))
                for b in range(GB):
                    cut = slice(b * S, (b + 1) * S)
                    ins = pe.matmul(ps[:, cut], kT[:, cut], qT[:, cut], start=True, stop=True)
                ins.then_inc(scores_psum.sem, 1)

            def mix(it, g, k):
                ps = free(it, "mix", 0, 0, (v_ready, 1), (banded, 1))
                for b in range(GB):
                    ins = pe.matmul(ps[:, b * D:(b + 1) * D], st[:, b], v1[:, b], start=True, stop=True)
                ins.then_inc(mix_psum.sem, 1)

            def turn(it, step, src, ready, g, signal):
                ps = free(it, step, 0, 0, (ready, 1))
                for b in range(GB):
                    ins = pe.transpose(ps[:, b * S:(b + 1) * S], src(b), ident[:])
                ins.then_inc(signal.sem, 1)

            def xn_turn(it, g, k):
                turn(it, "xnT", lambda b: n1[:, b], n2_ready, g, xn_psum)

            def kv_proj(it, g, k):
                weights("wkv2")
                ps = free(it, "kv", 0, 0, (xn_low, 1))
                for b in range(GB):
                    ins = three(ps[:, b * 128:(b + 1) * 128], [x[:, b * S:(b + 1) * S] for x in xnT], [w[:] for w in wkv2])
                ins.then_inc(kv_psum.sem, 1)

            def q_proj(it, g, c):
                weights("wq2")
                three(free(it, "q", c, 0, (xn_low, 1))[:], [w[:, c * 128:(c + 1) * 128] for w in wq2], [x[:] for x in xnT])\
                    .then_inc(q_psum.sem, 1)

            def q_sum(it, g, c):
                ps = free(it, "qs", 0) if c == 0 else bank(it, "qs", 0)
                pe.wait_ge(q_squared.sem, q_squared.at(g, c + 1))
                for b in range(GB):
                    ins = pe.matmul(ps[:, b * HEADS + 2 * c:b * HEADS + 2 * c + 2], sq[:, c % 2, b * S:(b + 1) * S],
                                    halves[:], start=True, stop=True)
                ins.then_inc(ssq_psum.sem, 1)

            def k_turn(it, g, k):
                turn(it, "kT", lambda b: kd[:, b].rearrange("p n d -> p (n d)"), k_normed, g, kT_psum)

            def sim(it, g, j):
                k = j // 4
                for m in range(2):
                    pe.matmul(free(it, "sim", j, m, (kT_copied, 1), (q_copied, NP))[:, 0:2 * NK],
                              qs[:, 2 * (j % 4) + m, k * S:(k + 1) * S], kbd[:, k].rearrange("p n s -> p (n s)"), start=True, stop=True).then_inc(sim_psum.sem, 1)

            def p_turn(it, g, j):
                ps = free(it, "PT", j, 0, (p_normed, j + 1))
                for h in range(4):
                    ins = pe.transpose(ps[:, h * S:(h + 1) * S], sm[:, j % 4 * 4 + h, 1:NK], ident[:])
                ins.then_inc(pt_psum.sem, 1)

            def pv(it, g, n):
                ps = free(it, "PV", n, 0, (v_shifted, 1), (pt_low, 2 * n + 2))
                for odd in range(2):
                    values = [vz[:, n // 2, i, DH * (1 - odd):DH * (3 - odd)] for i in range(2)]
                    probs = [p[:, n % 2 * 8 + odd:n % 2 * 8 + 8:2] for p in (pTh, pTl)]
                    ins = three(ps[:].rearrange("p (h s) -> p h s", h=4), values, probs, start=odd == 0, stop=odd == 1)
                ins.then_inc(pv_psum.sem, 1)

            def z_proj(it, g, n):
                weights("wout")
                if n == 0:
                    pe.wait_ge(n3_ready.sem, n3_ready.at(g, 0))
                pe.wait_ge(ot_copied.sem, ot_copied.at(g, n + 1))
                k = n // 2
                for c in range(n % 2 * 4, n % 2 * 4 + 4):
                    ins = pe.matmul(zbank[:, k * D:(k + 1) * D], oT[:, c], wout[:, c], start=(c == 0), stop=(c == NP - 1))
                ins.then_inc(z_psum.sem, 1)

            def z_turn(it, g, k):
                turn(it, "zT", lambda b: n3[:, b], n3_ready, g, zT_psum)

            def layer1(it, g, o):
                weights("w12")
                for n in range(2):
                    first = n * HID + o * 128
                    three(free(it, "l1", o, n, (z_low, 1))[:], [w[:, first:first + 128] for w in w12], [z[:] for z in zT])\
                        .then_inc(l1_psum.sem, 1)

            def layer(step, w, src, ready, signal):
                def part(it, g, o):
                    weights("h1", "h2")
                    ps = free(it, step, o, 0, (ready, 1 if o == 0 else NO))
                    for c in range(NO):
                        if o == 0 and c > 0:
                            pe.wait_ge(ready.sem, ready.at(g, c + 1))
                        ins = pe.matmul(ps[:], w[:, c, o * 128:(o + 1) * 128], src[:, c], start=(c == 0), stop=(c == NO - 1))
                    ins.then_inc(signal.sem, 1)
                return part

            def layer4(it, g, k):
                weights("w3")
                ps = free(it, "l4", 0, 0, (l3_ready, NO))
                for b in range(GB):
                    for c in range(NO):
                        ins = pe.matmul(ps[:, b * D:(b + 1) * D], hA[:, c, b * S:(b + 1) * S], w3[:, c],
                                        start=(c == 0), stop=(c == NO - 1))
                ins.then_inc(l4_psum.sem, 1)

            iterations(pe, ORDER["pe"], {
                "rw": rw_turn, "exp": expert, "down": down, "qkv": qkv, "scores": scores, "mix": mix, "xnT": xn_turn,
                "kv": kv_proj, "q": q_proj, "qs": q_sum, "kT": k_turn, "sim": sim, "PT": p_turn, "PV": pv,
                "z": z_proj, "zT": z_turn, "l1": layer1, "l2": layer("l2", h1, hA, l1_ready, l2_psum),
                "l3": layer("l3", h2, hB, l2_ready, l3_psum), "l4": layer4})


def kernel(**inputs):
    import numpy as np
    import concourse.bacc as bacc
    from concourse.bass_utils import run_bass_kernel_spmd

    x, cond = np.asarray(inputs["x"]), np.asarray(inputs["cond_64"])
    i = {k: np.asarray(v) for k, v in inputs.items()}
    L = {k[3:]: v for k, v in i.items() if k.startswith("L0_")}

    def tiles(w):
        return w.reshape(-1, 128, w.shape[1]).transpose(1, 0, 2)

    def col(v):
        return v.reshape(-1, 128).T

    twice = lambda v: np.concatenate([v, v])
    wexp = lambda w, s: np.concatenate([w.transpose(1, 0, 2).reshape(D, E * EM), s], axis=1)
    arrays = {
        "x": x,
        "xT": x.reshape(B * S, D).T,
        "mask": i["mask_BxS_bf1"].reshape(B * S),
        "cols": np.concatenate(
            [col(L["ffn_w1_s"]), col(L["ffn_w2_s"]), col(L["ffn_h1_s"]), col(L["ffn_h2_s"]),
             col(L["attn_b_qkv"][0:D]), col(L["attn_b_qkv"][D:2 * D]), col(L["cond2_g_norm"]), col(L["cond2_g_out"]),
             col(twice(L["cond2_q_scale"])), col(twice(L["cond2_k_scale"])), col(twice(cond[0])), col(twice(cond[1]))],
            axis=1),
        "rows": np.concatenate(
            [L["attn_ln_w"], L["attn_ln_b"], L["attn_b_qkv"][2 * D:], L["ffn_w3_s"], L["cond2_w0"][0], L["cond2_b0"],
             L["cond2_g0"], L["cond2_b1"], L["cond2_g1"], cond[0], cond[1], L["cond2_null_attn_bias"]])[None],
        "wt": L["cond_wt"].T, "wgT": L["cond_wg"].T, "condT": cond.T,
        "pw1": L["cond2_w1"], "pw2": L["cond2_w2"], "pb2": L["cond2_b2"][:, None],
        "wg": wexp(L["cond_w_gate"], L["cond_sw_gate"]), "wu": wexp(L["cond_w_up"], L["cond_sw_up"]),
        "wd": tiles(np.concatenate([L["cond_w_down"].reshape(E * EM, D), L["cond_sw_down"]])),
        "wqkv": L["attn_W_qkv"], "wq2": L["cond2_Wq"], "wkv2": L["cond2_Wkv"], "wout": tiles(L["cond2_Wout"]),
        "w12": np.concatenate([L["ffn_w1_w"].T, L["ffn_w2_w"].T], axis=1),
        "h1": tiles(L["ffn_h1_w"].T), "h2": tiles(L["ffn_h2_w"].T),
        "w3": tiles(L["ffn_w3_w"].T),
    }
    arrays = {n: np.ascontiguousarray(v) for n, v in arrays.items()}
    nc = bacc.Bacc("TRN2", target_bir_lowering=False, num_devices=1)
    aps = {n: nc.dram_tensor("in_" + n, v.shape, mybir.dt.from_np(v.dtype), kind="ExternalInput").ap()
           for n, v in arrays.items()}
    out = nc.dram_tensor("out_y", (B, S, D), mybir.dt.float32, kind="ExternalOutput").ap()
    layer_kernel(nc, aps, out)
    r = run_bass_kernel_spmd(nc, [{"in_" + n: v for n, v in arrays.items()}], core_ids=[0])
    return r.results[0]["out_y"]
```
